# Optimizing a Trainium2 kernel written in Bass

```python
import numpy as np
import jax
import jax.numpy as jnp

def _softmax(x, axis=-1):
    return jax.nn.softmax(x, axis=axis)

def _gelu(x):
    return jax.nn.gelu(x, approximate=True)

def _silu(x):
    return jax.nn.silu(x)

def _sigmoid(x):
    return jax.nn.sigmoid(x)

def _layernorm(x, axis=-1, eps=1e-05):
    m = jnp.mean(x, axis=axis, keepdims=True)
    v = jnp.var(x, axis=axis, keepdims=True)
    return (x - m) / jnp.sqrt(v + eps)

def _scatter_add(tgt, idx, src, axis=0):
    return tgt.at[idx].add(src)

def _segment_sum(src, seg, n):
    return jax.ops.segment_sum(src, seg, n)
kernel_name = 'mk_hybrid_d1_jaxref_r8_d6889a'

def setup_inputs(seed: int=0):
    np.random.seed(seed)
    _w = jnp.asarray

    def _L0_attn_a_setup():
        import jax, jax.numpy as jnp
        import numpy as np
        B, N, DIM, H = (4, 512, 128, 16)
        HD = DIM // H
        SCALE = HD ** (-0.5)

        def _heads(t, bsz, ntok):
            return t.reshape(bsz, ntok, H, HD).transpose(0, 2, 1, 3)

        def _fwd(x, q_w1, q_b1, q_w2, q_b2, k_w1, k_b1, k_w2, k_b2, v_w, v_b, g_w, g_b, p_w, p_b):
            bsz, ntok, dim = x.shape
            gelu = lambda t: jax.nn.gelu(t, approximate=False)
            q = _heads(jax.nn.softplus(gelu(x @ q_w1.T + q_b1) @ q_w2.T + q_b2), bsz, ntok)
            k = _heads(jax.nn.softplus(gelu(x @ k_w1.T + k_b1) @ k_w2.T + k_b2), bsz, ntok)
            v = _heads(gelu(x @ v_w.T + v_b), bsz, ntok)
            g = _heads(gelu(x @ g_w.T + g_b), bsz, ntok)
            z = jnp.einsum('bhcn,bhc->bhn', q, k.sum(axis=-1)) * SCALE
            z = 1.0 / (z + dim)
            A = jnp.einsum('bhcn,bhcm->bhnm', q, k)
            out = jnp.einsum('bhnm,bhdm->bhdn', A, v) * SCALE
            out = (out + v) * z[:, :, None, :]
            out = out.reshape(bsz, ntok, dim)
            out = out * g.reshape(bsz, ntok, dim)
            return out @ p_w.T + p_b
        key = jax.random.key(seed)
        ks = jax.random.split(key, 16)
        w = lambda k: jax.random.normal(k, (DIM, DIM), jnp.float32) * 0.02
        b = lambda k: jax.random.normal(k, (DIM,), jnp.float32) * 0.02
        return {'x': jax.random.normal(ks[0], (B, N, DIM), jnp.float32), 'q_w1': w(ks[1]), 'q_b1': b(ks[2]), 'q_w2': w(ks[3]), 'q_b2': b(ks[4]), 'k_w1': w(ks[5]), 'k_b1': b(ks[6]), 'k_w2': w(ks[7]), 'k_b2': b(ks[8]), 'v_w': w(ks[9]), 'v_b': b(ks[10]), 'g_w': w(ks[11]), 'g_b': b(ks[12]), 'p_w': w(ks[13]), 'p_b': b(ks[14])}
    _L0_attn_a_in = _L0_attn_a_setup()

    def _L0_attn_b_setup():
        import jax, jax.numpy as jnp
        import numpy as np
        B, T, C = (4, 128, 128)
        HS = 64
        H = C // HS

        def wkv7(r, w, k, v, a, b):
            Bn, Tn, Cn = r.shape
            N = Cn // H

            def rs(z):
                return z.reshape(Bn, Tn, H, N).transpose(1, 0, 2, 3)
            r_, w_, k_, v_, a_, b_ = map(rs, (r, w, k, v, a, b))
            decay = jnp.exp(w_)
            S0 = jnp.zeros((Bn, H, N, N), dtype=r.dtype)

            def step(S, inp):
                rt, dt, kt, vt, at, bt = inp
                sa = jnp.einsum('bhij,bhj->bhi', S, at)
                S = S * dt[:, :, None, :] + sa[..., None] * bt[:, :, None, :] + vt[..., None] * kt[:, :, None, :]
                y = jnp.einsum('bhij,bhj->bhi', S, rt)
                return (S, y)
            _, ys = jax.lax.scan(step, S0, (r_, decay, k_, v_, a_, b_))
            return ys.transpose(1, 0, 2, 3).reshape(Bn, Tn, Cn)

        def timemix(x, lambdas, k_A, k_B, g_A, g_B, w_A, w_B, w_miu, a_A, a_B, a_time, x_A, x_B, x_miu, x_time, gn_gamma, gn_beta, rW, kW, vW, oW):
            Bn, Tn, Cn = x.shape
            Hn, Nn = x_time.shape
            x_last = jnp.concatenate([jnp.zeros_like(x[:, :1]), x[:, :-1]], axis=1)
            dx = x_last - x
            xm = x + dx * x_miu
            mix = jnp.tanh(xm @ x_A).reshape(Bn, Tn, 6, 32)
            miu = lambdas + jnp.einsum('btgk,gkc->gbtc', mix, x_B)
            xd = x[None] + dx[None] * miu
            r_in, w_in, k_in, v_in, a_in, g_in = xd
            v = v_in @ vW.T
            r = r_in @ rW.T
            g = jnp.tanh(g_in @ g_A) @ g_B
            w = -jax.nn.softplus(-(w_miu + jnp.tanh(w_in @ w_A) @ w_B)) - 0.5
            k = k_in @ kW.T + jnp.tanh(k_in @ k_A) @ k_B
            k = k / jnp.maximum(jnp.linalg.norm(k, axis=-1, keepdims=True), 1e-12)
            a_gate = jax.nn.sigmoid(a_time + a_in @ a_A @ a_B) * 2.0
            kk = k * jnp.exp(jnp.minimum(w * 0.5, 0.0))
            y = wkv7(r, w, kk, v, -k, k * a_gate)
            eps = 1e-05 * Hn
            yg = y.reshape(Bn * Tn, Hn, Nn)
            mean = yg.mean(-1, keepdims=True)
            var = yg.var(-1, keepdims=True)
            yg = (yg - mean) / jnp.sqrt(var + eps)
            y = yg.reshape(Bn * Tn, Cn) * gn_gamma + gn_beta
            y = y.reshape(Bn, Tn, Cn)
            rh = r.reshape(Bn, Tn, Hn, Nn)
            kh = k.reshape(Bn, Tn, Hn, Nn)
            vh = v.reshape(Bn, Tn, Hn, Nn)
            bonus = ((rh * kh * x_time).sum(-1, keepdims=True) * vh).reshape(Bn, Tn, Cn)
            out = (y + bonus) * g @ oW.T
            return out
        key = jax.random.key(seed)
        ks = jax.random.split(key, 24)
        s = 0.02
        d = {'x': jax.random.normal(ks[0], (B, T, C), jnp.float32), 'lambdas': jax.random.normal(ks[1], (6, 1, 1, C), jnp.float32) * s, 'k_A': jax.random.normal(ks[2], (C, 64), jnp.float32) * s, 'k_B': jax.random.normal(ks[3], (64, C), jnp.float32) * s, 'g_A': jax.random.normal(ks[4], (C, 128), jnp.float32) * s, 'g_B': jax.random.normal(ks[5], (128, C), jnp.float32) * s, 'w_A': jax.random.normal(ks[6], (C, 64), jnp.float32) * s, 'w_B': jax.random.normal(ks[7], (64, C), jnp.float32) * s, 'w_miu': jax.random.normal(ks[8], (1, 1, C), jnp.float32) * s, 'a_A': jax.random.normal(ks[9], (C, 64), jnp.float32) * s, 'a_B': jax.random.normal(ks[10], (64, C), jnp.float32) * s, 'a_time': jax.random.normal(ks[11], (1, 1, C), jnp.float32) * s, 'x_A': jax.random.normal(ks[12], (C, 32 * 6), jnp.float32) * s, 'x_B': jax.random.normal(ks[13], (6, 32, C), jnp.float32) * s, 'x_miu': jax.random.normal(ks[14], (1, 1, C), jnp.float32) * s, 'x_time': jax.random.normal(ks[15], (H, HS), jnp.float32) * s, 'gn_gamma': jnp.ones((C,), jnp.float32), 'gn_beta': jnp.zeros((C,), jnp.float32), 'rW': jax.random.normal(ks[16], (C, C), jnp.float32) * s, 'kW': jax.random.normal(ks[17], (C, C), jnp.float32) * s, 'vW': jax.random.normal(ks[18], (C, C), jnp.float32) * s, 'oW': jax.random.normal(ks[19], (C, C), jnp.float32) * s}
        return d
    _L0_attn_b_in = _L0_attn_b_setup()

    def _L0_ffn_setup():
        import jax, jax.numpy as jnp
        import numpy as np
        DIM = 128
        DEPTH = 2
        HEADS = 8
        DIM_HEAD = 64
        WINDOW = 64
        INNER = HEADS * DIM_HEAD
        HID = int(DIM * 4 * 2 / 3)
        B, N = (2, 1024)
        QK_SCALE = 8.0

        def shift_token(t):
            t1, t2 = jnp.split(t, 2, axis=-1)
            t2 = jnp.pad(t2, ((0, 0), (1, 0), (0, 0)))[:, :-1]
            return jnp.concatenate([t1, t2], axis=-1)

        def l2norm(t):
            return t / jnp.clip(jnp.linalg.norm(t, axis=-1, keepdims=True), 1e-12)

        def rotate_half(x):
            x1, x2 = jnp.split(x, 2, axis=-1)
            return jnp.concatenate([-x2, x1], axis=-1)

        def rotary_xpos(q, k):
            n = q.shape[-2]
            half_idx = jnp.arange(0, DIM_HEAD, 2, dtype=jnp.float32)
            inv_freq = 1.0 / 10000.0 ** (half_idx / DIM_HEAD)
            t = jnp.arange(n, dtype=jnp.float32)
            freqs = t[:, None] * inv_freq[None, :]
            freqs = jnp.concatenate([freqs, freqs], axis=-1)
            base = (half_idx + 0.4 * DIM_HEAD) / (1.4 * DIM_HEAD)
            power = (t - n // 2) / float(WINDOW // 2)
            scale = base[None, :] ** power[:, None]
            scale = jnp.concatenate([scale, scale], axis=-1)
            cos, sin = (jnp.cos(freqs), jnp.sin(freqs))
            q = q * cos * scale + rotate_half(q) * sin * scale
            k = k * cos / scale + rotate_half(k) * sin / scale
            return (q, k)

        def local_attention(q, k, v):
            b, h, n, d = q.shape
            w = n // WINDOW
            bq = q.reshape(b, h, w, WINDOW, d) * QK_SCALE
            bk = k.reshape(b, h, w, WINDOW, d)
            bv = v.reshape(b, h, w, WINDOW, d)

            def look_around(t):
                p = jnp.pad(t, ((0, 0), (0, 0), (1, 0), (0, 0), (0, 0)))
                return jnp.concatenate([p[:, :, :w], p[:, :, 1:]], axis=3)
            bk, bv = (look_around(bk), look_around(bv))
            bt = jnp.arange(n).reshape(w, WINDOW)
            btp = jnp.pad(bt, ((1, 0), (0, 0)), constant_values=-1)
            btk = jnp.concatenate([btp[:w], btp[1:]], axis=1)
            sim = jnp.einsum('bhwid,bhwjd->bhwij', bq, bk)
            i = bt[:, :, None]
            j = btk[:, None, :]
            mask = (i < j) | (i > j + WINDOW) | (j == -1)
            sim = jnp.where(mask, -jnp.finfo(sim.dtype).max, sim)
            attn = jax.nn.softmax(sim, axis=-1)
            out = jnp.einsum('bhwij,bhwjd->bhwid', attn, bv)
            return out.reshape(b, h, n, d)

        def _layer(x, wqkv, qs, ksc, wo, lg, lb, w1, b1, w2, b2):
            b, n, _ = x.shape
            h = shift_token(x)
            qkv = h @ wqkv
            q, k, v = jnp.split(qkv, 3, axis=-1)
            to_heads = lambda t: t.reshape(b, n, HEADS, DIM_HEAD).transpose(0, 2, 1, 3)
            q, k, v = (to_heads(q), to_heads(k), to_heads(v))
            q = l2norm(q) * qs
            k = l2norm(k) * ksc
            q, k = rotary_xpos(q, k)
            o = local_attention(q, k, v)
            o = o.transpose(0, 2, 1, 3).reshape(b, n, INNER)
            x = x + o @ wo
            h = shift_token(x)
            mu = h.mean(-1, keepdims=True)
            var = h.var(-1, keepdims=True)
            h = (h - mu) / jnp.sqrt(var + 1e-05) * lg + lb
            h = h @ w1 + b1
            a, g = jnp.split(h, 2, axis=-1)
            h = a * jax.nn.gelu(g, approximate=False)
            x = x + h @ w2 + b2
            return x
        key = jax.random.key(seed)
        ks = jax.random.split(key, 6)
        return {'x': jax.random.normal(ks[0], (B, N, DIM), jnp.float32), 'wqkv': jax.random.normal(ks[1], (DEPTH, DIM, 3 * INNER), jnp.float32) * 0.02, 'q_scale': jnp.ones((DEPTH, DIM_HEAD), jnp.float32), 'k_scale': jnp.ones((DEPTH, DIM_HEAD), jnp.float32), 'wo': jax.random.normal(ks[2], (DEPTH, INNER, DIM), jnp.float32) * 0.02, 'ln_g': jnp.ones((DEPTH, DIM), jnp.float32), 'ln_b': jnp.zeros((DEPTH, DIM), jnp.float32), 'w1': jax.random.normal(ks[3], (DEPTH, DIM, 2 * HID), jnp.float32) * 0.02, 'b1': jnp.zeros((DEPTH, 2 * HID), jnp.float32), 'w2': jax.random.normal(ks[4], (DEPTH, HID, DIM), jnp.float32) * 0.02, 'b2': jnp.zeros((DEPTH, DIM), jnp.float32)}
    _L0_ffn_in = _L0_ffn_setup()
    _d = {'L0_attn_a_x': _L0_attn_a_in['x'], 'L0_attn_a_q_w1': _L0_attn_a_in['q_w1'], 'L0_attn_a_q_b1': _L0_attn_a_in['q_b1'], 'L0_attn_a_q_w2': _L0_attn_a_in['q_w2'], 'L0_attn_a_q_b2': _L0_attn_a_in['q_b2'], 'L0_attn_a_k_w1': _L0_attn_a_in['k_w1'], 'L0_attn_a_k_b1': _L0_attn_a_in['k_b1'], 'L0_attn_a_k_w2': _L0_attn_a_in['k_w2'], 'L0_attn_a_k_b2': _L0_attn_a_in['k_b2'], 'L0_attn_a_v_w': _L0_attn_a_in['v_w'], 'L0_attn_a_v_b': _L0_attn_a_in['v_b'], 'L0_attn_a_g_w': _L0_attn_a_in['g_w'], 'L0_attn_a_g_b': _L0_attn_a_in['g_b'], 'L0_attn_a_p_w': _L0_attn_a_in['p_w'], 'L0_attn_a_p_b': _L0_attn_a_in['p_b'], 'L0_attn_b_lambdas': _L0_attn_b_in['lambdas'], 'L0_attn_b_k_A': _L0_attn_b_in['k_A'], 'L0_attn_b_k_B': _L0_attn_b_in['k_B'], 'L0_attn_b_g_A': _L0_attn_b_in['g_A'], 'L0_attn_b_g_B': _L0_attn_b_in['g_B'], 'L0_attn_b_w_A': _L0_attn_b_in['w_A'], 'L0_attn_b_w_B': _L0_attn_b_in['w_B'], 'L0_attn_b_w_miu': _L0_attn_b_in['w_miu'], 'L0_attn_b_a_A': _L0_attn_b_in['a_A'], 'L0_attn_b_a_B': _L0_attn_b_in['a_B'], 'L0_attn_b_a_time': _L0_attn_b_in['a_time'], 'L0_attn_b_x_A': _L0_attn_b_in['x_A'], 'L0_attn_b_x_B': _L0_attn_b_in['x_B'], 'L0_attn_b_x_miu': _L0_attn_b_in['x_miu'], 'L0_attn_b_x_time': _L0_attn_b_in['x_time'], 'L0_attn_b_gn_gamma': _L0_attn_b_in['gn_gamma'], 'L0_attn_b_gn_beta': _L0_attn_b_in['gn_beta'], 'L0_attn_b_rW': _L0_attn_b_in['rW'], 'L0_attn_b_kW': _L0_attn_b_in['kW'], 'L0_attn_b_vW': _L0_attn_b_in['vW'], 'L0_attn_b_oW': _L0_attn_b_in['oW'], 'L0_ffn_wqkv': _L0_ffn_in['wqkv'], 'L0_ffn_q_scale': _L0_ffn_in['q_scale'], 'L0_ffn_k_scale': _L0_ffn_in['k_scale'], 'L0_ffn_wo': _L0_ffn_in['wo'], 'L0_ffn_ln_g': _L0_ffn_in['ln_g'], 'L0_ffn_ln_b': _L0_ffn_in['ln_b'], 'L0_ffn_w1': _L0_ffn_in['w1'], 'L0_ffn_b1': _L0_ffn_in['b1'], 'L0_ffn_w2': _L0_ffn_in['w2'], 'L0_ffn_b2': _L0_ffn_in['b2']}
    _x0 = _d['L0_attn_a_x']
    _d['L0_attn_a_x'] = jax.random.normal(jax.random.fold_in(jax.random.key(seed), 1), (4, 1024, 128), dtype=_x0.dtype)
    del _x0
    return _d

def reference(L0_attn_a_x, L0_attn_a_q_w1, L0_attn_a_q_b1, L0_attn_a_q_w2, L0_attn_a_q_b2, L0_attn_a_k_w1, L0_attn_a_k_b1, L0_attn_a_k_w2, L0_attn_a_k_b2, L0_attn_a_v_w, L0_attn_a_v_b, L0_attn_a_g_w, L0_attn_a_g_b, L0_attn_a_p_w, L0_attn_a_p_b, L0_attn_b_lambdas, L0_attn_b_k_A, L0_attn_b_k_B, L0_attn_b_g_A, L0_attn_b_g_B, L0_attn_b_w_A, L0_attn_b_w_B, L0_attn_b_w_miu, L0_attn_b_a_A, L0_attn_b_a_B, L0_attn_b_a_time, L0_attn_b_x_A, L0_attn_b_x_B, L0_attn_b_x_miu, L0_attn_b_x_time, L0_attn_b_gn_gamma, L0_attn_b_gn_beta, L0_attn_b_rW, L0_attn_b_kW, L0_attn_b_vW, L0_attn_b_oW, L0_ffn_wqkv, L0_ffn_q_scale, L0_ffn_k_scale, L0_ffn_wo, L0_ffn_ln_g, L0_ffn_ln_b, L0_ffn_w1, L0_ffn_b1, L0_ffn_w2, L0_ffn_b2):

    def _L0_attn_a_ref(x, q_w1, q_b1, q_w2, q_b2, k_w1, k_b1, k_w2, k_b2, v_w, v_b, g_w, g_b, p_w, p_b):
        import jax, jax.numpy as jnp
        import numpy as np
        B, N, DIM, H = (4, 512, 128, 16)
        HD = DIM // H
        SCALE = HD ** (-0.5)

        def _heads(t, bsz, ntok):
            return t.reshape(bsz, ntok, H, HD).transpose(0, 2, 1, 3)

        def _fwd(x, q_w1, q_b1, q_w2, q_b2, k_w1, k_b1, k_w2, k_b2, v_w, v_b, g_w, g_b, p_w, p_b):
            bsz, ntok, dim = x.shape
            gelu = lambda t: jax.nn.gelu(t, approximate=False)
            q = _heads(jax.nn.softplus(gelu(x @ q_w1.T + q_b1) @ q_w2.T + q_b2), bsz, ntok)
            k = _heads(jax.nn.softplus(gelu(x @ k_w1.T + k_b1) @ k_w2.T + k_b2), bsz, ntok)
            v = _heads(gelu(x @ v_w.T + v_b), bsz, ntok)
            g = _heads(gelu(x @ g_w.T + g_b), bsz, ntok)
            z = jnp.einsum('bhcn,bhc->bhn', q, k.sum(axis=-1)) * SCALE
            z = 1.0 / (z + dim)
            A = jnp.einsum('bhcn,bhcm->bhnm', q, k)
            out = jnp.einsum('bhnm,bhdm->bhdn', A, v) * SCALE
            out = (out + v) * z[:, :, None, :]
            out = out.reshape(bsz, ntok, dim)
            out = out * g.reshape(bsz, ntok, dim)
            return out @ p_w.T + p_b
        return _fwd(x, q_w1, q_b1, q_w2, q_b2, k_w1, k_b1, k_w2, k_b2, v_w, v_b, g_w, g_b, p_w, p_b)

    def _L0_attn_b_ref(x, lambdas, k_A, k_B, g_A, g_B, w_A, w_B, w_miu, a_A, a_B, a_time, x_A, x_B, x_miu, x_time, gn_gamma, gn_beta, rW, kW, vW, oW):
        import jax, jax.numpy as jnp
        import numpy as np
        B, T, C = (4, 128, 128)
        HS = 64
        H = C // HS

        def wkv7(r, w, k, v, a, b):
            Bn, Tn, Cn = r.shape
            N = Cn // H

            def rs(z):
                return z.reshape(Bn, Tn, H, N).transpose(1, 0, 2, 3)
            r_, w_, k_, v_, a_, b_ = map(rs, (r, w, k, v, a, b))
            decay = jnp.exp(w_)
            S0 = jnp.zeros((Bn, H, N, N), dtype=r.dtype)

            def step(S, inp):
                rt, dt, kt, vt, at, bt = inp
                sa = jnp.einsum('bhij,bhj->bhi', S, at)
                S = S * dt[:, :, None, :] + sa[..., None] * bt[:, :, None, :] + vt[..., None] * kt[:, :, None, :]
                y = jnp.einsum('bhij,bhj->bhi', S, rt)
                return (S, y)
            _, ys = jax.lax.scan(step, S0, (r_, decay, k_, v_, a_, b_))
            return ys.transpose(1, 0, 2, 3).reshape(Bn, Tn, Cn)

        def timemix(x, lambdas, k_A, k_B, g_A, g_B, w_A, w_B, w_miu, a_A, a_B, a_time, x_A, x_B, x_miu, x_time, gn_gamma, gn_beta, rW, kW, vW, oW):
            Bn, Tn, Cn = x.shape
            Hn, Nn = x_time.shape
            x_last = jnp.concatenate([jnp.zeros_like(x[:, :1]), x[:, :-1]], axis=1)
            dx = x_last - x
            xm = x + dx * x_miu
            mix = jnp.tanh(xm @ x_A).reshape(Bn, Tn, 6, 32)
            miu = lambdas + jnp.einsum('btgk,gkc->gbtc', mix, x_B)
            xd = x[None] + dx[None] * miu
            r_in, w_in, k_in, v_in, a_in, g_in = xd
            v = v_in @ vW.T
            r = r_in @ rW.T
            g = jnp.tanh(g_in @ g_A) @ g_B
            w = -jax.nn.softplus(-(w_miu + jnp.tanh(w_in @ w_A) @ w_B)) - 0.5
            k = k_in @ kW.T + jnp.tanh(k_in @ k_A) @ k_B
            k = k / jnp.maximum(jnp.linalg.norm(k, axis=-1, keepdims=True), 1e-12)
            a_gate = jax.nn.sigmoid(a_time + a_in @ a_A @ a_B) * 2.0
            kk = k * jnp.exp(jnp.minimum(w * 0.5, 0.0))
            y = wkv7(r, w, kk, v, -k, k * a_gate)
            eps = 1e-05 * Hn
            yg = y.reshape(Bn * Tn, Hn, Nn)
            mean = yg.mean(-1, keepdims=True)
            var = yg.var(-1, keepdims=True)
            yg = (yg - mean) / jnp.sqrt(var + eps)
            y = yg.reshape(Bn * Tn, Cn) * gn_gamma + gn_beta
            y = y.reshape(Bn, Tn, Cn)
            rh = r.reshape(Bn, Tn, Hn, Nn)
            kh = k.reshape(Bn, Tn, Hn, Nn)
            vh = v.reshape(Bn, Tn, Hn, Nn)
            bonus = ((rh * kh * x_time).sum(-1, keepdims=True) * vh).reshape(Bn, Tn, Cn)
            out = (y + bonus) * g @ oW.T
            return out
        return timemix(x, lambdas, k_A, k_B, g_A, g_B, w_A, w_B, w_miu, a_A, a_B, a_time, x_A, x_B, x_miu, x_time, gn_gamma, gn_beta, rW, kW, vW, oW)

    def _L0_ffn_ref(x, wqkv, q_scale, k_scale, wo, ln_g, ln_b, w1, b1, w2, b2):
        import jax, jax.numpy as jnp
        import numpy as np
        DIM = 128
        DEPTH = 2
        HEADS = 8
        DIM_HEAD = 64
        WINDOW = 64
        INNER = HEADS * DIM_HEAD
        HID = int(DIM * 4 * 2 / 3)
        B, N = (2, 1024)
        QK_SCALE = 8.0

        def shift_token(t):
            t1, t2 = jnp.split(t, 2, axis=-1)
            t2 = jnp.pad(t2, ((0, 0), (1, 0), (0, 0)))[:, :-1]
            return jnp.concatenate([t1, t2], axis=-1)

        def l2norm(t):
            return t / jnp.clip(jnp.linalg.norm(t, axis=-1, keepdims=True), 1e-12)

        def rotate_half(x):
            x1, x2 = jnp.split(x, 2, axis=-1)
            return jnp.concatenate([-x2, x1], axis=-1)

        def rotary_xpos(q, k):
            n = q.shape[-2]
            half_idx = jnp.arange(0, DIM_HEAD, 2, dtype=jnp.float32)
            inv_freq = 1.0 / 10000.0 ** (half_idx / DIM_HEAD)
            t = jnp.arange(n, dtype=jnp.float32)
            freqs = t[:, None] * inv_freq[None, :]
            freqs = jnp.concatenate([freqs, freqs], axis=-1)
            base = (half_idx + 0.4 * DIM_HEAD) / (1.4 * DIM_HEAD)
            power = (t - n // 2) / float(WINDOW // 2)
            scale = base[None, :] ** power[:, None]
            scale = jnp.concatenate([scale, scale], axis=-1)
            cos, sin = (jnp.cos(freqs), jnp.sin(freqs))
            q = q * cos * scale + rotate_half(q) * sin * scale
            k = k * cos / scale + rotate_half(k) * sin / scale
            return (q, k)

        def local_attention(q, k, v):
            b, h, n, d = q.shape
            w = n // WINDOW
            bq = q.reshape(b, h, w, WINDOW, d) * QK_SCALE
            bk = k.reshape(b, h, w, WINDOW, d)
            bv = v.reshape(b, h, w, WINDOW, d)

            def look_around(t):
                p = jnp.pad(t, ((0, 0), (0, 0), (1, 0), (0, 0), (0, 0)))
                return jnp.concatenate([p[:, :, :w], p[:, :, 1:]], axis=3)
            bk, bv = (look_around(bk), look_around(bv))
            bt = jnp.arange(n).reshape(w, WINDOW)
            btp = jnp.pad(bt, ((1, 0), (0, 0)), constant_values=-1)
            btk = jnp.concatenate([btp[:w], btp[1:]], axis=1)
            sim = jnp.einsum('bhwid,bhwjd->bhwij', bq, bk)
            i = bt[:, :, None]
            j = btk[:, None, :]
            mask = (i < j) | (i > j + WINDOW) | (j == -1)
            sim = jnp.where(mask, -jnp.finfo(sim.dtype).max, sim)
            attn = jax.nn.softmax(sim, axis=-1)
            out = jnp.einsum('bhwij,bhwjd->bhwid', attn, bv)
            return out.reshape(b, h, n, d)

        def _layer(x, wqkv, qs, ksc, wo, lg, lb, w1, b1, w2, b2):
            b, n, _ = x.shape
            h = shift_token(x)
            qkv = h @ wqkv
            q, k, v = jnp.split(qkv, 3, axis=-1)
            to_heads = lambda t: t.reshape(b, n, HEADS, DIM_HEAD).transpose(0, 2, 1, 3)
            q, k, v = (to_heads(q), to_heads(k), to_heads(v))
            q = l2norm(q) * qs
            k = l2norm(k) * ksc
            q, k = rotary_xpos(q, k)
            o = local_attention(q, k, v)
            o = o.transpose(0, 2, 1, 3).reshape(b, n, INNER)
            x = x + o @ wo
            h = shift_token(x)
            mu = h.mean(-1, keepdims=True)
            var = h.var(-1, keepdims=True)
            h = (h - mu) / jnp.sqrt(var + 1e-05) * lg + lb
            h = h @ w1 + b1
            a, g = jnp.split(h, 2, axis=-1)
            h = a * jax.nn.gelu(g, approximate=False)
            x = x + h @ w2 + b2
            return x
        for l in range(DEPTH):
            x = _layer(x, wqkv[l], q_scale[l], k_scale[l], wo[l], ln_g[l], ln_b[l], w1[l], b1[l], w2[l], b2[l])
        return x
    x = L0_attn_a_x
    x = x + _L0_attn_a_ref(_layernorm(x, axis=-1), L0_attn_a_q_w1, L0_attn_a_q_b1, L0_attn_a_q_w2, L0_attn_a_q_b2, L0_attn_a_k_w1, L0_attn_a_k_b1, L0_attn_a_k_w2, L0_attn_a_k_b2, L0_attn_a_v_w, L0_attn_a_v_b, L0_attn_a_g_w, L0_attn_a_g_b, L0_attn_a_p_w, L0_attn_a_p_b)
    x = x + _L0_ffn_ref(_layernorm(x, axis=-1), L0_ffn_wqkv, L0_ffn_q_scale, L0_ffn_k_scale, L0_ffn_wo, L0_ffn_ln_g, L0_ffn_ln_b, L0_ffn_w1, L0_ffn_b1, L0_ffn_w2, L0_ffn_b2)
    x = x + _L0_attn_b_ref(_layernorm(x, axis=-1), L0_attn_b_lambdas, L0_attn_b_k_A, L0_attn_b_k_B, L0_attn_b_g_A, L0_attn_b_g_B, L0_attn_b_w_A, L0_attn_b_w_B, L0_attn_b_w_miu, L0_attn_b_a_A, L0_attn_b_a_B, L0_attn_b_a_time, L0_attn_b_x_A, L0_attn_b_x_B, L0_attn_b_x_miu, L0_attn_b_x_time, L0_attn_b_gn_gamma, L0_attn_b_gn_beta, L0_attn_b_rW, L0_attn_b_kW, L0_attn_b_vW, L0_attn_b_oW)
    x = x + _L0_ffn_ref(_layernorm(x, axis=-1), L0_ffn_wqkv, L0_ffn_q_scale, L0_ffn_k_scale, L0_ffn_wo, L0_ffn_ln_g, L0_ffn_ln_b, L0_ffn_w1, L0_ffn_b1, L0_ffn_w2, L0_ffn_b2)
    return x

_drawn_inputs = setup_inputs


def setup_inputs(seed=0):
    import zlib

    import numpy as np

    out = dict(_drawn_inputs(seed))
    spreads = {'L0_attn_b_gn_gamma': (1.0, 0.6),
     'L0_attn_b_gn_beta': (0.0, 0.8),
     'L0_ffn_q_scale': (1.0, 0.6),
     'L0_ffn_k_scale': (1.0, 0.6),
     'L0_ffn_ln_g': (1.0, 0.6),
     'L0_ffn_ln_b': (0.0, 0.8),
     'L0_ffn_b1': (0.0, 0.8),
     'L0_ffn_b2': (0.0, 0.1)}
    factors = {'L0_attn_a_q_w1': 8.0,
     'L0_attn_a_q_b1': 40.347,
     'L0_attn_a_q_w2': 8.0,
     'L0_attn_a_q_b2': 43.705,
     'L0_attn_a_k_w1': 8.0,
     'L0_attn_a_k_b1': 8.0,
     'L0_attn_a_k_w2': 8.0,
     'L0_attn_a_k_b2': 8.0,
     'L0_attn_a_v_w': 8.0,
     'L0_attn_a_v_b': 8.0,
     'L0_attn_a_g_w': 8.0,
     'L0_attn_a_g_b': 8.0,
     'L0_attn_a_p_w': 8.0,
     'L0_attn_a_p_b': 2.846,
     'L0_attn_b_lambdas': 8.0,
     'L0_attn_b_k_A': 8.0,
     'L0_attn_b_k_B': 8.0,
     'L0_attn_b_g_A': 8.0,
     'L0_attn_b_g_B': 8.0,
     'L0_attn_b_w_A': 8.0,
     'L0_attn_b_w_B': 8.0,
     'L0_attn_b_w_miu': 8.0,
     'L0_attn_b_a_A': 8.0,
     'L0_attn_b_a_B': 8.0,
     'L0_attn_b_a_time': 64.0,
     'L0_attn_b_x_A': 8.0,
     'L0_attn_b_x_B': 8.0,
     'L0_attn_b_x_miu': 8.0,
     'L0_attn_b_x_time': 8.0,
     'L0_attn_b_rW': 8.0,
     'L0_attn_b_kW': 8.0,
     'L0_attn_b_vW': 8.0,
     'L0_attn_b_oW': 8.0,
     'L0_ffn_w1': 3.72,
     'L0_ffn_w2': 3.663}
    for name, (base, spread) in spreads.items():
        noise = np.random.default_rng([zlib.crc32(name.encode()), seed]).standard_normal(out[name].shape)
        drawn = base * np.exp(spread * noise) if base else spread * noise
        out[name] = jnp.asarray(drawn.astype(out[name].dtype))
    for name, factor in factors.items():
        out[name] = (out[name] * factor).astype(out[name].dtype)
    return out
```

```python
from contextlib import ExitStack, contextmanager

import numpy as np
import concourse.bass as bass
from concourse import mybir

F32 = mybir.dt.float32
ALU = mybir.AluOpType
ACT = mybir.ActivationFunctionType
AX = mybir.AxisListType

P = 128
B = 4
T = 8
NT = B * T
DEPTH = 2
H = 8
D = 64
W = 64
HID = 341
CH = [(0, 128), (128, 128), (256, 85)]
QK_SCALE = 8.0
LN_EPS = 1e-5
MASKED = -1e37


class Memory:

    def __init__(self, nc, ctx):
        def sb(name, shape):
            return ctx.enter_context(nc.sbuf_tensor(name, shape, F32))

        self.x = sb("x_res", [P, B, T, P])
        self.ua = sb("u_a", [P, B, T + 1, P])
        self.ident = sb("ident", [P, P])
        self.minus_half = sb("minus_half", [P, NT])
        self.loaded = ctx.enter_context(nc.semaphore("loaded"))
        self.stats = sb("x_stats", [P, NT, 6])
        self.moments = sb("x_moments", [P, NT, 2])
        self.rstd = sb("x_rstd", [P, NT])
        self.ps = [ctx.enter_context(nc.psum_tensor(f"bank{n}", [P, 512], F32)) for n in (0, 3)]
        self.bank0, self.bank3 = self.ps
        self.bank12 = ctx.enter_context(nc.psum_tensor("bank12", [P, 1024], F32))
        self.bank45 = ctx.enter_context(nc.psum_tensor("bank45", [P, 1024], F32))
        self.bank67 = ctx.enter_context(nc.psum_tensor("bank67", [P, 1024], F32))



class FfnMemory:
    def __init__(self, nc, ctx, mem, times=0):
        def sb(name, shape):
            return ctx.enter_context(nc.sbuf_tensor(f"{name}_{times}", shape, F32))

        self.ub = sb("u_b", [P, B, T + 1, P])
        self.wqkv = sb("wqkv", [P, DEPTH, 3 * H * D])
        self.wo = sb("wo", [P, DEPTH, 4, P])
        self.w1 = sb("w1", [P, DEPTH, 2 * HID])
        self.w2 = sb("w2", [P, DEPTH, 3, P])
        self.b1 = sb("b1", [P, DEPTH, 2, 3])
        self.b2 = sb("b2", [P, DEPTH, P])
        self.lnp = sb("lnp", [P, DEPTH, 2])
        self.rope_raw = sb("rope_raw", [P, T, 4, D])
        self.qk_scales = sb("qk_scales", [P, DEPTH, 4, D])
        self.rope = sb("rope", [P, T, 4, D])
        self.mask = sb("mask", [P, T, P])
        self.shift = sb("shift", [P, 2, P])
        self.minus_half = mem.minus_half
        self.u_tile = sb("u_tile", [P, B, P])
        self.hT = sb("hT", [P, B, P])
        self.last_col = sb("last_col", [P, B, 1])
        self.sq = sb("sq", [P, 2, 1024])
        self.ss = sb("ss", [P, B, 16])
        self.rnorm = sb("rnorm", [P, B, 16])
        self.rot_c = sb("rot_c", [P, 2, 16, D])
        self.rot_s = sb("rot_s", [P, 2, 16, D])
        self.qT = sb("qT", [P, 2, 4, 2, P])
        self.kT = sb("kT", [P, B, 4, 3, W])
        self.v = sb("v", [P, B, H * D])
        self.v0 = sb("v0", [P, B, H * D])
        self.logits = sb("logits", [P, 2, H, P])
        self.neg_max = sb("neg_max", [P, B, 2, H])
        self.sums = sb("sums", [P, B, 2, H])
        self.probs = sb("probs", [P, B, H, P])
        self.pT = sb("pT", [P, 2, H, P])
        self.oT = sb("oT", [P, 2, 4, P])
        self.stats = sb("h_stats", [P, 2, 2, 6])
        self.moments = sb("h_moments", [P, 2, 2, 2])
        self.rstd = sb("h_rstd", [P, 2, 2])
        place = self.logits[:, :, :, :].rearrange("p r h k -> p (r h k)")
        self.h, self.hn = (place[:, n * 4 * P:(n + 1) * 4 * P].rearrange("p (r m c) -> p r m c", r=2, m=2)
                           for n in range(2))
        self.hnT = place[:, 8 * P:12 * P].rearrange("p (r n) -> p r n", r=2)
        place = self.probs[:, 0:3].rearrange("p b h k -> p (b h k)").rearrange("p (n c q) -> p n c q", n=4, c=3)
        self.gelu, self.hidden = place[:, 0:2], place[:, 2:4]


ATT_SEMS = ("tables_ready", "tile_copied", "uT_done", "carried", "hT_ready", "qk_done", "v_done", "squares_ready",
            "ss_clamped", "ss_ready", "rotated", "rnorm_ready", "rot_summed", "qk_normed", "qT_done", "kT_done", "qT_ready",
            "kT_ready", "v_ready", "keys_kept", "values_kept", "sims_done", "masked", "max_found",
            "max_ready", "exp_ready", "sums_inverted", "probs_ready", "pT_done", "pT_ready", "pv_done",
            "oT_ready", "wo_done", "u_updated")
FF_SEMS = ("f_shifted", "f_hi_ready", "f_lo_ready", "f_stats", "f_var_ready", "f_eps_added",
           "f_rstd_ready", "f_normed", "f_hnT_done", "f_hnT_ready", "f_up_done", "f_gelu_ready",
           "f_hidden_ready", "f_bias_added", "f_down_done", "f_out_ready")


def run_steps(eng, steps_of_loop, n, last_lag, step, ahead=0):
    first = -(-last_lag // steps_of_loop) * steps_of_loop + steps_of_loop
    last = n - (steps_of_loop if ahead else 0)
    for k in range(first):
        step(k, k % steps_of_loop)
    with eng.Fori(first // steps_of_loop, last // steps_of_loop) as m:
        for u in range(steps_of_loop):
            step(steps_of_loop * m + u, u, m)
    for k in range(last, n + last_lag):
        step(k, k % steps_of_loop)


def wait_apart(eng, i):
    if not isinstance(i, int):
        eng.nop(nofuse=True)


def tile_of(k, u, m, lag, per_turn, n):
    turn, pos = divmod(u - lag, per_turn)
    if m is None:
        i = k - lag
        return (i, i // per_turn, i % per_turn) if 0 <= i < n else None
    return per_turn * (m + turn) + pos, m + turn, pos


def attention(nc, mem, f, sem, u_buf, layer, run):
    base = NT * run

    def at(i):
        return base + i + 1

    LAG_SOFTMAX, LAG_SCALE, LAG_PV = 2, 3, 4

    def step_of(stages):
        def step(k, u, m=None):
            for lag, stage in stages:
                tile = tile_of(k, u, m, lag, B, NT)
                if tile is not None:
                    stage(*tile)
        return step

    def later(i, t, n):
        return not isinstance(i, int) or i >= n

    with nc.Block() as block:

        @block.gpsimd
        def _(pool):
            def copy_tile(i, t, b):
                if later(i, t, B):
                    pool.wait_ge(sem["uT_done"], at(i) - B)
                wait_apart(pool, i)
                nc.gpsimd.tensor_copy(f.u_tile[:, b, :], u_buf[:, b, t + 1, :]).then_inc(sem["tile_copied"], 1)

            def scale_probs(i, t, b):
                pool.wait_ge(sem["sums_inverted"], at(i))
                nc.gpsimd.tensor_tensor(f.probs[:, b], f.probs[:, b],
                                        f.sums[:, b, 1, :].unsqueeze(2).to_broadcast([P, H, P]),
                                        ALU.mult).then_inc(sem["probs_ready"], 1)

            def norm_qk(i, t, b):
                pool.wait_ge(sem["ss_ready"], at(i))
                nc.gpsimd.tensor_tensor(f.rnorm[:, b, :], f.ss[:, b, :], f.minus_half[:, 0:16],
                                        ALU.pow).then_inc(sem["rnorm_ready"], 1)
                pool.wait_ge(sem["rotated"], at(i))
                nc.gpsimd.tensor_tensor(f.rot_c[:, b % 2], f.rot_c[:, b % 2], f.rot_s[:, b % 2],
                                        ALU.add).then_inc(sem["rot_summed"], 1)
                pool.wait_ge(sem["rnorm_ready"], at(i))
                pool.wait_ge(sem["rot_summed"], at(i))
                nc.gpsimd.tensor_tensor(f.rot_c[:, b % 2], f.rot_c[:, b % 2],
                                        f.rnorm[:, b, :].unsqueeze(2).to_broadcast([P, 16, D]),
                                        ALU.mult).then_inc(sem["qk_normed"], 1)

            if layer == 0:
                nc.gpsimd.memset(f.kT[:, :, :, 1, :], 0.0).then_inc(sem["tables_ready"], 1)
                nc.gpsimd.memset(f.v0[:, :, :], 0.0).then_inc(sem["tables_ready"], 1)
                nc.gpsimd.memset(f.qT[:, :, :, :, :], 0.0).then_inc(sem["tables_ready"], 1)
            copy_tile(0, 0, 0)
            run_steps(pool, B, NT, LAG_PV, step_of([
                (-1, copy_tile), (LAG_SCALE, scale_probs), (0, norm_qk)]), ahead=1)

        @block.vector
        def _(dve):
            def hT(i, t, b):
                dve.wait_ge(sem["uT_done"], at(i))
                if later(i, t, B):
                    dve.wait_ge(sem["v_done"], at(i) - B)
                nc.vector.tensor_copy(f.hT[W:P, b, 0:1], f.last_col[W:P, b, :]).then_inc(sem["carried"], 1)
                nc.vector.tensor_copy(f.hT[0:W, b, :], mem.bank0[0:W, 0:P])
                nc.vector.tensor_copy(f.hT[W:P, b, 1:P], mem.bank0[W:P, 0:P - 1])
                dve.wait_ge(sem["carried"], at(i))
                nc.vector.tensor_copy(f.last_col[W:P, b, :], mem.bank0[W:P, P - 1:P]).then_inc(sem["hT_ready"], 1)

            def mask_and_max(i, t, b):
                r = b % 2
                dve.wait_ge(sem["sims_done"], at(i))
                if later(i, t, 2):
                    dve.wait_ge(sem["exp_ready"], at(i) - 2)
                nc.vector.tensor_tensor(f.logits[:, r], mem.bank67[:, :].rearrange("p (h k) -> p h k", h=H),
                                        f.mask[:, t, :].unsqueeze(1).to_broadcast([P, H, P]),
                                        ALU.add).then_inc(sem["masked"], 1)
                dve.wait_ge(sem["masked"], at(i))
                nc.vector.tensor_reduce(f.neg_max[:, b, 0, :], f.logits[:, r], AX.X,
                                        ALU.max).then_inc(sem["max_found"], 1)
                dve.wait_ge(sem["max_found"], at(i))
                nc.vector.tensor_scalar(f.neg_max[:, b, 1, :], f.neg_max[:, b, 0, :], -QK_SCALE, None,
                                        ALU.mult).then_inc(sem["max_ready"], 1)

            def invert_sums(i, t, b):
                dve.wait_ge(sem["exp_ready"], at(i))
                nc.vector.reciprocal(f.sums[:, b, 1, :], f.sums[:, b, 0, :]).then_inc(sem["sums_inverted"], 1)

            def sum_squares(i, t, b):
                r = b % 2
                dve.wait_ge(sem["squares_ready"], at(i))
                nc.vector.tensor_reduce(f.ss[:, b, :], f.sq[:, r, :].rearrange("p (h d) -> p h d", d=D), AX.X,
                                        ALU.add).then_inc(sem["ss_clamped"], 1)
                dve.wait_ge(sem["ss_clamped"], at(i))
                nc.vector.tensor_scalar(f.ss[:, b, :], f.ss[:, b, :], 1e-24, None,
                                        ALU.max).then_inc(sem["ss_ready"], 1)

            def rotate(i, t, b):
                r = b % 2
                if later(i, t, 2):
                    dve.wait_ge(sem["kT_done"], at(i) - 2)
                qk = mem.bank12[:, :].rearrange("p (a h d) -> p a h d", a=2, h=H)
                out_c = f.rot_c[:, r].rearrange("p (a h) d -> p a h d", a=2)
                out_s = f.rot_s[:, r].rearrange("p (a h) d -> p a h d", a=2)

                def table(part, lo):
                    return f.rope[:, t, 2 * part:2 * part + 2, lo:lo + (D if part == 0 else D // 2)] \
                        .unsqueeze(2).to_broadcast([P, 2, H, D if part == 0 else D // 2])

                nc.vector.tensor_tensor(out_c, qk, table(0, 0), ALU.mult)
                nc.vector.tensor_tensor(out_s[:, :, :, 0:32], qk[:, :, :, 32:64], table(1, 0), ALU.mult)
                nc.vector.tensor_tensor(out_s[:, :, :, 32:64], qk[:, :, :, 0:32], table(1, 32),
                                        ALU.mult).then_inc(sem["rotated"], 1)

            def keep_keys(i, t, b):
                if not later(i, t, B):
                    return
                dve.wait_ge(sem["sims_done"], at(i) - B)
                nc.vector.tensor_copy(f.kT[:, b, :, 1, :], f.kT[:, b, :, 2, :]).then_inc(sem["keys_kept"], 1)

            def keep_values(i, t, b):
                if not later(i, t, B):
                    return
                dve.wait_ge(sem["pv_done"], at(i) - B)
                nc.vector.tensor_copy(f.v0[W:P, b, :], f.v[W:P, b, :]).then_inc(sem["values_kept"], 1)

            def update(i, t, b):
                dve.wait_ge(sem["wo_done"], at(i))
                nc.vector.tensor_tensor(u_buf[:, b, t + 1, :], u_buf[:, b, t + 1, :], mem.bank0[:, 0:P],
                                        ALU.add).then_inc(sem["u_updated"], 1)

            def kT(i, t, b):
                dve.wait_ge(sem["kT_done"], at(i))
                if later(i, t, B):
                    dve.wait_ge(sem["keys_kept"], (at(i) - B) - B * run)
                nc.vector.tensor_copy(f.kT[:, b, :, 0:3:2, :],
                                      mem.bank45[:, 512:1024].rearrange("p (c w k) -> p c w k", c=4, w=2)) \
                    .then_inc(sem["kT_ready"], 1)

            nc.vector.tensor_tensor(f.rope[:, :, :, :], f.rope_raw[:, :, :, :],
                                    f.qk_scales[:, layer].unsqueeze(1).to_broadcast([P, T, 4, D]),
                                    ALU.mult).then_inc(sem["tables_ready"], 1)
            nc.vector.memset(f.last_col[:, :, :], 0.0).then_inc(sem["tables_ready"], 1)
            dve.wait_ge(sem["tables_ready"], 7 * (run // 2) + (7 if layer else 5))
            hT(0, 0, 0)
            run_steps(dve, B, NT, LAG_PV, step_of([
                (LAG_SCALE, invert_sums), (LAG_SOFTMAX, mask_and_max), (1, keep_values), (1, keep_keys), (0, sum_squares), (1, kT),
                (-1, hT), (0, rotate), (LAG_PV, update)]), ahead=1)

        @block.scalar
        def _(act):
            def pT(i, t, b):
                act.wait_ge(sem["pT_done"], at(i))
                if later(i, t, 2):
                    act.wait_ge(sem["pv_done"], at(i) - 2)
                nc.scalar.copy(f.pT[:, b % 2], mem.bank45[:, :].rearrange("p (h q) -> p h q", h=H)) \
                    .then_inc(sem["pT_ready"], 1)

            def exps(i, t, b):
                act.wait_ge(sem["max_ready"], at(i))
                if later(i, t, B):
                    act.wait_ge(sem["pT_done"], at(i) - B)
                for h in range(H):
                    last = nc.scalar.activation(f.probs[:, b, h, :], f.logits[:, b % 2, h, :], ACT.Exp,
                                                bias=f.neg_max[:, b, 1, h:h + 1], scale=QK_SCALE,
                                                accum_out=f.sums[:, b, 0, h:h + 1])
                last.then_inc(sem["exp_ready"], 1)

            def oT(i, t, b):
                act.wait_ge(sem["pv_done"], at(i))
                if later(i, t, 2):
                    act.wait_ge(sem["wo_done"], at(i) - 2)
                nc.scalar.copy(f.oT[:, b % 2], mem.bank3[:, :].rearrange("p (c q) -> p c q", c=4)) \
                    .then_inc(sem["oT_ready"], 1)

            def squares(i, t, b):
                act.wait_ge(sem["qk_done"], at(i))
                if later(i, t, 2):
                    act.wait_ge(sem["ss_ready"], at(i) - 2)
                nc.scalar.activation(f.sq[:, b % 2, :], mem.bank12[:, :], ACT.Square) \
                    .then_inc(sem["squares_ready"], 1)

            def qT(i, t, b):
                act.wait_ge(sem["qT_done"], at(i))
                if later(i, t, 2):
                    act.wait_ge(sem["sims_done"], at(i) - 2)
                for e in range(2):
                    rows = slice(e * D, (e + 1) * D)
                    last = nc.scalar.copy(f.qT[rows, b % 2, :, e, :],
                                          mem.bank45[rows, 0:512].rearrange("p (c q) -> p c q", c=4))
                last.then_inc(sem["qT_ready"], 1)

            def values(i, t, b):
                act.wait_ge(sem["v_done"], at(i))
                if later(i, t, B):
                    act.wait_ge(sem["values_kept"], (at(i) - B) - B * run)
                nc.scalar.copy(f.v[:, b, :], mem.bank3[:, :])
                nc.scalar.copy(f.v0[0:W, b, :], mem.bank3[0:W, :]).then_inc(sem["v_ready"], 1)

            run_steps(act, B, NT, LAG_PV, step_of([
                (LAG_PV, pT), (0, squares), (LAG_PV, oT), (1, qT), (LAG_SOFTMAX, exps), (1, values)]))

        @block.tensor
        def _(pe):
            def transpose_probs(i, t, b):
                pe.wait_ge(sem["probs_ready"], at(i))
                pe.wait_ge(sem["qT_ready"], at(min(i + LAG_PV - 2, NT - 1) if isinstance(i, int) else i + LAG_PV - 2))
                pe.wait_ge(sem["kT_ready"], at(min(i + LAG_PV - 2, NT - 1) if isinstance(i, int) else i + LAG_PV - 2))
                for h in range(H):
                    last = nc.tensor.transpose(mem.bank45[:, h * P:(h + 1) * P], f.probs[:, b, h, :],
                                               mem.ident[:, :])
                last.then_inc(sem["pT_done"], 1)

            def transpose_u(i, t, b):
                pe.wait_ge(sem["tile_copied"], at(i))
                if later(i, t, LAG_PV + 2):
                    pe.wait_ge(sem["u_updated"], at(i) - LAG_PV - 2)
                if later(i, t, 1):
                    pe.wait_ge(sem["hT_ready"], at(i) - 1)
                nc.tensor.transpose(mem.bank0[:, 0:P], f.u_tile[:, b, :], mem.ident[:, :]) \
                    .then_inc(sem["uT_done"], 1)

            def values_by_probs(i, t, b):
                pe.wait_ge(sem["pT_ready"], at(i))
                pe.wait_ge(sem["v_ready"], at(min(i + LAG_PV - 2, NT - 1) if isinstance(i, int) else i + LAG_PV - 2))
                for c in range(4):
                    for e in range(2):
                        cols = slice((2 * c + e) * D, (2 * c + e + 1) * D)
                        for w, v in ((0, f.v0), (1, f.v)):
                            last = nc.tensor.matmul(
                                mem.bank3[e * D:(e + 1) * D, c * P + w * W:c * P + (w + 1) * W],
                                v[:, b, cols], f.pT[:, b % 2, 4 * e + c, w * W:(w + 1) * W],
                                start=True, stop=True)
                last.then_inc(sem["pv_done"], 1)

            def queries_keys(i, t, b):
                pe.wait_ge(sem["hT_ready"], at(i))
                if later(i, t, 1):
                    pe.wait_ge(sem["rotated"], at(i) - 1)
                for a in range(2):
                    last = nc.tensor.matmul(mem.bank12[:, a * 512:(a + 1) * 512], f.hT[:, b, :],
                                            f.wqkv[:, layer, a * 512:(a + 1) * 512], start=True, stop=True)
                last.then_inc(sem["qk_done"], 1)

            def out_proj(i, t, b):
                pe.wait_ge(sem["oT_ready"], at(i))
                pe.wait_ge(sem["hT_ready"], at(min(i + LAG_PV + 1, NT - 1) if isinstance(i, int) else i + LAG_PV + 1))
                if later(i, t, 1):
                    pe.wait_ge(sem["u_updated"], at(i) - 1)
                for c in range(4):
                    last = nc.tensor.matmul(mem.bank0[:, 0:P], f.oT[:, b % 2, c, :], f.wo[:, layer, c, :],
                                            start=(c == 0), stop=(c == 3))
                last.then_inc(sem["wo_done"], 1)

            def transpose_qk(i, t, b):
                pe.wait_ge(sem["qk_normed"], at(i))
                if later(i, t, LAG_PV - 1):
                    pe.wait_ge(sem["pT_ready"], at(i) - (LAG_PV - 1))
                if later(i, t, 1):
                    pe.wait_ge(sem["qT_ready"], at(i) - 1)
                    pe.wait_ge(sem["kT_ready"], at(i) - 1)
                for a, done in ((0, "qT_done"), (1, "kT_done")):
                    for c in range(4):
                        last = nc.tensor.transpose(mem.bank45[:, (4 * a + c) * P:(4 * a + c + 1) * P],
                                                   f.rot_c[:, b % 2, 8 * a + 2 * c:8 * a + 2 * c + 2, :],
                                                   mem.ident[:, :])
                    last.then_inc(sem[done], 1)

            def values(i, t, b):
                if later(i, t, LAG_PV - 1):
                    pe.wait_ge(sem["oT_ready"], at(i) - (LAG_PV - 1))
                if later(i, t, 1):
                    pe.wait_ge(sem["v_ready"], at(i) - 1)
                nc.tensor.matmul(mem.bank3[:, :], f.hT[:, b, :], f.wqkv[:, layer, 1024:1536],
                                 start=True, stop=True).then_inc(sem["v_done"], 1)

            def sims(i, t, b):
                pe.wait_ge(sem["qT_ready"], at(i))
                pe.wait_ge(sem["kT_ready"], at(i))
                if later(i, t, 1):
                    pe.wait_ge(sem["masked"], at(i) - 1)
                for c in range(4):
                    for e in range(2):
                        for w in range(2):
                            keys = f.kT[:, b, c, 0:2, :] if w == 0 else f.kT[:, b, c, 0:3:2, :]
                            last = nc.tensor.matmul(
                                mem.bank67[w * W:(w + 1) * W, e * 512 + c * P:e * 512 + (c + 1) * P],
                                f.qT[:, b % 2, c, e, w * W:(w + 1) * W], keys, start=True, stop=True)
                last.then_inc(sem["sims_done"], 1)

            transpose_u(0, 0, 0)
            run_steps(pe, B, NT, LAG_PV, step_of([
                (LAG_PV, transpose_probs), (0, queries_keys), (LAG_PV, values_by_probs), (1, transpose_qk),
                (-1, transpose_u), (1, values), (LAG_PV, out_proj), (1, sims)]), ahead=1)


def feed_forward(nc, mem, f, sem, src, dst, layer, run):
    n = NT // 2
    base = n * run

    def at(j):
        return base + j + 1

    def later(j, count):
        return not isinstance(j, int) or j >= count

    def step_of(stages):
        def step(k, u, m=None):
            for lag, stage in stages:
                group = tile_of(k, u, m, lag, 2, n)
                if group is not None:
                    stage(*group)
        return step

    LAG = 2

    with nc.Block() as block:

        @block.gpsimd
        def _(pool):
            def low(j, t, r):
                if later(j, 2):
                    pool.wait_ge(sem["f_normed"], at(j) - 2)
                wait_apart(pool, j)
                nc.gpsimd.tensor_copy(f.h[:, r, :, 0:W], src[:, 2 * r:2 * r + 2, t + 1, 0:W]) \
                    .then_inc(sem["f_lo_ready"], 1)

            def rstd(j, t, r):
                pool.wait_ge(sem["f_var_ready"], at(j))
                wait_apart(pool, j)
                nc.gpsimd.tensor_scalar(f.rstd[:, r, :], f.moments[:, r, :, 1], LN_EPS, None,
                                        ALU.add).then_inc(sem["f_eps_added"], 1)
                pool.wait_ge(sem["f_eps_added"], at(j))
                nc.gpsimd.tensor_tensor(f.rstd[:, r, :], f.rstd[:, r, :], f.minus_half[:, 0:2],
                                        ALU.pow).then_inc(sem["f_rstd_ready"], 1)

            def add_bias(j, t, r):
                nc.gpsimd.tensor_tensor(dst[:, 2 * r:2 * r + 2, t + 1, :], src[:, 2 * r:2 * r + 2, t + 1, :],
                                        f.b2[:, layer].unsqueeze(1).to_broadcast([P, 2, P]),
                                        ALU.add).then_inc(sem["f_bias_added"], 1)

            low(0, 0, 0)
            run_steps(pool, 2, n, LAG, step_of([(-1, low), (0, rstd), (1, add_bias)]), ahead=1)

        @block.vector
        def _(dve):
            def stats(j, t, r):
                dve.wait_ge(sem["f_shifted"], at(j))
                if later(j, 2):
                    dve.wait_ge(sem["f_normed"], at(j) - 2)
                nc.vector.tensor_copy(f.h[:, r, :, W:P], mem.bank0[:, 0:P].rearrange("p (a c) -> p a c", a=2)) \
                    .then_inc(sem["f_hi_ready"], 1)
                dve.wait_ge(sem["f_hi_ready"], at(j))
                dve.wait_ge(sem["f_lo_ready"], at(j))
                nc.vector.bn_stats(f.stats[:, r, 0, :], f.h[:, r, 0, :])
                nc.vector.bn_stats(f.stats[:, r, 1, :], f.h[:, r, 1, :]).then_inc(sem["f_stats"], 1)
                dve.wait_ge(sem["f_stats"], at(j))
                wait_apart(dve, j)
                nc.vector.bn_aggr(f.moments[:, r, 0, :], f.stats[:, r, 0, :])
                nc.vector.bn_aggr(f.moments[:, r, 1, :], f.stats[:, r, 1, :]).then_inc(sem["f_var_ready"], 1)

            def normalise(j, t, r):
                dve.wait_ge(sem["f_rstd_ready"], at(j))
                if later(j, 2):
                    dve.wait_ge(sem["f_hnT_done"], at(j) - 2)
                for a in range(2):
                    last = nc.vector.tensor_scalar(f.hn[:, r, a, :], f.h[:, r, a, :], f.moments[:, r, a, 0:1],
                                                   f.rstd[:, r, a:a + 1], ALU.subtract, ALU.mult)
                last.then_inc(sem["f_normed"], 1)

            def gate(j, t, r):
                dve.wait_ge(sem["f_gelu_ready"], at(j))
                if later(j, 2):
                    dve.wait_ge(sem["f_down_done"], at(j) - 2)
                for c, (_, m) in enumerate(CH):
                    last = nc.vector.scalar_tensor_tensor(
                        out=f.hidden[0:m, r, c, :], in0=mem.bank45[0:m, c * 256:(c + 1) * 256],
                        scalar=f.b1[0:m, layer, 0, c:c + 1], in1=f.gelu[0:m, r, c, :],
                        op0=ALU.add, op1=ALU.mult)
                last.then_inc(sem["f_hidden_ready"], 1)

            def output(j, t, r):
                dve.wait_ge(sem["f_down_done"], at(j))
                dve.wait_ge(sem["f_bias_added"], at(j))
                nc.vector.tensor_tensor(dst[:, 2 * r:2 * r + 2, t + 1, :], dst[:, 2 * r:2 * r + 2, t + 1, :],
                                        mem.bank67[:, 0:256].rearrange("p (a c) -> p a c", a=2),
                                        ALU.add).then_inc(sem["f_out_ready"], 1)

            run_steps(dve, 2, n, LAG, step_of([(0, stats), (LAG, output), (0, normalise), (1, gate)]))

        @block.scalar
        def _(act):
            def hnT(j, t, r):
                act.wait_ge(sem["f_hnT_done"], at(j))
                if later(j, 2):
                    act.wait_ge(sem["f_up_done"], at(j) - 2)
                nc.scalar.activation(f.hnT[:, r, :], mem.bank3[:, 0:256], ACT.Identity,
                                     bias=f.lnp[:, layer, 1:2], scale=f.lnp[:, layer, 0:1]) \
                    .then_inc(sem["f_hnT_ready"], 1)

            def gelu(j, t, r):
                act.wait_ge(sem["f_up_done"], at(j))
                if later(j, 2):
                    act.wait_ge(sem["f_hidden_ready"], at(j) - 2)
                for c, (_, m) in enumerate(CH):
                    last = nc.scalar.activation(f.gelu[0:m, r, c, :], mem.bank12[0:m, c * 256:(c + 1) * 256],
                                                ACT.Gelu, bias=f.b1[0:m, layer, 1, c:c + 1])
                last.then_inc(sem["f_gelu_ready"], 1)

            run_steps(act, 2, n, LAG, step_of([(1, hnT), (1, gelu)]))

        @block.tensor
        def _(pe):
            def down(j, t, r):
                pe.wait_ge(sem["f_hidden_ready"], at(j))
                if later(j, 1):
                    pe.wait_ge(sem["f_out_ready"], at(j) - 1)
                for a in range(2):
                    for c, (_, m) in enumerate(CH):
                        last = nc.tensor.matmul(mem.bank67[:, a * P:(a + 1) * P],
                                                f.hidden[0:m, r, c, a * P:(a + 1) * P],
                                                f.w2[0:m, layer, c, :], start=(c == 0), stop=(c == 2))
                last.then_inc(sem["f_down_done"], 1)

            def shift_rows(j, t, r):
                if later(j, 1):
                    pe.wait_ge(sem["f_hi_ready"], at(j) - 1)
                nc.tensor.matmul(mem.bank0[:, 0:P], f.shift[:, 0, :], src[:, 2 * r:2 * r + 2, t + 1, W:P],
                                 start=True, stop=False)
                nc.tensor.matmul(mem.bank0[:, 0:P], f.shift[:, 1, :], src[:, 2 * r:2 * r + 2, t, W:P],
                                 start=False, stop=True).then_inc(sem["f_shifted"], 1)

            def transpose_hn(j, t, r):
                pe.wait_ge(sem["f_normed"], at(j))
                if later(j, 1):
                    pe.wait_ge(sem["f_hnT_ready"], at(j) - 1)
                for a in range(2):
                    last = nc.tensor.transpose(mem.bank3[:, a * P:(a + 1) * P], f.hn[:, r, a, :],
                                               mem.ident[:, :])
                last.then_inc(sem["f_hnT_done"], 1)

            def up(j, t, r):
                pe.wait_ge(sem["f_hnT_ready"], at(j))
                if later(j, 1):
                    pe.wait_ge(sem["f_gelu_ready"], at(j) - 1)
                    pe.wait_ge(sem["f_hidden_ready"], at(j) - 1)
                for half, bank in ((1, mem.bank12), (0, mem.bank45)):
                    for c, (c0, m) in enumerate(CH):
                        last = nc.tensor.matmul(bank[0:m, c * 256:(c + 1) * 256],
                                                f.w1[:, layer, half * HID + c0:half * HID + c0 + m],
                                                f.hnT[:, r, :], start=True, stop=True)
                last.then_inc(sem["f_up_done"], 1)

            run_steps(pe, 2, n, LAG, step_of([(0, shift_rows), (LAG, down), (1, transpose_hn), (1, up)]))



HEADS_A = 16
DA = 8
SCALE_A = DA ** -0.5
GROUP = 4
NG = NT // GROUP


class AttnAMemory:

    def __init__(self, nc, ctx):
        def sb(name, shape):
            return ctx.enter_context(nc.sbuf_tensor(name, shape, F32))

        self.xp = sb("a_x", [P, NT, P])
        self.w = sb("a_weights", [P, 7, P])
        self.bias_ch = sb("a_bias_ch", [P, 3])
        self.bias_row = sb("a_bias_row", [P, 4, P])
        self.blocks = sb("a_blocks", [P, P])
        self.stats = sb("a_stats", [P, NT, 6])
        self.moments = sb("a_moments", [P, NT, 2])
        self.rstd = sb("a_rstd", [P, NT])
        self.xn = sb("a_xn", [P, 2, GROUP, P])
        self.xT = sb("a_xT", [P, 2, GROUP * P])
        self.hq = sb("a_hidden", [P, 2, NG, GROUP * P])
        self.vT = sb("a_vT", [P, NG, GROUP * P])
        self.g_in = sb("a_g_in", [P, 2, GROUP, P])
        self.g = sb("a_g", [P, NG, GROUP, P])
        self.lin = sb("a_lin", [P, 2, 2, GROUP, P])
        self.log = sb("a_log", [P, 2, 2, GROUP, P])
        self.qk = sb("a_qk", [P, 2, 2, GROUP, P])
        self.heads = sb("a_heads", [P, B, P])
        self.z = sb("a_z", [P, B, 3])
        self.mix = sb("a_mix", [P, B, P])
        self.mixT = sb("a_mixT", [P, B, P])
        self.o = self.xp[:, :, :].rearrange("p (a h) (j n) -> p a h j n", a=2, n=DA)
        self.rows = sb("a_rows", [P, 2, 2, HEADS_A, W])


A_SEMS = ("a_stats_done", "a_var", "a_eps", "a_rstd", "a_normed", "a_xT_done", "a_xT_ready", "a_up_done", "a_hidden_ready",
          "a_g_in_ready", "a_g_ready", "a_lin_done", "a_lin_ready", "a_abs", "a_exp", "a_log_ready", "a_qk_ready",
          "a_heads_done", "a_heads_ready", "a_z_sum", "a_z_den", "a_z_ready", "a_mix_sum", "a_mix_ready", "a_mixT_done",
          "a_mixT_ready", "a_o_done", "a_o_ready", "a_rows_done", "a_rows_ready", "a_y_done", "a_y_added",
          "a_bias_added")


def linear_attention(nc, mem, a, sem):

    def step_of(stages):
        def step(k, u, m=None):
            for lag, stage in stages:
                group = tile_of(k, u, m, lag, 2, NG)
                if group is not None:
                    i, _, r = group
                    stage(i, r)
        return step

    def later(i, count):
        return not isinstance(i, int) or i >= count

    with nc.Block() as block:

        @block.vector
        def _(dve):
            for i in range(NT):
                last = nc.vector.bn_stats(a.stats[:, i, :], a.xp[:, i, :])
            last.then_inc(sem["a_stats_done"], 1)
            dve.wait_ge(sem["a_stats_done"], 1)
            for i in range(NT):
                last = nc.vector.bn_aggr(a.moments[:, i, :], a.stats[:, i, :])
            last.then_inc(sem["a_var"], 1)
            dve.wait_ge(sem["a_rstd"], 1)

            def normalise(i, r):
                if later(i, 2):
                    dve.wait_ge(sem["a_xT_done"], i - 1)
                for n in range(GROUP):
                    tile = GROUP * i + n
                    last = nc.vector.tensor_scalar(a.xn[:, r, n, :], a.xp[:, tile, :], a.moments[:, tile, 0:1],
                                                   a.rstd[:, bass.ds(tile, 1)], ALU.subtract, ALU.mult)
                last.then_inc(sem["a_normed"], 1)

            def xT(i, r):
                dve.wait_ge(sem["a_xT_done"], i + 1)
                if later(i, 2):
                    dve.wait_ge(sem["a_up_done"], i - 1)
                nc.vector.tensor_copy(a.xT[:, r, :], mem.bank0[:, :]).then_inc(sem["a_xT_ready"], 1)

            def g_in(i, r):
                dve.wait_ge(sem["a_up_done"], i + 1)
                if later(i, 2):
                    dve.wait_ge(sem["a_g_ready"], i - 1)
                nc.vector.tensor_tensor(a.g_in[:, r], mem.bank45[:, 0:512].rearrange("p (n c) -> p n c", c=P),
                                        a.bias_row[:, 0].unsqueeze(1).to_broadcast([P, GROUP, P]),
                                        ALU.add).then_inc(sem["a_g_in_ready"], 1)

            run_steps(dve, 2, NG, 1, step_of([(0, normalise), (0, xT), (1, g_in)]))

        @block.gpsimd
        def _(pool):
            pool.wait_ge(sem["a_var"], 1)
            nc.gpsimd.tensor_scalar(a.rstd[:, :], a.moments[:, :, 1], LN_EPS, None,
                                    ALU.add).then_inc(sem["a_eps"], 1)
            pool.wait_ge(sem["a_eps"], 1)
            nc.gpsimd.tensor_tensor(a.rstd[:, :], a.rstd[:, :], mem.minus_half[:, :],
                                    ALU.pow).then_inc(sem["a_rstd"], 1)
            nc.gpsimd.tensor_tensor(mem.x[:, :, :, :].rearrange("p b t c -> p (b t) c"),
                                    mem.x[:, :, :, :].rearrange("p b t c -> p (b t) c"),
                                    a.bias_row[:, 3].unsqueeze(1).to_broadcast([P, NT, P]),
                                    ALU.add).then_inc(sem["a_bias_added"], 1)

        @block.scalar
        def _(act):
            def gelus(i, r):
                act.wait_ge(sem["a_up_done"], i + 1)
                nc.scalar.activation(a.hq[:, 0, i, :], mem.bank12[:, 0:512], ACT.Gelu, bias=a.bias_ch[:, 0:1])
                nc.scalar.activation(a.hq[:, 1, i, :], mem.bank12[:, 512:1024], ACT.Gelu, bias=a.bias_ch[:, 1:2])
                nc.scalar.activation(a.vT[:, i, :], mem.bank3[:, :], ACT.Gelu, bias=a.bias_ch[:, 2:3]) \
                    .then_inc(sem["a_hidden_ready"], 1)
                act.wait_ge(sem["a_g_in_ready"], i + 1)
                nc.scalar.activation(a.g[:, i], a.g_in[:, r], ACT.Gelu).then_inc(sem["a_g_ready"], 1)

            run_steps(act, 2, NG, 1, step_of([(1, gelus)]))

        @block.tensor
        def _(pe):
            def transposes(i, r):
                pe.wait_ge(sem["a_normed"], i + 1)
                if later(i, 1):
                    pe.wait_ge(sem["a_xT_ready"], i)
                for n in range(GROUP):
                    last = nc.tensor.transpose(mem.bank0[:, n * P:(n + 1) * P], a.xn[:, r, n, :], mem.ident[:, :])
                last.then_inc(sem["a_xT_done"], 1)

            def products(i, r):
                pe.wait_ge(sem["a_xT_ready"], i + 1)
                if later(i, 1):
                    pe.wait_ge(sem["a_hidden_ready"], i)
                    pe.wait_ge(sem["a_g_in_ready"], i)
                for n, bank in enumerate((mem.bank12[:, 0:512], mem.bank12[:, 512:1024], mem.bank3[:, :])):
                    nc.tensor.matmul(bank, a.w[:, n, :], a.xT[:, r, :], start=True, stop=True)
                for n in range(GROUP):
                    last = nc.tensor.matmul(mem.bank45[:, n * P:(n + 1) * P], a.xT[:, r, n * P:(n + 1) * P],
                                            a.w[:, 3, :], start=True, stop=True)
                last.then_inc(sem["a_up_done"], 1)

            run_steps(pe, 2, NG, 1, step_of([(0, transposes), (1, products)]))

    with nc.Block() as block:

        @block.vector
        def _(dve):
            def linear(i):
                dve.wait_ge(sem["a_lin_done"], i + 1)
                if i >= 2:
                    dve.wait_ge(sem["a_qk_ready"], i - 1)
                nc.vector.tensor_tensor(a.lin[:, i % 2], mem.bank12[:, :].rearrange("p (a n c) -> p a n c", a=2, c=P),
                                        a.bias_row[:, 1:3].unsqueeze(2).to_broadcast([P, 2, GROUP, P]),
                                        ALU.add).then_inc(sem["a_lin_ready"], 1)

            def softplus(i):
                dve.wait_ge(sem["a_log_ready"], i + 1)
                if i >= 2:
                    dve.wait_ge(sem["a_heads_done"], i - 1)
                nc.vector.scalar_tensor_tensor(
                    out=a.qk[:, i % 2].rearrange("p a n c -> p (a n c)"),
                    in0=a.lin[:, i % 2].rearrange("p a n c -> p (a n c)"), scalar=0.0,
                    in1=a.log[:, i % 2].rearrange("p a n c -> p (a n c)"),
                    op0=ALU.max, op1=ALU.add).then_inc(sem["a_qk_ready"], 1)

            def mix(pair):
                dve.wait_ge(sem["a_heads_done"], NG // 2 * (pair + 1))
                for e in range(2):
                    b = 2 * pair + e
                    nc.vector.tensor_tensor(a.heads[:, b, :], mem.bank67[:, e * 512:e * 512 + P], a.blocks[:, :],
                                            ALU.mult).then_inc(sem["a_heads_ready"], 1)
                dve.wait_ge(sem["a_heads_ready"], 2 * (pair + 1))
                bs = slice(2 * pair, 2 * pair + 2)
                nc.vector.tensor_reduce(a.z[:, bs, 0], a.heads[:, bs, :], AX.X, ALU.add).then_inc(sem["a_z_sum"], 1)
                dve.wait_ge(sem["a_z_sum"], pair + 1)
                nc.vector.tensor_scalar(a.z[:, bs, 1], a.z[:, bs, 0], SCALE_A, float(P), ALU.mult,
                                        ALU.add).then_inc(sem["a_z_den"], 1)
                dve.wait_ge(sem["a_z_den"], pair + 1)
                nc.vector.reciprocal(a.z[:, bs, 2], a.z[:, bs, 1]).then_inc(sem["a_z_ready"], 1)
                for b in (2 * pair, 2 * pair + 1):
                    nc.vector.scalar_tensor_tensor(out=a.mix[:, b, :], in0=a.heads[:, b, :], scalar=SCALE_A,
                                                   in1=mem.ident[:, :], op0=ALU.mult,
                                                   op1=ALU.add).then_inc(sem["a_mix_sum"], 1)
                dve.wait_ge(sem["a_z_ready"], pair + 1)
                dve.wait_ge(sem["a_mix_sum"], 2 * (pair + 1))
                for b in (2 * pair, 2 * pair + 1):
                    nc.vector.tensor_scalar(a.mix[:, b, :], a.mix[:, b, :], a.z[:, b, 2:3], None,
                                            ALU.mult).then_inc(sem["a_mix_ready"], 1)
                dve.wait_ge(sem["a_mixT_done"], pair + 1)
                nc.vector.tensor_copy(a.mixT[:, bs, :], mem.bank0[:, 0:256].rearrange("p (b c) -> p b c", b=2)) \
                    .then_inc(sem["a_mixT_ready"], 1)

            def gated(i):
                pair, j = i // 4, GROUP * (i % 4)
                dve.wait_ge(sem["a_o_done"], i + 1)
                nc.vector.tensor_tensor(a.o[:, pair, :, j:j + GROUP, :].rearrange("p h j n -> p j h n"),
                                        mem.bank45[:, i % 2 * 512:(i % 2 + 1) * 512].rearrange("p (j h n) -> p j h n", j=GROUP, n=DA),
                                        a.g[:, i].rearrange("p j (h n) -> p j h n", n=DA),
                                        ALU.mult).then_inc(sem["a_o_ready"], 1)

            def residual(n):
                b, t = n // 2, 4 * (n % 2)
                dve.wait_ge(sem["a_y_done"], n + 1)
                nc.vector.tensor_tensor(mem.x[:, b, t:t + 4, :], mem.x[:, b, t:t + 4, :],
                                        mem.bank67[:, n % 2 * 512:(n % 2 + 1) * 512].rearrange("p (t c) -> p t c", t=4),
                                        ALU.add).then_inc(sem["a_y_added"], 1)

            for i in range(NG + 1):
                if i < NG:
                    linear(i)
                if i > 0:
                    softplus(i - 1)
                if i == NG // 2:
                    mix(0)
            mix(1)
            for i in range(NG):
                gated(i)
            for n in range(NG):
                residual(n)

        @block.scalar
        def _(act):
            for i in range(NG):
                r = i % 2
                act.wait_ge(sem["a_lin_ready"], i + 1)
                if i >= 2:
                    act.wait_ge(sem["a_qk_ready"], i - 1)
                nc.scalar.activation(a.log[:, r], a.lin[:, r], ACT.Abs).then_inc(sem["a_abs"], 1)
                act.wait_ge(sem["a_abs"], i + 1)
                nc.scalar.activation(a.log[:, r], a.log[:, r], ACT.Exp, scale=-1.0).then_inc(sem["a_exp"], 1)
                act.wait_ge(sem["a_exp"], i + 1)
                nc.scalar.activation(a.log[:, r], a.log[:, r], ACT.Ln, bias=1.0).then_inc(sem["a_log_ready"], 1)
            for n in range(NG):
                pair, h = n // 4, 4 * (n % 4)
                act.wait_ge(sem["a_rows_done"], n + 1)
                nc.scalar.copy(a.rows[:, pair, :, h:h + 4, :].rearrange("p e h r -> p h e r"),
                               mem.bank12[:, n % 2 * 512:(n % 2 + 1) * 512].rearrange("p (h e r) -> p h e r", h=4, e=2)) \
                    .then_inc(sem["a_rows_ready"], 1)

        @block.tensor
        def _(pe):
            def second(i):
                if i >= 1:
                    pe.wait_ge(sem["a_lin_ready"], i)
                for q in range(2):
                    for n in range(GROUP):
                        last = nc.tensor.matmul(mem.bank12[:, q * 512 + n * P:q * 512 + (n + 1) * P],
                                                a.hq[:, q, i, n * P:(n + 1) * P], a.w[:, 4 + q, :],
                                                start=True, stop=True)
                last.then_inc(sem["a_lin_done"], 1)

            def heads(i):
                pe.wait_ge(sem["a_qk_ready"], i + 1)
                if i == NG // 2:
                    pe.wait_ge(sem["a_heads_ready"], 2)
                for n in range(GROUP):
                    for e in range(2):
                        rows = slice(e * W, (e + 1) * W)
                        last = nc.tensor.matmul(mem.bank67[:, e * 512:e * 512 + P], a.qk[rows, i % 2, 0, n, :],
                                                a.qk[rows, i % 2, 1, n, :], start=(i % 4 == 0 and n == 0),
                                                stop=(i % 4 == 3 and n == GROUP - 1))
                last.then_inc(sem["a_heads_done"], 1)

            def turn_mix(pair):
                pe.wait_ge(sem["a_mix_ready"], 2 * (pair + 1))
                if pair:
                    pe.wait_ge(sem["a_mixT_ready"], pair)
                for e in range(2):
                    last = nc.tensor.transpose(mem.bank0[:, e * P:(e + 1) * P], a.mix[:, 2 * pair + e, :], mem.ident[:, :])
                last.then_inc(sem["a_mixT_done"], 1)

            def outputs(i):
                pair = i // 4
                pe.wait_ge(sem["a_mixT_ready"], pair + 1)
                if i >= 2:
                    pe.wait_ge(sem["a_o_ready"], i - 1)
                for n in range(GROUP):
                    for e in range(2):
                        last = nc.tensor.matmul(mem.bank45[e * W:(e + 1) * W, i % 2 * 512 + n * P:i % 2 * 512 + (n + 1) * P],
                                                a.vT[:, i, n * P + e * W:n * P + (e + 1) * W], a.mixT[:, 2 * pair + e, :],
                                                start=True, stop=True)
                last.then_inc(sem["a_o_done"], 1)

            def turn_rows(n):
                pair, h = n // 4, 4 * (n % 4)
                pe.wait_ge(sem["a_o_ready"], 4 * (pair + 1))
                if n >= 2:
                    pe.wait_ge(sem["a_rows_ready"], n - 1)
                for q in range(4):
                    last = nc.tensor.transpose(mem.bank12[:, n % 2 * 512 + q * P:n % 2 * 512 + (q + 1) * P],
                                               a.o[:, pair, h + q, :, :], mem.ident[:, :])
                last.then_inc(sem["a_rows_done"], 1)

            def project(n):
                b, t = n // 2, 4 * (n % 2)
                pe.wait_ge(sem["a_rows_ready"], 4 * (b // 2 + 1))
                if n >= 2:
                    pe.wait_ge(sem["a_y_added"], n - 1)
                for q in range(4):
                    last = nc.tensor.matmul(mem.bank67[:, n % 2 * 512 + q * P:n % 2 * 512 + (q + 1) * P],
                                            a.rows[:, b // 2, b % 2, 2 * (t + q):2 * (t + q) + 2, :],
                                            a.w[:, 6, :], start=True, stop=True)
                last.then_inc(sem["a_y_done"], 1)

            for i in range(NG + 1):
                if i < NG:
                    second(i)
                if i > 0:
                    heads(i - 1)
                if i == NG // 2:
                    turn_mix(0)
            turn_mix(1)
            for i in range(NG):
                outputs(i)
            for n in range(NG):
                turn_rows(n)
            for n in range(NG):
                project(n)


def attn_a_inputs(nc, a, arr, loaded):
    loads = [(a.xp[64 * (b % 2):64 * (b % 2) + 64, 16 * (b // 2):16 * (b // 2) + 16, :],
              arr["x"][b].rearrange("(r j) c -> r j c", j=16)) for b in range(B)]
    loads += [(a.w[:, :, :], arr["a_w"]), (a.bias_ch[:, :], arr["a_bias_ch"]),
              (a.bias_row[:, :, :], arr["a_bias_row"]), (a.blocks[:, :], arr["blocks"])]
    for dst, src in loads:
        nc.sync.dma_start(dst, src).then_inc(loaded, 16)
    return len(loads)


def attn_a_layout(v):
    w = np.stack([v[n].T for n in ("q_w1", "k_w1", "v_w", "g_w", "q_w2", "k_w2", "p_w")], 1)
    rows = np.stack([v[n] for n in ("g_b", "q_b2", "k_b2", "p_b")])
    return {"a_w": np.ascontiguousarray(w), "a_bias_ch": np.stack([v[n] for n in ("q_b1", "k_b1", "v_b")], 1),
            "a_bias_row": np.repeat(rows[None], P, 0)}



HB = 2
C = 32
NC = P // C
LEVELS = 5
HALF = 512
GN_EPS = 1e-5 * HB
MIXES = ("r", "w", "k", "v", "a", "g")


class AttnBMemory:

    def __init__(self, nc, ctx):
        def sb(name, shape):
            return ctx.enter_context(nc.sbuf_tensor(name, shape, F32))

        self.sb = sb
        self.ar = sb("b_ar", [P, 2, B, T * P])
        self.kb = sb("b_kb", [P, 2, B, T * P])
        self.xT = sb("b_xT", [P, B, T * P + 1])
        self.cum = self.xT[:, :, 0:T * P]
        self.v_tok = sb("b_v_tok", [P, B, T, P])
        self.g_tok = sb("b_g_tok", [P, B, T, P])
        self.y_tok = self.cum.rearrange("p b (t c) -> p b t c", c=P)
        self.oW = sb("b_oW", [P, P])
        self.bonus_w = sb("b_bonus_w", [P, HB])

    def stage_one(self, nc, ctx):
        def sb(name, shape):
            return ctx.enter_context(nc.sbuf_tensor(name, shape, F32))

        self.w = sb("b_w", [P, B, T * P])
        self.w128 = sb("b_w128", [P, 7, P])
        self.gA = sb("b_gA", [P, P])
        self.vec = sb("b_vec", [P, 10])
        self.ones = sb("b_ones", [P, P])
        self.xA = sb("b_xA", [P, 192])
        self.xB = sb("b_xB", [P, 2, P])
        self.w64 = sb("b_w64", [P, 3, D])
        self.resets = sb("b_resets", [P, HALF])
        self.tiles = sb("b_tiles", [P, 2, 4, P])
        self.dx = sb("b_dx", [P, 2, HALF])
        self.xm = sb("b_xm", [P, HALF])
        self.mix = sb("b_mix", [P, 2, 2, HALF])
        self.xd = sb("b_xd", [P, 6, HALF])
        self.k_ss = sb("b_k_ss", [P, 4])
        self.k_rn = sb("b_k_rn", [P, 4])
        place = self.kb[:, 0].rearrange("p b (n c) -> p (b n) c", c=HALF)
        self.low = place[:, 0:4, :]
        self.k_raw, self.k_sq, self.gate = place[:, 4, :], place[:, 5, :], place[:, 6, :]
        self.k_diag = place[:, 7, :].rearrange("p (t c) -> p t c", c=P)
        self.t1 = self.xd[:, 0:2]
        self.t2 = self.xd[:, 2:4]
        self.t3 = self.xd[:, 4:6]

    def stage_two(self, nc, ctx, mem):
        def sb(name, shape):
            return ctx.enter_context(nc.sbuf_tensor(name, shape, F32))

        self.masks = sb("b_masks", [P, LEVELS, C // 2])
        self.diag = sb("b_diag", [P, C])
        self.e_in = sb("b_e_in", [P, LEVELS * 3 * D + 2 * P])
        self.e_out = sb("b_e_out", [P, LEVELS * 3 * D + 3 * P])
        self.q_lev = sb("b_q_lev", [P, 2, LEVELS, HB, 2, D])
        self.kb_t = sb("b_kb_t", [P, 2, 2, P])
        self.r_t = sb("b_r_t", [P, 2, HB, P])
        self.acc = sb("b_acc", [P, 2, 8, C])
        self.bd = sb("b_bd", [P, 2, 8, P])
        self.from_start = sb("b_from_start", [P, 4, 2, P])
        self.to_end = sb("b_to_end", [P, 4, 2, P])
        self.decay = sb("b_decay", [P, T, B, NC])
        self.z = sb("b_z", [P, HB, 2, D])
        self.v_t = sb("b_v_t", [P, P])
        self.hat = sb("b_hat", [P, NC, 2, P])
        place = mem.ua[:, :, :, :].rearrange("p b t c -> p (b t c)")
        n, m = 4 * LEVELS * P, 8 * P
        self.k_lev = place[:, 0:n].rearrange("p (r l x s) -> p r l x s", r=2, l=LEVELS, x=2)
        self.pw = place[:, n:n + m].rearrange("p (r e x s) -> p r e x s", r=2, e=HB, x=2)
        self.m_t = place[:, n + m:n + 2 * m].rearrange("p (b c j) -> p b c j", b=B, c=NC)
        self.g_t = sb("b_g_t", [P, 4, P])
        self.yc = sb("b_yc", [P, 4, P + NC * D])
        self.s = sb("b_s", [P, 2, B, D])
        self.sd = sb("b_sd", [P, B, D])

    def stage_three(self, nc, ctx):
        def sb(name, shape):
            return ctx.enter_context(nc.sbuf_tensor(name, shape, F32))

        self.gn = sb("b_gn", [P, 2, P])
        self.rk = sb("b_rk", [P, 2, 4 * P])
        self.y_stats = sb("b_y_stats", [P, 2, 8, 6])
        self.y_mom = sb("b_y_mom", [P, 2, 8, 2])
        self.y_rstd = sb("b_y_rstd", [P, 2, 8])
        self.coef = sb("b_coef", [P, 2, 8])
        self.y1 = sb("b_y1", [P, 2, 4, P])
        self.bon = sb("b_bon", [P, 2, 4, P])
        self.yT = sb("b_yT", [P, 2, 4, P])


B1_SEMS = ("b_copied", "b_xT_done", "b_xT_ready", "b_dx_ready", "b_xm_ready", "b_mix_done", "b_mix_ready", "b_miu_done",
           "b_xd_part", "b_xd_ready", "b_p_done", "b_p_read", "b_z_done", "b_z_ready", "b_ss_done", "b_ss_ready",
           "b_rn_ready", "b_diag_ready", "b_bc_done", "b_k_ready", "b_gated", "b_consts",
           "b_abs", "b_exp", "b_log", "b_min", "b_w_ready", "b_half", "b_kk_ready", "b_cum_ready")
B2_SEMS = ("c_zeroed", "c_ein", "c_raw", "c_exps", "c_r_raw", "c_levels", "c_levels_done", "c_acc_level", "c_acc", "c_bd", "c_to_end",
           "c_turned", "c_n_turned", "c_z0", "c_n_ready", "c_z_done", "c_sq_done", "c_z_ready", "c_p_ready", "c_m_done", "c_y_done",
           "c_m_ready", "c_yc_ready", "c_s_done", "c_yp_half", "c_yp_done", "c_s_ready", "c_sd", "c_sdd", "c_y_ready")
B3_SEMS = ("d_rk", "d_coef_done", "d_coef_ready", "d_stats", "d_mom", "d_eps", "d_rstd", "d_c1", "d_normed", "d_g1", "d_g2",
           "d_bonus", "d_sum", "d_gated", "d_yT_done", "d_yT_ready", "d_o_done", "d_added")


def time_mixing_inputs(nc, mem, a, sem):

    def cols(i):
        b, half = divmod(i, 2)
        return b, half * HALF

    N_ACT = 9

    with nc.Block() as block:

        @block.gpsimd
        def _(pool):
            nc.gpsimd.memset(a.xT[:, :, 0:1], 0.0).then_inc(sem["b_consts"], 1)
            nc.gpsimd.memset(a.ones[:, :], 1.0).then_inc(sem["b_consts"], 1)

            def copy_tiles(i):
                b, c0 = cols(i)
                if i >= 2:
                    pool.wait_ge(sem["b_xT_done"], i - 1)
                nc.gpsimd.tensor_copy(a.tiles[:, i % 2], mem.ua[:, b, c0 // P + 1:c0 // P + 5, :]) \
                    .then_inc(sem["b_copied"], 1)

            def mixed_inputs(i):
                b, c0 = cols(i)
                for g in range(6):
                    pool.wait_ge(sem["b_xd_part"], 6 * i + g + 1)
                    nc.gpsimd.tensor_tensor(a.xd[:, g, :], a.xd[:, g, :], a.xT[:, b, c0 + 1:c0 + 1 + HALF],
                                            ALU.add).then_inc(sem["b_xd_ready"], 1)

            def norms(i):
                pool.wait_ge(sem["b_ss_ready"], i + 1)
                nc.gpsimd.tensor_tensor(a.k_rn[:, :], a.k_ss[:, :], mem.minus_half[:, 0:4],
                                        ALU.pow).then_inc(sem["b_rn_ready"], 1)
                pool.wait_ge(sem["b_rn_ready"], i + 1)
                if i >= 1:
                    pool.wait_ge(sem["b_bc_done"], i)
                nc.gpsimd.tensor_tensor(a.k_diag[:, :, :], mem.ident[:, :].unsqueeze(1).to_broadcast([P, 4, P]),
                                        a.k_rn[:, :].unsqueeze(2).to_broadcast([P, 4, P]),
                                        ALU.mult).then_inc(sem["b_diag_ready"], 1)

            copy_tiles(0)
            for k in range(NG + 1):
                if k + 1 < NG:
                    copy_tiles(k + 1)
                if k >= 1:
                    mixed_inputs(k - 1)
                    norms(k - 1)

        @block.vector
        def _(dve):
            nc.vector.tensor_scalar(a.vec[:, 3:4], a.vec[:, 2:3], -0.5, None, ALU.mult).then_inc(sem["b_consts"], 1)

            def inputs(i):
                for g in range(6):
                    n = 6 * i + g
                    dve.wait_ge(sem["b_miu_done"], n + 1)
                    if i >= 1 and g == 0:
                        dve.wait_ge(sem["b_p_done"], N_ACT * (i - 1) + 6)
                    bank = (mem.bank3[:, :], mem.bank45[:, 0:512])[n % 2]
                    nc.vector.scalar_tensor_tensor(out=a.xd[:, g, :], in0=bank, scalar=a.vec[:, 4 + g:5 + g],
                                                   in1=a.dx[:, i % 2, :], op0=ALU.add,
                                                   op1=ALU.mult).then_inc(sem["b_xd_part"], 1)

            def differences(i):
                b, c0 = cols(i)
                dve.wait_ge(sem["b_xT_ready"], i + 1)
                if i == 0:
                    dve.wait_ge(sem["b_consts"], 3)
                nc.vector.tensor_tensor(a.dx[:, i % 2, :], a.xT[:, b, c0:c0 + HALF], a.xT[:, b, c0 + 1:c0 + 1 + HALF],
                                        ALU.subtract).then_inc(sem["b_dx_ready"], 1)
                dve.wait_ge(sem["b_dx_ready"], i + 1)
                if i >= 1:
                    dve.wait_ge(sem["b_mix_done"], i)
                nc.vector.scalar_tensor_tensor(out=a.xm[:, :], in0=a.dx[:, i % 2, :], scalar=a.vec[:, 0:1],
                                               in1=a.xT[:, b, c0 + 1:c0 + 1 + HALF], op0=ALU.mult,
                                               op1=ALU.add).then_inc(sem["b_xm_ready"], 1)

            def outputs(i):
                b, c0 = cols(i)
                dve.wait_ge(sem["b_z_done"], i + 1)
                nc.vector.tensor_scalar(a.w[:, b, c0:c0 + HALF], mem.bank67[:, 512:1024], a.vec[:, 1:2], None,
                                        ALU.add).then_inc(sem["b_z_ready"], 1)
                dve.wait_ge(sem["b_ss_done"], i + 1)
                nc.vector.tensor_scalar(a.k_ss[:, :], mem.bank67[:, 512:516], 1e-24, None,
                                        ALU.max).then_inc(sem["b_ss_ready"], 1)
                dve.wait_ge(sem["b_bc_done"], i + 1)
                nc.vector.tensor_tensor(a.ar[:, 0, b, c0:c0 + HALF], a.k_raw[:, :], mem.bank67[:, 512:1024],
                                        ALU.mult).then_inc(sem["b_k_ready"], 1)
                dve.wait_ge(sem["b_k_ready"], i + 1)
                dve.wait_ge(sem["b_p_read"], N_ACT * i + 8)
                nc.vector.scalar_tensor_tensor(out=a.kb[:, 1, b, c0:c0 + HALF], in0=a.gate[:, :], scalar=-1.0,
                                               in1=a.ar[:, 0, b, c0:c0 + HALF], op0=ALU.add,
                                               op1=ALU.mult).then_inc(sem["b_gated"], 1)

            for k in range(NG + 1):
                if k >= 1:
                    inputs(k - 1)
                if k < NG:
                    differences(k)
                if k >= 1:
                    outputs(k - 1)

        @block.scalar
        def _(act):
            def bank(n):
                return mem.bank67[:, 0:512] if n % 2 else mem.bank45[:, 512:1024]

            def xT(i):
                b, c0 = cols(i)
                act.wait_ge(sem["b_xT_done"], i + 1)
                nc.scalar.copy(a.xT[:, b, c0 + 1:c0 + 1 + HALF], mem.bank0[:, :]).then_inc(sem["b_xT_ready"], 1)

            def mix(i):
                act.wait_ge(sem["b_mix_done"], i + 1)
                if i >= 2:
                    act.wait_ge(sem["b_miu_done"], 6 * (i - 1))
                nc.scalar.activation(a.mix[:, i % 2, 0, :], mem.bank12[:, 0:512], ACT.Tanh)
                nc.scalar.activation(a.mix[0:D, i % 2, 1, :], mem.bank12[0:D, 512:1024], ACT.Tanh) \
                    .then_inc(sem["b_mix_ready"], 1)

            def first(i):
                b, c0 = cols(i)
                n = N_ACT * i
                act.wait_ge(sem["b_p_done"], n + 1)
                nc.scalar.copy(a.ar[:, 1, b, c0:c0 + HALF], bank(n)).then_inc(sem["b_p_read"], 1)
                for q, func in ((0, ACT.Tanh), (1, ACT.Tanh), (2, ACT.Identity)):
                    act.wait_ge(sem["b_p_done"], n + 2 + q)
                    nc.scalar.activation(a.low[0:D, q, :], bank(n + 1 + q)[0:D], func).then_inc(sem["b_p_read"], 1)
                act.wait_ge(sem["b_p_done"], n + 5)
                nc.scalar.activation(a.low[:, 3, :], bank(n + 4), ACT.Tanh).then_inc(sem["b_p_read"], 1)
                act.wait_ge(sem["b_p_done"], n + 6)
                nc.scalar.copy(a.v_tok[:, b, c0 // P:c0 // P + 4, :], bank(n + 5).rearrange("p (t c) -> p t c", c=P)) \
                    .then_inc(sem["b_p_read"], 1)

            def second(i):
                b, c0 = cols(i)
                n = N_ACT * i + 6
                act.wait_ge(sem["b_p_done"], n + 1)
                if i >= 1:
                    act.wait_ge(sem["b_k_ready"], i)
                nc.scalar.copy(a.k_raw[:, :], bank(n))
                nc.scalar.activation(a.k_sq[:, :], bank(n), ACT.Square).then_inc(sem["b_p_read"], 1)
                act.wait_ge(sem["b_p_done"], n + 2)
                if i == 0:
                    act.wait_ge(sem["b_consts"], 3)
                else:
                    act.wait_ge(sem["b_gated"], i)
                nc.scalar.activation(a.gate[:, :], bank(n + 1), ACT.Tanh, bias=a.vec[:, 3:4], scale=-0.5) \
                    .then_inc(sem["b_p_read"], 1)
                act.wait_ge(sem["b_p_done"], n + 3)
                nc.scalar.copy(a.g_tok[:, b, c0 // P:c0 // P + 4, :], bank(n + 2).rearrange("p (t c) -> p t c", c=P)) \
                    .then_inc(sem["b_p_read"], 1)

            for k in range(NG + 1):
                if k >= 1:
                    first(k - 1)
                if k < NG:
                    xT(k)
                    mix(k)
                if k >= 1:
                    second(k - 1)

        @block.tensor
        def _(pe):
            def bank(n):
                if n >= 2:
                    pe.wait_ge(sem["b_p_read"], n - 1)
                return mem.bank67[:, 0:512] if n % 2 else mem.bank45[:, 512:1024]

            def turn_x(i):
                pe.wait_ge(sem["b_copied"], i + 1)
                if i >= 1:
                    pe.wait_ge(sem["b_xT_ready"], i)
                for n in range(4):
                    last = nc.tensor.transpose(mem.bank0[:, n * P:(n + 1) * P], a.tiles[:, i % 2, n, :], mem.ident[:, :])
                last.then_inc(sem["b_xT_done"], 1)

            def mix(i):
                pe.wait_ge(sem["b_xm_ready"], i + 1)
                if i >= 1:
                    pe.wait_ge(sem["b_mix_ready"], i)
                nc.tensor.matmul(mem.bank12[:, 0:512], a.xA[:, 0:P], a.xm[:, :], start=True, stop=True)
                nc.tensor.matmul(mem.bank12[0:D, 512:1024], a.xA[:, P:192], a.xm[:, :], start=True, stop=True) \
                    .then_inc(sem["b_mix_done"], 1)

            def miu(i):
                pe.wait_ge(sem["b_mix_ready"], i + 1)
                for g in range(6):
                    n = 6 * i + g
                    rows = slice(32 * (g % 4), 32 * (g % 4) + 32)
                    if n >= 2:
                        pe.wait_ge(sem["b_xd_part"], n - 1)
                    nc.tensor.matmul((mem.bank3[:, :], mem.bank45[:, 0:512])[n % 2], a.xB[rows, g // 4, :],
                                     a.mix[rows, i % 2, g // 4, :], start=True, stop=True) \
                        .then_inc(sem["b_miu_done"], 1)

            def first(i):
                n = N_ACT * i
                R, WI, K, V, A, G = range(6)
                pe.wait_ge(sem["b_xd_ready"], 6 * (i + 1))
                nc.tensor.matmul(bank(n), a.w128[:, 0, :], a.xd[:, R, :], start=True, stop=True) \
                    .then_inc(sem["b_p_done"], 1)
                for q, g in ((0, K), (1, WI), (2, A)):
                    nc.tensor.matmul(bank(n + 1 + q)[0:D], a.w64[:, q, :], a.xd[:, g, :], start=True, stop=True) \
                        .then_inc(sem["b_p_done"], 1)
                nc.tensor.matmul(bank(n + 4), a.gA[:, :], a.xd[:, G, :], start=True, stop=True) \
                    .then_inc(sem["b_p_done"], 1)
                out = bank(n + 5)
                for t in range(4):
                    last = nc.tensor.matmul(out[:, t * P:(t + 1) * P], a.xd[:, V, t * P:(t + 1) * P], a.w128[:, 2, :],
                                            start=True, stop=True)
                out = bank(n + 6)
                last.then_inc(sem["b_p_done"], 1)
                nc.tensor.matmul(out, a.w128[:, 1, :], a.xd[:, K, :], start=True, stop=False)

            def second(i):
                n = N_ACT * i + 6
                pe.wait_ge(sem["b_p_read"], N_ACT * i + 5)
                nc.tensor.matmul(mem.bank67[:, 0:512] if n % 2 else mem.bank45[:, 512:1024], a.w128[0:D, 3, :],
                                 a.low[0:D, 0, :], start=False, stop=True).then_inc(sem["b_p_done"], 1)
                nc.tensor.matmul(bank(n + 1), a.w128[0:D, 5, :], a.low[0:D, 2, :], start=True, stop=True) \
                    .then_inc(sem["b_p_done"], 1)
                if i >= 1:
                    pe.wait_ge(sem["b_k_ready"], i)
                nc.tensor.matmul(mem.bank67[:, 512:1024], a.w128[0:D, 4, :], a.low[0:D, 1, :], start=True, stop=True) \
                    .then_inc(sem["b_z_done"], 1)
                out = bank(n + 2)
                for t in range(4):
                    last = nc.tensor.matmul(out[:, t * P:(t + 1) * P], a.low[:, 3, t * P:(t + 1) * P], a.w128[:, 6, :],
                                            start=True, stop=True)
                last.then_inc(sem["b_p_done"], 1)
                pe.wait_ge(sem["b_p_read"], n + 1)
                pe.wait_ge(sem["b_z_ready"], i + 1)
                for t in range(4):
                    last = nc.tensor.matmul(mem.bank67[:, 512 + t:513 + t], a.k_sq[:, t * P:(t + 1) * P], a.ones[:, 0:1],
                                            start=True, stop=True)
                last.then_inc(sem["b_ss_done"], 1)
                pe.wait_ge(sem["b_diag_ready"], i + 1)
                nc.tensor.matmul(mem.bank67[:, 512:1024], a.ones[:, :], a.k_diag[:, :, :].rearrange("p t c -> p (t c)"),
                                 start=True, stop=True).then_inc(sem["b_bc_done"], 1)

            pe.wait_ge(sem["b_consts"], 3)
            for k in range(NG + 1):
                if k >= 1:
                    miu(k - 1)
                    first(k - 1)
                if k < NG:
                    turn_x(k)
                    mix(k)
                if k >= 1:
                    second(k - 1)

    with nc.Block() as block:

        @block.vector
        def _(dve):
            def decay(i):
                b, c0 = cols(i)
                z = a.w[:, b, c0:c0 + HALF]
                dve.wait_ge(sem["b_abs"], i + 1)
                nc.vector.tensor_scalar(z, z, 0.0, -0.5, ALU.min, ALU.add).then_inc(sem["b_min"], 1)
                dve.wait_ge(sem["b_min"], i + 1)
                dve.wait_ge(sem["b_log"], i + 1)
                nc.vector.tensor_tensor(z, z, a.t1[:, i % 2], ALU.subtract).then_inc(sem["b_w_ready"], 1)
                dve.wait_ge(sem["b_w_ready"], i + 1)
                nc.vector.tensor_tensor_scan(a.cum[:, b, c0:c0 + HALF], a.resets[:, :], z, 0.0, ALU.mult,
                                             ALU.add).then_inc(sem["b_cum_ready"], 1)

            def kk(i):
                b, c0 = cols(i)
                dve.wait_ge(sem["b_half"], i + 1)
                nc.vector.tensor_tensor(a.kb[:, 0, b, c0:c0 + HALF], a.ar[:, 0, b, c0:c0 + HALF], a.t3[:, i % 2],
                                        ALU.mult).then_inc(sem["b_kk_ready"], 1)

            for i in range(NG):
                decay(i)
                if i >= 1:
                    kk(i - 1)
            kk(NG - 1)

        @block.scalar
        def _(act):
            for i in range(NG):
                b, c0 = cols(i)
                if i >= 2:
                    act.wait_ge(sem["b_w_ready"], i - 1)
                nc.scalar.activation(a.t1[:, i % 2], a.w[:, b, c0:c0 + HALF], ACT.Abs).then_inc(sem["b_abs"], 1)
                act.wait_ge(sem["b_abs"], i + 1)
                nc.scalar.activation(a.t1[:, i % 2], a.t1[:, i % 2], ACT.Exp, scale=-1.0).then_inc(sem["b_exp"], 1)
                act.wait_ge(sem["b_exp"], i + 1)
                nc.scalar.activation(a.t1[:, i % 2], a.t1[:, i % 2], ACT.Ln, bias=1.0).then_inc(sem["b_log"], 1)
                act.wait_ge(sem["b_w_ready"], i + 1)
                if i >= 2:
                    act.wait_ge(sem["b_kk_ready"], i - 1)
                nc.scalar.activation(a.t3[:, i % 2], a.w[:, b, c0:c0 + HALF], ACT.Exp, scale=0.5) \
                    .then_inc(sem["b_half"], 1)


def recurrence(nc, mem, a, sem):

    def at(i):
        return i + 1

    def later(i, count):
        return not isinstance(i, int) or i >= count

    def step_of(stages):
        def step(k, u, m=None):
            for lag, stage in stages:
                tile = tile_of(k, u, m, lag, B, NT)
                if tile is not None:
                    stage(*tile)
        return step

    LEV, SOLVE, OUT = 1, 2, 3
    ROUNDS = 5

    def chunk_view(ap, level):
        m = 1 << level
        return ap.rearrange("p (n h m) -> p n h m", h=2, m=m)

    def token_slice(t):
        return bass.ds(t * P, P)

    with nc.Block() as block:

        @block.gpsimd
        def _(pool):
            nc.gpsimd.memset(a.k_lev[:, :, :, :, :], 0.0).then_inc(sem["c_zeroed"], 1)
            nc.gpsimd.memset(a.r_t[:, :, :, :], 0.0).then_inc(sem["c_zeroed"], 1)
            nc.gpsimd.memset(a.acc[:, :, :, :], 0.0).then_inc(sem["c_zeroed"], 1)
            nc.gpsimd.memset(a.bd[:, :, :, :], 0.0).then_inc(sem["c_zeroed"], 1)
            nc.gpsimd.memset(a.q_lev[:, :, :, :, :, :], 0.0).then_inc(sem["c_zeroed"], 1)
            nc.gpsimd.memset(a.s[:, :, :, :], 0.0).then_inc(sem["c_zeroed"], 1)
            nc.gpsimd.memset(a.hat[:, :, :, :], 0.0).then_inc(sem["c_zeroed"], 1)
            nc.gpsimd.memset(a.e_in[:, :], 0.0).then_inc(sem["c_zeroed"], 1)
            pool.wait_ge(sem["c_zeroed"], 8)

            def exponents(i, t, b):
                r = b % 2
                cum = a.cum[:, b, token_slice(t)]
                if later(i, 1):
                    pool.wait_ge(sem["c_exps"], at(i) - 1)
                for level in range(LEVELS):
                    m = 1 << level
                    n = D // m
                    left = chunk_view(cum, level)[:, :, 0, :]
                    right = chunk_view(cum, level)[:, :, 1, :]
                    mid = left[:, :, m - 1:m].to_broadcast([P, n, m])
                    out = a.e_in[:, 192 * level:192 * (level + 1)].rearrange("p (q n m) -> p q n m", q=3, m=m)
                    if m > 1:
                        nc.gpsimd.tensor_tensor(out[:, 0, :, 1:m], right[:, :, 0:m - 1],
                                                left[:, :, m - 1:m].to_broadcast([P, n, m - 1]), ALU.subtract)
                    nc.gpsimd.tensor_tensor(out[:, 1], right, mid, ALU.subtract)
                    nc.gpsimd.tensor_tensor(out[:, 2], mid, left, ALU.subtract)
                base = 192 * LEVELS
                chunks = cum.rearrange("p (c s) -> p c s", s=C)
                nc.gpsimd.tensor_tensor(a.e_in[:, base + P:base + 2 * P].rearrange("p (c s) -> p c s", s=C),
                                        chunks[:, :, C - 1:C].to_broadcast([P, NC, C]), chunks, ALU.subtract)
                nc.gpsimd.tensor_copy(a.e_in[:, base:base + P].rearrange("p (c s) -> p c s", s=C)[:, :, 1:C],
                                      chunks[:, :, 0:C - 1]).then_inc(sem["c_ein"], 1)
                if later(i, 2):
                    pool.wait_ge(sem["c_levels_done"], at(i) - 2)
                wait_apart(pool, i)
                nc.gpsimd.tensor_copy(a.kb_t[:, r], a.kb[:, :, b, token_slice(t)]).then_inc(sem["c_raw"], 1)

            def to_end(i, t, b):
                base = 192 * LEVELS
                pool.wait_ge(sem["c_exps"], at(i))
                if later(i, B):
                    pool.wait_ge(sem["c_turned"], at(i) - B)
                pool.wait_ge(sem["c_raw"], at(i))
                nc.gpsimd.tensor_tensor(a.to_end[:, b], a.kb_t[:, b % 2],
                                        a.e_out[:, base + P:base + 2 * P].unsqueeze(1).to_broadcast([P, 2, P]),
                                        ALU.mult)
                nc.gpsimd.tensor_copy(a.decay[:, t, b, :], a.e_out[:, base + 2 * P + C - 1:base + 3 * P:C]) \
                    .then_inc(sem["c_to_end"], 1)

            def state(t, c):
                n = 4 * t + c
                if c:
                    pool.wait_ge(sem["c_s_ready"], n)
                else:
                    pool.wait_ge(sem["c_yc_ready"], 4 * t + 4)
                    pool.wait_ge(sem["c_to_end"], 4 * t + 4)
                    if not isinstance(t, int) or t >= 1:
                        pool.wait_ge(sem["c_s_ready"], n)
                nc.gpsimd.tensor_tensor(a.sd[:, :, :], a.s[:, c % 2], a.decay[:, t, :, c:c + 1].to_broadcast([P, B, D]),
                                        ALU.mult).then_inc(sem["c_sdd"], 1)
                pool.wait_ge(sem["c_sdd"], n + 1)
                nc.gpsimd.tensor_tensor(a.sd[:, :, :], a.sd[:, :, :], a.yc[:, :, P + c * D:P + (c + 1) * D],
                                        ALU.add).then_inc(sem["c_sd"], 1)

            def states(i, t, b):
                if b == B - 1:
                    for c in range(NC):
                        state(t, c)

            run_steps(pool, B, NT, OUT, step_of([(0, exponents), (OUT, states), (0, to_end)]))

        @block.scalar
        def _(act):
            def exps(i, t, b):
                base = 192 * LEVELS
                act.wait_ge(sem["c_ein"], at(i))
                if later(i, 1):
                    act.wait_ge(sem["c_levels"], at(i) - 1)
                    act.wait_ge(sem["c_to_end"], at(i) - 1)
                nc.scalar.activation(a.e_out[:, 0:base], a.e_in[:, 0:base], ACT.Exp)
                nc.scalar.activation(a.e_out[:, base:base + 2 * P], a.e_in[:, base:base + 2 * P], ACT.Exp)
                nc.scalar.activation(a.e_out[:, base + 2 * P:base + 3 * P], a.cum[:, b, token_slice(t)],
                                     ACT.Exp).then_inc(sem["c_exps"], 1)
                if later(i, 2):
                    act.wait_ge(sem["c_levels_done"], at(i) - 2)
                elif i == 0:
                    act.wait_ge(sem["c_zeroed"], 8)
                for e in range(HB):
                    rows = slice(e * D, (e + 1) * D)
                    last = nc.scalar.copy(a.r_t[rows, b % 2, e, :], a.ar[rows, 1, b, token_slice(t)])
                last.then_inc(sem["c_r_raw"], 1)

            def block_diagonal(i, t, b):
                act.wait_ge(sem["c_acc"], at(i))
                if later(i, 2):
                    act.wait_ge(sem["c_y_done"], at(i) - 2)
                for c in range(NC):
                    rows = slice(c * C, (c + 1) * C)
                    last = nc.scalar.copy(a.bd[rows, b % 2, :, c * C:(c + 1) * C], a.acc[rows, b % 2])
                last.then_inc(sem["c_bd"], 1)

            def turned(i, t, b):
                r = b % 2
                act.wait_ge(sem["c_n_turned"], at(i))
                if later(i, 1):
                    act.wait_ge(sem["c_z_done"], ROUNDS * i)
                nc.scalar.copy(a.pw[:, 0, :, 0, :], mem.bank45[:, 512:768].rearrange("p (e s) -> p e s", e=2))
                nc.scalar.copy(a.pw[:, 0, :, 1, :], a.bd[:, r, 4:8:2, :]).then_inc(sem["c_n_ready"], 1)
                act.wait_ge(sem["c_turned"], at(i))
                if later(i, 1):
                    act.wait_ge(sem["c_y_done"], at(i) - 1)
                nc.scalar.copy(a.z[:, :, 0, :], mem.bank0[:, 0:P].rearrange("p (e j) -> p e j", e=2))
                nc.scalar.copy(a.z[:, :, 1, :], mem.bank0[:, 3 * P:4 * P].rearrange("p (e j) -> p e j", e=2))
                nc.scalar.copy(a.v_t[:, :], a.v_tok[:, b, t, :])
                for c in range(NC):
                    rows = slice(c * C, (c + 1) * C)
                    last = nc.scalar.copy(a.hat[rows, c], mem.bank0[rows, P:3 * P].rearrange("p (x j) -> p x j", x=2))
                last.then_inc(sem["c_z0"], 1)
                for n in range(ROUNDS - 1):
                    act.wait_ge(sem["c_sq_done"], (ROUNDS - 1) * i + n + 1)
                    if n:
                        act.wait_ge(sem["c_z_done"], ROUNDS * i + n)
                    nc.scalar.copy(a.pw[:, (n + 1) % 2], mem.bank45[:, 512:1024].rearrange("p (e x s) -> p e x s", e=2, x=2)) \
                        .then_inc(sem["c_p_ready"], 1)

            def y_and_own(i, t, b):
                act.wait_ge(sem["c_y_done"], at(i))
                if later(i, B):
                    act.wait_ge(sem["c_y_ready"], t)
                nc.scalar.copy(a.yc[:, b, :], mem.bank67[:, 512:512 + P + NC * D]).then_inc(sem["c_yc_ready"], 1)

            run_steps(act, B, NT, OUT, step_of([
                (OUT, y_and_own), (0, exps), (SOLVE, turned), (LEV, block_diagonal)]))

        @block.vector
        def _(dve):
            dve.wait_ge(sem["c_zeroed"], 8)

            def levels(i, t, b):
                r = b % 2
                dve.wait_ge(sem["c_exps"], at(i))
                if later(i, 2):
                    dve.wait_ge(sem["c_levels_done"], at(i) - 2)
                for level in range(LEVELS):
                    m = 1 << level
                    e = a.e_out[:, 192 * level:192 * (level + 1)].rearrange("p (q n m) -> p q n m", q=3, m=m)
                    for x in range(2):
                        nc.vector.tensor_tensor(
                            chunk_view(a.k_lev[:, r, level, x, :], level)[:, :, 0, :],
                            chunk_view(a.kb[:, x, b, token_slice(t)], level)[:, :, 0, :], e[:, 2], ALU.mult)
                    for head in range(HB):
                        rows = slice(head * D, (head + 1) * D)
                        for x in range(2):
                            nc.vector.tensor_tensor(
                                a.q_lev[rows, r, level, head, x, :].rearrange("p (n m) -> p n m", m=m),
                                chunk_view(a.ar[rows, x, b, token_slice(t)], level)[:, :, 1, :], e[rows, x], ALU.mult)
                base = 192 * LEVELS
                if later(i, B):
                    dve.wait_ge(sem["c_m_ready"], at(i) - B)
                nc.vector.tensor_tensor(a.from_start[:, b, 0, :], a.ar[:, 0, b, token_slice(t)],
                                        a.e_out[:, base:base + P], ALU.mult)
                nc.vector.tensor_tensor(a.from_start[:, b, 1, :], a.ar[:, 1, b, token_slice(t)],
                                        a.e_out[:, base + 2 * P:base + 3 * P], ALU.mult).then_inc(sem["c_levels"], 1)

            def accumulate(i, t, b):
                r = b % 2
                dve.wait_ge(sem["c_levels_done"], at(i))
                if later(i, 2):
                    dve.wait_ge(sem["c_bd"], at(i) - 2)
                for level in range(LEVELS):
                    if level:
                        dve.wait_ge(sem["c_acc_level"], LEVELS * i + level)
                    wait_apart(dve, i)
                    m = 1 << level
                    n = C // (2 * m)
                    out = a.acc[:, r].rearrange("p q (n h m) -> p q n h m", h=2, m=m)[:, :, :, 1, :]
                    mask = a.masks[:, level, :].rearrange("p (n m) -> p n m", m=m).unsqueeze(1) \
                        .to_broadcast([P, 8, n, m]).bitcast(mybir.dt.int32)
                    data = mem.bank12[:, P * level:P * (level + 1)].rearrange("p (q n m) -> p q n m", q=8, m=m)
                    nc.vector.copy_predicated(out, mask, data).then_inc(sem["c_acc_level"], 1)
                dve.wait_ge(sem["c_acc_level"], LEVELS * at(i))
                wait_apart(dve, i)
                out = a.acc[:, r, 1:8:2, :]
                last = nc.vector.copy_predicated(
                    out, a.diag[:, :].unsqueeze(1).to_broadcast([P, 4, C]).bitcast(mybir.dt.int32),
                    mem.bank12[:, P * LEVELS:P * (LEVELS + 1)].rearrange("p (q s) -> p q s", q=4))
                last.then_inc(sem["c_acc"], 1)

            def solve(i, t, b):
                r = b % 2
                z = a.z[:, :, :, :].rearrange("p e x j -> p (e x j)")
                for n in range(ROUNDS):
                    dve.wait_ge(sem["c_z_done"], ROUNDS * i + n + 1)
                    nc.vector.tensor_tensor(z, z, mem.bank67[:, 0:256], ALU.add).then_inc(sem["c_z_ready"], 1)

            def chunk_parts(i, t, b):
                dve.wait_ge(sem["c_m_done"], at(i))
                if later(i, B):
                    dve.wait_ge(sem["c_y_ready"], t)
                nc.vector.tensor_copy(a.m_t[:, b], mem.bank67[:, 0:256].rearrange("p (c j) -> p c j", c=NC))
                nc.vector.tensor_tensor(a.g_t[:, b, :], mem.bank67[:, 256:384], a.from_start[:, b, 1, :],
                                        ALU.add).then_inc(sem["c_m_ready"], 1)

            def states(i, t, b):
                if b != B - 1:
                    return
                for c in range(NC):
                    n = 4 * t + c
                    dve.wait_ge(sem["c_s_done"], n + 1)
                    dve.wait_ge(sem["c_sd"], n + 1)
                    nc.vector.tensor_tensor(a.s[:, (c + 1) % 2], a.sd[:, :, :],
                                            mem.bank45[:, 0:256].rearrange("p (b j) -> p b j", b=B),
                                            ALU.add).then_inc(sem["c_s_ready"], 1)
                dve.wait_ge(sem["c_yp_done"], t + 1)
                nc.vector.tensor_tensor(a.y_tok[:, :, t, :], a.yc[:, :, 0:P],
                                        mem.bank3[:, :].rearrange("p (b c) -> p b c", b=B),
                                        ALU.add).then_inc(sem["c_y_ready"], 1)

            run_steps(dve, B, NT, OUT, step_of([
                (OUT, chunk_parts), (OUT, states), (0, levels), (SOLVE, solve), (LEV, accumulate)]))

        @block.tensor
        def _(pe):
            pe.wait_ge(sem["c_zeroed"], 8)

            def chunk_parts(i, t, b):
                r = b % 2
                pe.wait_ge(sem["c_z_ready"], ROUNDS * i + ROUNDS)
                if later(i, 1):
                    pe.wait_ge(sem["c_m_ready"], at(i) - 1)
                    pe.wait_ge(sem["c_yc_ready"], at(i) - 1)
                for e in range(HB):
                    heads = slice(e * D, (e + 1) * D)
                    nc.tensor.matmul(mem.bank67[heads, 0:NC * D], a.z[:, e, 0, :], a.hat[:, :, 1, heads],
                                     start=True, stop=True)
                for e in range(HB):
                    last = nc.tensor.matmul(mem.bank67[e * D:(e + 1) * D, 256:384], a.z[:, e, 0, :],
                                            a.bd[:, r, 4 + 2 * e + 1, :], start=True, stop=True)
                last.then_inc(sem["c_m_done"], 1)
                for e in range(HB):
                    heads = slice(e * D, (e + 1) * D)
                    out = mem.bank67[:, 512 + e * D:512 + (e + 1) * D]
                    nc.tensor.matmul(out, a.bd[:, r, 4 + 2 * e + 1, :], a.z[:, e, 1, :], start=True, stop=False)
                    nc.tensor.matmul(out, a.bd[:, r, 2 * e + 1, :], a.v_t[:, heads], start=False, stop=True)
                for c in range(NC):
                    for e in range(HB):
                        heads = slice(e * D, (e + 1) * D)
                        out = mem.bank67[heads, 512 + P + c * D:512 + P + (c + 1) * D]
                        nc.tensor.matmul(out, a.hat[:, c, 1, heads], a.z[:, e, 1, :], start=True, stop=False)
                        last = nc.tensor.matmul(out, a.hat[:, c, 0, heads], a.v_t[:, heads],
                                                start=False, stop=True)
                last.then_inc(sem["c_y_done"], 1)

            def turn(i, t, b):
                r = b % 2
                pe.wait_ge(sem["c_bd"], at(i))
                if later(i, 1):
                    pe.wait_ge(sem["c_p_ready"], (ROUNDS - 1) * i)
                    pe.wait_ge(sem["c_z0"], at(i) - 1)
                for e in range(HB):
                    last = nc.tensor.transpose(mem.bank45[:, 512 + e * P:512 + (e + 1) * P], a.bd[:, r, 4 + 2 * e, :],
                                               mem.ident[:, :])
                last.then_inc(sem["c_n_turned"], 1)
                pe.wait_ge(sem["c_levels"], at(i))
                pe.wait_ge(sem["c_to_end"], at(i))
                nc.tensor.transpose(mem.bank0[:, 0:P], a.from_start[:, b, 0, :], mem.ident[:, :])
                for x in range(2):
                    nc.tensor.transpose(mem.bank0[:, (1 + x) * P:(2 + x) * P], a.to_end[:, b, x, :], mem.ident[:, :])
                for e in range(HB):
                    last = nc.tensor.matmul(mem.bank0[:, 3 * P + e * D:3 * P + (e + 1) * D], a.bd[:, r, 2 * e, :],
                                            a.v_tok[:, b, t, e * D:(e + 1) * D], start=True, stop=True)
                last.then_inc(sem["c_turned"], 1)

            def solve_round(n, i, t, b):
                r = b % 2
                if n == 0:
                    pe.wait_ge(sem["c_n_ready"], at(i))
                    pe.wait_ge(sem["c_z0"], at(i))
                    if later(i, 1):
                        pe.wait_ge(sem["c_m_ready"], at(i) - 1)
                else:
                    pe.wait_ge(sem["c_p_ready"], (ROUNDS - 1) * i + n)
                    pe.wait_ge(sem["c_z_ready"], ROUNDS * i + n)
                for e in range(HB):
                    last = nc.tensor.matmul(mem.bank67[:, e * P:(e + 1) * P], a.pw[:, n % 2, e, 1, :],
                                            a.z[:, e].rearrange("p x j -> p (x j)"), start=True, stop=True)
                last.then_inc(sem["c_z_done"], 1)
                if n < ROUNDS - 1:
                    for e in range(HB):
                        for x in range(2):
                            last = nc.tensor.matmul(mem.bank45[:, 512 + (2 * e + x) * P:512 + (2 * e + x + 1) * P],
                                                    a.pw[:, n % 2, e, 1 - x, :], a.pw[:, n % 2, e, x, :],
                                                    start=True, stop=True)
                    last.then_inc(sem["c_sq_done"], 1)

            def level_chunk(c, i, t, b):
                r = b % 2
                if c == 0:
                    pe.wait_ge(sem["c_levels"], at(i))
                    pe.wait_ge(sem["c_raw"], at(i))
                    pe.wait_ge(sem["c_r_raw"], at(i))
                    if later(i, 1):
                        pe.wait_ge(sem["c_acc"], at(i) - 1)
                rows = slice(c * C, (c + 1) * C)
                for level in range(LEVELS):
                    q = a.q_lev[:, r, level, :, :, c * C // 2:(c + 1) * C // 2].rearrange("p e x m -> p (e x) m")
                    for x in range(2):
                        nc.tensor.matmul(mem.bank12[rows, P * level + D * x:P * level + D * (x + 1)],
                                         a.k_lev[:, r, level, x, rows], q, start=True, stop=True)
                for x in range(2):
                    last = nc.tensor.matmul(mem.bank12[rows, P * LEVELS + D * x:P * LEVELS + D * (x + 1)],
                                            a.kb_t[:, r, x, rows], a.r_t[:, r, :, rows], start=True, stop=True)
                if c == NC - 1:
                    last.then_inc(sem["c_levels_done"], 1)

            def states(i, t, b):
                if b != B - 1:
                    return
                pe.wait_ge(sem["c_m_ready"], 4 * t + 4)
                if not isinstance(t, int) or t >= 1:
                    pe.wait_ge(sem["c_y_ready"], t)
                for c in range(NC):
                    n = 4 * t + c
                    if not (isinstance(t, int) and n == 0):
                        pe.wait_ge(sem["c_s_ready"], n)
                    wait_apart(pe, i)
                    for e in range(HB):
                        heads = slice(e * D, (e + 1) * D)
                        for bb in range(B):
                            last = nc.tensor.matmul(mem.bank45[heads, bb * D:(bb + 1) * D], a.m_t[heads, bb, c, :],
                                                    a.s[heads, c % 2, bb, :], start=True, stop=True)
                    last.then_inc(sem["c_s_done"], 1)
                    for e in range(HB):
                        if e:
                            pe.wait_ge(sem["c_yp_half"], n + 1)
                            wait_apart(pe, i)
                        heads = slice(e * D, (e + 1) * D)
                        for bb in range(B):
                            last = nc.tensor.matmul(mem.bank3[c * C:(c + 1) * C, bb * P + e * D:bb * P + (e + 1) * D],
                                                    a.g_t[heads, bb, c * C:(c + 1) * C], a.s[heads, c % 2, bb, :],
                                                    start=True, stop=True)
                        if not e:
                            last.then_inc(sem["c_yp_half"], 1)
                last.then_inc(sem["c_yp_done"], 1)

            def step(k, u, m=None):
                def tile(lag):
                    return tile_of(k, u, m, lag, B, NT)
                if tile(OUT):
                    chunk_parts(*tile(OUT))
                    states(*tile(OUT))
                if tile(SOLVE):
                    turn(*tile(SOLVE))
                for c in range(NC):
                    if tile(SOLVE):
                        solve_round(c, *tile(SOLVE))
                    if tile(LEV):
                        level_chunk(c, *tile(LEV))
                if tile(SOLVE):
                    solve_round(ROUNDS - 1, *tile(SOLVE))

            run_steps(pe, B, NT, OUT, step)


def time_mixing_outputs(nc, mem, a, sem):

    def cols(i):
        b, half = divmod(i, 2)
        return b, half * HALF

    def heads(ap):
        return ap.rearrange("p t (h j) -> p (t h) j", h=HB)

    def wide(ap):
        return ap.unsqueeze(2).to_broadcast([P, 8, D])

    with nc.Block() as block:

        @block.gpsimd
        def _(pool):
            def products(i):
                b, c0 = cols(i)
                if i >= 2:
                    pool.wait_ge(sem["d_coef_done"], i - 1)
                nc.gpsimd.tensor_tensor(a.rk[:, i % 2, :], a.ar[:, 0, b, c0:c0 + HALF], a.ar[:, 1, b, c0:c0 + HALF],
                                        ALU.mult).then_inc(sem["d_rk"], 1)

            def rstd(i):
                pool.wait_ge(sem["d_mom"], i + 1)
                nc.gpsimd.tensor_scalar(a.y_rstd[:, i % 2, :], a.y_mom[:, i % 2, :, 1], GN_EPS, None,
                                        ALU.add).then_inc(sem["d_eps"], 1)
                pool.wait_ge(sem["d_eps"], i + 1)
                nc.gpsimd.tensor_tensor(a.y_rstd[:, i % 2, :], a.y_rstd[:, i % 2, :], mem.minus_half[:, 0:8],
                                        ALU.pow).then_inc(sem["d_rstd"], 1)

            def bonus(i):
                b, c0 = cols(i)
                t = c0 // P
                pool.wait_ge(sem["d_coef_ready"], i + 1)
                if i >= 2:
                    pool.wait_ge(sem["d_sum"], i - 1)
                nc.gpsimd.tensor_tensor(heads(a.bon[:, i % 2]), heads(a.v_tok[:, b, t:t + 4, :]),
                                        wide(a.coef[:, i % 2, :]), ALU.mult).then_inc(sem["d_bonus"], 1)

            products(0)
            for i in range(NG):
                if i + 1 < NG:
                    products(i + 1)
                rstd(i)
                bonus(i)

        @block.vector
        def _(dve):
            def stats(i):
                b, c0 = cols(i)
                t = c0 // P
                dve.wait_ge(sem["d_coef_done"], i + 1)
                nc.vector.tensor_copy(a.coef[:, i % 2, :], mem.bank0[:, 0:8]).then_inc(sem["d_coef_ready"], 1)
                for n in range(8):
                    last = nc.vector.bn_stats(a.y_stats[:, i % 2, n, :],
                                              a.y_tok[:, b, t + n // 2, (n % 2) * D:(n % 2 + 1) * D])
                last.then_inc(sem["d_stats"], 1)
                dve.wait_ge(sem["d_stats"], i + 1)
                for n in range(8):
                    last = nc.vector.bn_aggr(a.y_mom[:, i % 2, n, :], a.y_stats[:, i % 2, n, :])
                last.then_inc(sem["d_mom"], 1)

            def finish(i):
                b, c0 = cols(i)
                t = c0 // P
                y = a.y1[:, i % 2]
                if i >= 2:
                    dve.wait_ge(sem["d_yT_done"], i - 1)
                nc.vector.tensor_tensor(heads(y), heads(a.y_tok[:, b, t:t + 4, :]), wide(a.y_mom[:, i % 2, :, 0]),
                                        ALU.subtract).then_inc(sem["d_c1"], 1)
                dve.wait_ge(sem["d_c1"], i + 1)
                dve.wait_ge(sem["d_rstd"], i + 1)
                nc.vector.tensor_tensor(heads(y), heads(y), wide(a.y_rstd[:, i % 2, :]), ALU.mult) \
                    .then_inc(sem["d_normed"], 1)
                dve.wait_ge(sem["d_normed"], i + 1)
                nc.vector.tensor_tensor(y, y, a.gn[:, 0].unsqueeze(1).to_broadcast([P, 4, P]), ALU.mult) \
                    .then_inc(sem["d_g1"], 1)
                dve.wait_ge(sem["d_g1"], i + 1)
                nc.vector.tensor_tensor(y, y, a.gn[:, 1].unsqueeze(1).to_broadcast([P, 4, P]), ALU.add) \
                    .then_inc(sem["d_g2"], 1)
                dve.wait_ge(sem["d_g2"], i + 1)
                dve.wait_ge(sem["d_bonus"], i + 1)
                nc.vector.tensor_tensor(y, y, a.bon[:, i % 2], ALU.add).then_inc(sem["d_sum"], 1)
                dve.wait_ge(sem["d_sum"], i + 1)
                nc.vector.tensor_tensor(y, y, a.g_tok[:, b, t:t + 4, :], ALU.mult).then_inc(sem["d_gated"], 1)

            def residual(i):
                b, c0 = cols(i)
                t = c0 // P
                dve.wait_ge(sem["d_o_done"], i + 1)
                nc.vector.tensor_tensor(mem.x[:, b, t:t + 4, :], mem.x[:, b, t:t + 4, :],
                                        mem.bank3[:, :].rearrange("p (t c) -> p t c", t=4), ALU.add) \
                    .then_inc(sem["d_added"], 1)

            stats(0)
            for i in range(NG):
                if i + 1 < NG:
                    stats(i + 1)
                finish(i)
                if i >= 1:
                    residual(i - 1)
            residual(NG - 1)

        @block.scalar
        def _(act):
            for i in range(NG):
                act.wait_ge(sem["d_yT_done"], i + 1)
                if i >= 2:
                    act.wait_ge(sem["d_o_done"], i - 1)
                nc.scalar.copy(a.yT[:, i % 2], mem.bank12[:, 0:512].rearrange("p (t c) -> p t c", t=4)) \
                    .then_inc(sem["d_yT_ready"], 1)

        @block.tensor
        def _(pe):
            def coefs(i):
                pe.wait_ge(sem["d_rk"], i + 1)
                if i >= 1:
                    pe.wait_ge(sem["d_coef_ready"], i)
                for t in range(4):
                    last = nc.tensor.matmul(mem.bank0[:, 2 * t:2 * t + 2], a.rk[:, i % 2, t * P:(t + 1) * P],
                                            a.bonus_w[:, :], start=True, stop=True)
                last.then_inc(sem["d_coef_done"], 1)

            coefs(0)
            for i in range(NG):
                if i + 1 < NG:
                    coefs(i + 1)
                pe.wait_ge(sem["d_gated"], i + 1)
                if i >= 1:
                    pe.wait_ge(sem["d_yT_ready"], i)
                for t in range(4):
                    last = nc.tensor.transpose(mem.bank12[:, t * P:(t + 1) * P], a.y1[:, i % 2, t, :], mem.ident[:, :])
                last.then_inc(sem["d_yT_done"], 1)
                pe.wait_ge(sem["d_yT_ready"], i + 1)
                if i >= 1:
                    pe.wait_ge(sem["d_added"], i)
                for t in range(4):
                    last = nc.tensor.matmul(mem.bank3[:, t * P:(t + 1) * P], a.yT[:, i % 2, t, :], a.oW[:, :],
                                            start=True, stop=True)
                last.then_inc(sem["d_o_done"], 1)


def attn_b_inputs(nc, a, arr, loaded):
    loads = [(a.w128[:, :, :], arr["b_w128"]), (a.oW[:, :], arr["b_oW"]), (a.gA[:, :], arr["b_gA"]), (a.vec[:, :], arr["b_vec"]),
             (a.bonus_w[:, :], arr["b_bonus_w"]), (a.xA[:, :], arr["b_xA"]),
             (a.xB[:, :, :], arr["b_xB"]), (a.w64[:, :, :], arr["b_w64"]), (a.resets[:, :], arr["resets"])]
    for dst, src in loads:
        nc.sync.dma_start(dst, src).then_inc(loaded, 16)
    return len(loads)


def attn_b_layout(v):
    w128 = np.zeros((P, 7, P), np.float32)
    for n, name in enumerate(("rW", "kW", "vW")):
        w128[:, n] = v[name].T
    for n, name in enumerate(("k_B", "w_B", "a_B", "g_B")):
        w128[:v[name].shape[0], 3 + n] = v[name]
    vec = np.zeros((P, 10), np.float32)
    vec[:, 0], vec[:, 1], vec[:, 2] = v["x_miu"].ravel(), v["w_miu"].ravel(), v["a_time"].ravel()
    vec[:, 4:10] = v["lambdas"].reshape(6, P).T
    bonus = np.zeros((P, HB), np.float32)
    xb = np.zeros((P, 2, P), np.float32)
    for h in range(HB):
        bonus[h * D:(h + 1) * D, h] = v["x_time"][h]
    for g in range(6):
        xb[32 * (g % 4):32 * (g % 4) + 32, g // 4] = v["x_B"][g]
    return {"b_w128": w128, "b_oW": np.ascontiguousarray(v["oW"].T), "b_gA": v["g_A"], "b_vec": vec, "b_bonus_w": bonus, "b_xA": v["x_A"], "b_xB": xb,
            "b_w64": np.ascontiguousarray(np.stack([v["k_A"], v["w_A"], v["a_A"]], 1)),
            "b_gn": np.repeat(np.stack([v["gn_gamma"], v["gn_beta"]])[None], P, 0)}


def attn_b_constants():
    s, t = np.arange(P)[:, None] % C, np.arange(C)[None, :]
    masks = np.zeros((P, LEVELS, C // 2), np.float32)
    for level in range(LEVELS):
        m = 1 << level
        right = t[:, (t[0] // m) % 2 == 1]
        masks[:, level] = (s // (2 * m) == right // (2 * m)) & ((s // m) % 2 == 0)
    resets = np.ones((P, HALF), np.float32)
    resets[:, ::C] = 0.0
    return {"b_masks": masks, "b_diag": (s == t).astype(np.float32), "resets": resets}


LN_SEMS = ("l_summed", "l_stats", "l_var", "l_eps", "l_rstd", "l_ready")


def layernorm(nc, mem, sem, run, addend):
    with nc.Block() as block:

        @block.vector
        def _(dve):
            if addend is not None:
                for b in range(B):
                    last = nc.vector.tensor_tensor(mem.x[:, b], mem.x[:, b], addend[:, b, 1:T + 1, :], ALU.add)
                last.then_inc(sem["l_summed"], 1)
            else:
                nc.vector.memset(mem.moments[:, 0, :], 0.0).then_inc(sem["l_summed"], 1)
            dve.wait_ge(sem["l_summed"], run + 1)
            for i in range(NT):
                last = nc.vector.bn_stats(mem.stats[:, i, :], mem.x[:, i // T, i % T, :])
            last.then_inc(sem["l_stats"], 1)
            dve.wait_ge(sem["l_stats"], run + 1)
            for i in range(NT):
                last = nc.vector.bn_aggr(mem.moments[:, i, :], mem.stats[:, i, :])
            last.then_inc(sem["l_var"], 1)
            dve.wait_ge(sem["l_rstd"], run + 1)
            for i in range(NT):
                last = nc.vector.tensor_scalar(mem.ua[:, i // T, i % T + 1, :], mem.x[:, i // T, i % T, :],
                                               mem.moments[:, i, 0:1], mem.rstd[:, i:i + 1],
                                               ALU.subtract, ALU.mult)
            last.then_inc(sem["l_ready"], 1)
            dve.wait_ge(sem["l_ready"], run + 1)

        @block.gpsimd
        def _(pool):
            pool.wait_ge(sem["l_var"], run + 1)
            nc.gpsimd.tensor_scalar(mem.rstd[:, :], mem.moments[:, :, 1], LN_EPS, None,
                                    ALU.add).then_inc(sem["l_eps"], 1)
            pool.wait_ge(sem["l_eps"], run + 1)
            nc.gpsimd.tensor_tensor(mem.rstd[:, :], mem.rstd[:, :], mem.minus_half[:, :],
                                    ALU.pow).then_inc(sem["l_rstd"], 1)


def ffn_inputs(nc, mem, f, a, loaded):
    loads = [
        (f.wqkv[:, :, :], a["wqkv"].rearrange("l c n -> c l n")),
        (f.wo[:, :, :, :], a["wo"].rearrange("l (k p) n -> p (l k) n", p=P)),
        (f.w1[:, :, :], a["w1"].rearrange("l c n -> c l n")),
        (f.w2[:, :, :, :], a["w2"]),
        (f.b1[:, :, :, :], a["b1"]),
        (f.b2[:, :, :], a["b2"]),
        (f.lnp[:, :, :], a["lnp"]),
        (f.rope_raw[:, :, :, :], a["rope"]),
        (f.qk_scales[:, :, :, :], a["qk_scales"]),
        (f.mask[:, :, :], a["mask"]),
        (f.shift[:, :, :], a["shift"]),
    ]
    for dst, src in loads:
        nc.sync.dma_start(dst, src).then_inc(loaded, 16)
    return len(loads)


def shape_constants():
    k = np.arange(P)
    shift = np.zeros((P, 2, P), np.float32)
    shift[k[:-1], 0, k[1:]] = 1.0
    shift[P - 1, 1, 0] = 1.0
    tok = np.arange(P)[:, None]
    keys = np.empty((P, P), np.int64)
    keys[:W] = np.concatenate([np.arange(W), np.arange(-W, 0)])
    keys[W:] = np.arange(P)
    seen = (tok >= keys) & (tok <= keys + W)
    mask = np.zeros((P, T, P), np.float32)
    mask[~np.repeat(seen[:, None, :], T, 1)] = MASKED
    mask[:, 0][keys < 0] = MASKED
    half = np.arange(0, D, 2, dtype=np.float32)
    inv_freq = (np.float32(1.0) / np.float32(10000.0) ** (half / np.float32(D))).astype(np.float32)
    pos = np.arange(T * P, dtype=np.float32)
    freqs = (pos[:, None] * inv_freq[None, :]).astype(np.float32)
    base = ((half + np.float32(0.4 * D)) / np.float32(1.4 * D)).astype(np.float32)
    power = ((pos - T * P // 2) / np.float32(W // 2)).astype(np.float32)
    scale = base[None, :].astype(np.float64) ** power[:, None].astype(np.float64)
    cos, sin = np.cos(freqs.astype(np.float64)), np.sin(freqs.astype(np.float64))
    cos, sin, scale = (np.concatenate([v, v], 1) for v in (cos, sin, scale))
    sin[:, :D // 2] *= -1.0
    rope = np.stack([cos * scale, cos / scale, sin * scale, sin / scale], 1).astype(np.float32)
    rope = np.ascontiguousarray(rope.reshape(T, P, 4, D).transpose(1, 0, 2, 3))
    head = np.arange(P) // DA
    return {"blocks": (head[:, None] == head[None, :]).astype(np.float32),
            "ident": np.eye(P, dtype=np.float32), "shift": shift, "mask": mask, "rope": rope}


def ffn_layout(v):
    b1 = np.zeros((P, DEPTH, 2, 3), np.float32)
    for half in range(2):
        for c, (c0, m) in enumerate(CH):
            b1[:m, :, half, c] = v["b1"][:, half * HID + c0:half * HID + c0 + m].T
    w2 = np.zeros((P, DEPTH, 3, P), np.float32)
    for c, (c0, m) in enumerate(CH):
        w2[:m, :, c] = v["w2"][:, c0:c0 + m].transpose(1, 0, 2)
    qs, ks = v["q_scale"], v["k_scale"]
    swap = np.r_[D // 2:D, 0:D // 2]
    rows = np.stack([qs, ks, qs[:, swap], ks[:, swap]], 1)
    return {"wqkv": v["wqkv"], "wo": v["wo"], "w1": v["w1"], "w2": w2, "b1": b1,
            "b2": np.repeat(v["b2"][None], P, 0),
            "lnp": np.ascontiguousarray(np.stack([v["ln_g"], v["ln_b"]], 2).transpose(1, 0, 2)),
            "qk_scales": np.repeat(rows[None], P, 0)}


@contextmanager
def semaphores(nc, names):
    sem = {name: nc.alloc_semaphore(name) for name in names}
    yield sem
    nc.clear_and_free_semaphores(list(sem.values()))
    nc.all_engine_barrier()


def load_block(nc, loads, loaded, before, memsets=()):
    count = {}
    with nc.Block() as block:

        @block.sync
        def _(sync):
            count["all"] = before + loads()
            sync.wait_ge(loaded, 16 * count["all"])

        if memsets:
            @block.gpsimd
            def _(pool):
                for ap, value in memsets:
                    nc.gpsimd.memset(ap, value)
    return count["all"]


def hybrid_block(nc, arr, out):
    with ExitStack() as ctx:
        mem = Memory(nc, ctx)
        loaded = mem.loaded
        stored = ctx.enter_context(nc.semaphore("stored"))
        lasting = {name: ctx.enter_context(nc.semaphore(name)) for name in LN_SEMS + ATT_SEMS + FF_SEMS}

        def load(pairs):
            for dst, src in pairs:
                nc.sync.dma_start(dst, src).then_inc(loaded, 16)
            return len(pairs)

        with ExitStack() as phase:
            a = AttnAMemory(nc, phase)
            n = load_block(nc, lambda: attn_a_inputs(nc, a, arr, loaded) + load(
                [(mem.x[:, b], arr["x"][b].rearrange("(t p) c -> p t c", p=P)) for b in range(B)]
                + [(mem.ident[:, :], arr["ident"])]), loaded, 0,
                [(mem.minus_half[:, :], -0.5), (mem.ua[:, :, 0, :], 0.0)])
            with semaphores(nc, A_SEMS) as sem:
                linear_attention(nc, mem, a, sem)

        def transformer(n, times):
            with ExitStack() as phase:
                f = FfnMemory(nc, phase, mem, times)
                n = load_block(nc, lambda: ffn_inputs(nc, mem, f, arr, loaded), loaded, n,
                               [(f.ub[:, :, 0, :], 0.0), (mem.ua[:, :, 0, :], 0.0)])
                for layer in range(DEPTH):
                    src, dst = (f.ub, mem.ua) if layer % 2 else (mem.ua, f.ub)
                    run = DEPTH * times + layer
                    attention(nc, mem, f, lasting, src, layer, run)
                    feed_forward(nc, mem, f, lasting, src, dst, layer, run)
            return n

        layernorm(nc, mem, lasting, 0, None)
        n = transformer(n, 0)

        layernorm(nc, mem, lasting, 1, mem.ua)
        with ExitStack() as phase:
            a = AttnBMemory(nc, phase)
            with ExitStack() as stage, semaphores(nc, B1_SEMS) as sem:
                a.stage_one(nc, stage)
                n = load_block(nc, lambda: attn_b_inputs(nc, a, arr, loaded), loaded, n)
                time_mixing_inputs(nc, mem, a, sem)
            with ExitStack() as stage, semaphores(nc, B2_SEMS) as sem:
                a.stage_two(nc, stage, mem)
                n = load_block(nc, lambda: load([(a.masks[:, :, :], arr["b_masks"]), (a.diag[:, :], arr["b_diag"])]),
                               loaded, n)
                recurrence(nc, mem, a, sem)
            with ExitStack() as stage, semaphores(nc, B3_SEMS) as sem:
                a.stage_three(nc, stage)
                n = load_block(nc, lambda: load([(a.gn[:, :, :], arr["b_gn"])]), loaded, n)
                time_mixing_outputs(nc, mem, a, sem)

        layernorm(nc, mem, lasting, 2, None)
        n = transformer(n, 1)

        with nc.Block() as block:

            @block.vector
            def _(dve):
                for b in range(B):
                    nc.vector.tensor_tensor(mem.x[:, b], mem.x[:, b], mem.ua[:, b, 1:T + 1, :],
                                            ALU.add).then_inc(lasting["l_summed"], 1)

            @block.sync
            def _(sync):
                for b in range(B):
                    sync.wait_ge(lasting["l_summed"], 3 + b + 1)
                    nc.sync.dma_start(out[b].rearrange("(t p) c -> p t c", p=P), mem.x[:, b]).then_inc(stored, 16)
                sync.wait_ge(stored, 16 * B)


def kernel(**inputs):
    import concourse.bacc as bacc
    from concourse.bass_utils import run_bass_kernel_spmd

    def part(prefix):
        return {name[len(prefix):]: np.asarray(v) for name, v in inputs.items() if name.startswith(prefix)}

    a, b, f = part("L0_attn_a_"), part("L0_attn_b_"), part("L0_ffn_")
    arrays = {"x": a["x"], **shape_constants(), **attn_b_constants(), **attn_a_layout(a), **attn_b_layout(b),
              **ffn_layout(f)}
    arrays = {name: np.ascontiguousarray(v) for name, v in arrays.items()}
    nc = bacc.Bacc("TRN2", target_bir_lowering=False, num_devices=1)
    arr = {name: nc.dram_tensor(f"in_{name}_dram", v.shape, F32, kind="ExternalInput").ap()
           for name, v in arrays.items()}
    out = nc.dram_tensor("out_0_dram", (B, T * P, P), F32, kind="ExternalOutput").ap()
    hybrid_block(nc, arr, out)
    run = run_bass_kernel_spmd(nc, [{f"in_{name}_dram": v for name, v in arrays.items()}], core_ids=[0])
    return run.results[0]["out_0_dram"]
```

```python
from contextlib import ExitStack, contextmanager

import numpy as np
import concourse.bass as bass
from concourse import mybir

F32 = mybir.dt.float32
ALU = mybir.AluOpType
ACT = mybir.ActivationFunctionType
AX = mybir.AxisListType

P = 128
B = 4
T = 8
NT = B * T
DEPTH = 2
H = 8
D = 64
W = 64
HID = 341
CH = [(0, 128), (128, 128), (256, 85)]
QK_SCALE = 8.0
LN_EPS = 1e-5
MASKED = -1e25


class Memory:

    def __init__(self, nc, ctx):
        def sb(name, shape):
            return ctx.enter_context(nc.sbuf_tensor(name, shape, F32))

        self.x = sb("x_res", [P, B, T, P])
        self.ua = sb("u_a", [P, B, T + 1, P])
        self.ident = sb("ident", [P, P])
        self.minus_half = sb("minus_half", [P, NT])
        self.loaded = ctx.enter_context(nc.semaphore("loaded"))
        self.stats = sb("x_stats", [P, NT, 6])
        self.moments = sb("x_moments", [P, NT, 2])
        self.rstd = sb("x_rstd", [P, NT])
        self.ps = [ctx.enter_context(nc.psum_tensor(f"bank{n}", [P, 512], F32)) for n in (0, 3)]
        self.bank0, self.bank3 = self.ps
        self.bank12 = ctx.enter_context(nc.psum_tensor("bank12", [P, 1024], F32))
        self.bank45 = ctx.enter_context(nc.psum_tensor("bank45", [P, 1024], F32))
        self.bank67 = ctx.enter_context(nc.psum_tensor("bank67", [P, 1024], F32))



class FfnMemory:

    def __init__(self, nc, ctx, mem, times=0):
        def sb(name, shape):
            return ctx.enter_context(nc.sbuf_tensor(f"{name}_{times}", shape, F32))

        self.ub = sb("u_b", [P, B, T + 1, P])
        self.wqkv = sb("wqkv", [P, DEPTH, 3 * H * D])
        self.wo = sb("wo", [P, DEPTH, 4, P])
        self.w1 = sb("w1", [P, DEPTH, 2 * HID])
        self.w2 = sb("w2", [P, DEPTH, 3, P])
        self.b1 = sb("b1", [P, DEPTH, 2, 3])
        self.b2 = sb("b2", [P, DEPTH, P])
        self.lnp = sb("lnp", [P, DEPTH, 2])
        self.rope_raw = sb("rope_raw", [P, T, 4, D])
        self.qk_scales = sb("qk_scales", [P, DEPTH, 4, D])
        self.rope = sb("rope", [P, T, 4, D])
        self.mask = sb("mask", [P, T, P])
        self.shift = sb("shift", [P, 2, P])
        self.minus_half = mem.minus_half
        self.u_tile = sb("u_tile", [P, B, P])
        self.hT = sb("hT", [P, B, P])
        self.last_col = sb("last_col", [P, B, 1])
        self.sq = sb("sq", [P, 2, 1024])
        self.ss = sb("ss", [P, B, 16])
        self.rnorm = sb("rnorm", [P, B, 16])
        self.rot_c = sb("rot_c", [P, 2, 16, D])
        self.rot_s = sb("rot_s", [P, 2, 16, D])
        self.qT = sb("qT", [P, 2, 4, 2, P])
        self.kT = sb("kT", [P, B, 4, 3, W])
        self.v = sb("v", [P, B, H * D])
        self.v0 = sb("v0", [P, B, H * D])
        self.logits = sb("logits", [P, 2, H, P])
        self.neg_max = sb("neg_max", [P, B, 2, H])
        self.q_scale = sb("q_scale_of_head", [P, B, H])
        self.sums = sb("sums", [P, B, 2, H])
        self.probs = sb("probs", [P, B, H, P])
        self.pT = sb("pT", [P, 2, H, P])
        self.oT = sb("oT", [P, 2, 4, P])
        self.stats = sb("h_stats", [P, 2, 2, 6])
        self.moments = sb("h_moments", [P, 2, 2, 2])
        self.rstd = sb("h_rstd", [P, 2, 2])
        place = self.logits[:, :, :, :].rearrange("p r h k -> p (r h k)")
        self.h, self.hn = (place[:, n * 4 * P:(n + 1) * 4 * P].rearrange("p (r m c) -> p r m c", r=2, m=2)
                           for n in range(2))
        self.hnT = place[:, 8 * P:12 * P].rearrange("p (r n) -> p r n", r=2)
        place = self.probs[:, 0:3].rearrange("p b h k -> p (b h k)").rearrange("p (n c q) -> p n c q", n=4, c=3)
        self.gelu, self.hidden = place[:, 0:2], place[:, 2:4]


ATT_SEMS = ("tables_ready", "tile_copied", "uT_done", "carried", "hT_ready", "qk_done", "v_done", "squares_ready",
            "ss_clamped", "ss_ready", "rotated", "rnorm_ready", "rot_summed", "qk_normed", "qT_done", "kT_done", "qT_ready",
            "kT_ready", "v_ready", "keys_kept", "values_kept", "sims_done", "masked", "max_found",
            "max_ready", "exp_ready", "sums_inverted", "probs_ready", "pT_done", "pT_ready", "pv_done",
            "oT_ready", "wo_done", "u_updated")
FF_SEMS = ("f_shifted", "f_hi_ready", "f_lo_ready", "f_stats", "f_var_ready", "f_eps_added",
           "f_rstd_ready", "f_normed", "f_hnT_done", "f_hnT_ready", "f_gate_up_done", "f_up_done", "f_gelu_ready",
           "f_hidden_ready", "f_bias_added", "f_down_done", "f_out_ready")


def run_steps(eng, steps_of_loop, n, last_lag, step, ahead=0):
    first = -(-last_lag // steps_of_loop) * steps_of_loop + steps_of_loop
    last = n - (steps_of_loop if ahead else 0)
    for k in range(first):
        step(k, k % steps_of_loop)
    with eng.Fori(first // steps_of_loop, last // steps_of_loop) as m:
        for u in range(steps_of_loop):
            step(steps_of_loop * m + u, u, m)
    for k in range(last, n + last_lag):
        step(k, k % steps_of_loop)


def wait_apart(eng, i):
    if not isinstance(i, int):
        eng.nop(nofuse=True)


def tile_of(k, u, m, lag, per_turn, n):
    turn, pos = divmod(u - lag, per_turn)
    if m is None:
        i = k - lag
        return (i, i // per_turn, i % per_turn) if 0 <= i < n else None
    return per_turn * (m + turn) + pos, m + turn, pos


def attention(nc, mem, f, sem, u_buf, layer, run):
    base = NT * run

    def at(i):
        return base + i + 1

    LAG_SOFTMAX, LAG_SCALE, LAG_PV = 2, 3, 4

    def step_of(stages):
        def step(k, u, m=None):
            for lag, stage in stages:
                tile = tile_of(k, u, m, lag, B, NT)
                if tile is not None:
                    stage(*tile)
        return step

    def later(i, t, n):
        return not isinstance(i, int) or i >= n

    with nc.Block() as block:

        @block.gpsimd
        def _(pool):
            def scale_probs(i, t, b):
                pool.wait_ge(sem["sums_inverted"], at(i))
                nc.gpsimd.tensor_tensor(f.probs[:, b], f.probs[:, b],
                                        f.sums[:, b, 1, :].unsqueeze(2).to_broadcast([P, H, P]),
                                        ALU.mult).then_inc(sem["probs_ready"], 1)

            def norm_qk(i, t, b):
                pool.wait_ge(sem["ss_ready"], at(i))
                nc.gpsimd.tensor_tensor(f.rnorm[:, b, :], f.ss[:, b, :], f.minus_half[:, 0:16],
                                        ALU.pow).then_inc(sem["rnorm_ready"], 1)
                pool.wait_ge(sem["rotated"], at(i))
                nc.gpsimd.tensor_tensor(f.rot_c[:, b % 2], f.rot_c[:, b % 2], f.rot_s[:, b % 2],
                                        ALU.add).then_inc(sem["rot_summed"], 1)
                pool.wait_ge(sem["rnorm_ready"], at(i))
                pool.wait_ge(sem["rot_summed"], at(i))
                wait_apart(pool, i)
                nc.gpsimd.tensor_scalar(f.q_scale[:, b, :].rearrange("p (e c) -> p e c", e=2),
                                        f.rnorm[:, b, 0:8].rearrange("p (c e) -> p e c", e=2), QK_SCALE, None, ALU.mult)
                nc.gpsimd.tensor_tensor(f.rot_c[:, b % 2, 8:16, :], f.rot_c[:, b % 2, 8:16, :],
                                        f.rnorm[:, b, 8:16].unsqueeze(2).to_broadcast([P, 8, D]),
                                        ALU.mult).then_inc(sem["qk_normed"], 1)

            if layer == 0:
                nc.gpsimd.memset(f.kT[:, :, :, 1, :], 0.0).then_inc(sem["tables_ready"], 1)
                nc.gpsimd.memset(f.v0[:, :, :], 0.0).then_inc(sem["tables_ready"], 1)
                nc.gpsimd.memset(f.qT[:, :, :, :, :], 0.0).then_inc(sem["tables_ready"], 1)
            run_steps(pool, B, NT, LAG_PV, step_of([(LAG_SCALE, scale_probs), (0, norm_qk)]))

        @block.vector
        def _(dve):
            def hT(i, t, b):
                dve.wait_ge(sem["uT_done"], at(i))
                if later(i, t, B):
                    dve.wait_ge(sem["v_done"], at(i) - B)
                nc.vector.tensor_copy(f.hT[W:P, b, 0:1], f.last_col[W:P, b, :]).then_inc(sem["carried"], 1)
                nc.vector.tensor_copy(f.hT[0:W, b, :], mem.bank0[0:W, 0:P])
                nc.vector.tensor_copy(f.hT[W:P, b, 1:P], mem.bank0[W:P, 0:P - 1])
                dve.wait_ge(sem["carried"], at(i))
                nc.vector.tensor_copy(f.last_col[W:P, b, :], mem.bank0[W:P, P - 1:P]).then_inc(sem["hT_ready"], 1)

            def mask_and_max(i, t, b):
                r = b % 2
                dve.wait_ge(sem["sims_done"], at(i))
                if later(i, t, 2):
                    dve.wait_ge(sem["exp_ready"], at(i) - 2)
                nc.vector.tensor_tensor(f.logits[:, r], mem.bank67[:, :].rearrange("p (h k) -> p h k", h=H),
                                        f.mask[:, t, :].unsqueeze(1).to_broadcast([P, H, P]),
                                        ALU.add).then_inc(sem["masked"], 1)
                dve.wait_ge(sem["masked"], at(i))
                nc.vector.tensor_reduce(f.neg_max[:, b, 0, :], f.logits[:, r], AX.X,
                                        ALU.max).then_inc(sem["max_found"], 1)
                dve.wait_ge(sem["max_found"], at(i))
                nc.vector.scalar_tensor_tensor(out=f.neg_max[:, b, 1, :], in0=f.neg_max[:, b, 0, :], scalar=-1.0,
                                               in1=f.q_scale[:, b, :], op0=ALU.mult,
                                               op1=ALU.mult).then_inc(sem["max_ready"], 1)

            def invert_sums(i, t, b):
                dve.wait_ge(sem["exp_ready"], at(i))
                nc.vector.reciprocal(f.sums[:, b, 1, :], f.sums[:, b, 0, :]).then_inc(sem["sums_inverted"], 1)

            def sum_squares(i, t, b):
                r = b % 2
                dve.wait_ge(sem["squares_ready"], at(i))
                nc.vector.tensor_reduce(f.ss[:, b, :], f.sq[:, r, :].rearrange("p (h d) -> p h d", d=D), AX.X,
                                        ALU.add).then_inc(sem["ss_clamped"], 1)
                dve.wait_ge(sem["ss_clamped"], at(i))
                nc.vector.tensor_scalar(f.ss[:, b, :], f.ss[:, b, :], 1e-24, None,
                                        ALU.max).then_inc(sem["ss_ready"], 1)

            def rotate(i, t, b):
                r = b % 2
                if later(i, t, 2):
                    dve.wait_ge(sem["kT_done"], at(i) - 2)
                qk = mem.bank12[:, :].rearrange("p (a h d) -> p a h d", a=2, h=H)
                out_c = f.rot_c[:, r].rearrange("p (a h) d -> p a h d", a=2)
                out_s = f.rot_s[:, r].rearrange("p (a h) d -> p a h d", a=2)

                def table(part, lo):
                    return f.rope[:, t, 2 * part:2 * part + 2, lo:lo + (D if part == 0 else D // 2)] \
                        .unsqueeze(2).to_broadcast([P, 2, H, D if part == 0 else D // 2])

                nc.vector.tensor_tensor(out_c, qk, table(0, 0), ALU.mult)
                nc.vector.tensor_tensor(out_s[:, :, :, 0:32], qk[:, :, :, 32:64], table(1, 0), ALU.mult)
                nc.vector.tensor_tensor(out_s[:, :, :, 32:64], qk[:, :, :, 0:32], table(1, 32),
                                        ALU.mult).then_inc(sem["rotated"], 1)

            def keep_keys(i, t, b):
                if not later(i, t, B):
                    return
                dve.wait_ge(sem["sims_done"], at(i) - B)
                nc.vector.tensor_copy(f.kT[:, b, :, 1, :], f.kT[:, b, :, 2, :]).then_inc(sem["keys_kept"], 1)

            def keep_values(i, t, b):
                if not later(i, t, B):
                    return
                dve.wait_ge(sem["pv_done"], at(i) - B)
                nc.vector.tensor_copy(f.v0[W:P, b, :], f.v[W:P, b, :]).then_inc(sem["values_kept"], 1)

            def update(i, t, b):
                dve.wait_ge(sem["wo_done"], at(i))
                nc.vector.tensor_tensor(u_buf[:, b, t + 1, :], u_buf[:, b, t + 1, :], mem.bank0[:, 0:P],
                                        ALU.add).then_inc(sem["u_updated"], 1)

            def kT(i, t, b):
                dve.wait_ge(sem["kT_done"], at(i))
                if later(i, t, B):
                    dve.wait_ge(sem["keys_kept"], (at(i) - B) - B * run)
                nc.vector.tensor_copy(f.kT[:, b, :, 0:3:2, :],
                                      mem.bank45[:, 512:1024].rearrange("p (c w k) -> p c w k", c=4, w=2)) \
                    .then_inc(sem["kT_ready"], 1)

            nc.vector.tensor_tensor(f.rope[:, :, :, :], f.rope_raw[:, :, :, :],
                                    f.qk_scales[:, layer].unsqueeze(1).to_broadcast([P, T, 4, D]),
                                    ALU.mult).then_inc(sem["tables_ready"], 1)
            nc.vector.memset(f.last_col[:, :, :], 0.0).then_inc(sem["tables_ready"], 1)
            dve.wait_ge(sem["tables_ready"], 7 * (run // 2) + (7 if layer else 5))
            hT(0, 0, 0)
            run_steps(dve, B, NT, LAG_PV, step_of([
                (LAG_SCALE, invert_sums), (LAG_SOFTMAX, mask_and_max), (1, keep_values), (1, keep_keys), (0, sum_squares), (1, kT),
                (0, rotate), (LAG_PV, update), (-1, hT)]), ahead=1)

        @block.scalar
        def _(act):
            def copy_tile(i, t, b):
                if later(i, t, B):
                    act.wait_ge(sem["uT_done"], at(i) - B)
                nc.scalar.copy(f.u_tile[:, b, :], u_buf[:, b, t + 1, :]).then_inc(sem["tile_copied"], 1)

            def pT(i, t, b):
                act.wait_ge(sem["pT_done"], at(i))
                if later(i, t, 2):
                    act.wait_ge(sem["pv_done"], at(i) - 2)
                nc.scalar.copy(f.pT[:, b % 2], mem.bank45[:, :].rearrange("p (h q) -> p h q", h=H)) \
                    .then_inc(sem["pT_ready"], 1)

            def exps(i, t, b):
                act.wait_ge(sem["max_ready"], at(i))
                if later(i, t, B):
                    act.wait_ge(sem["pT_done"], at(i) - B)
                for h in range(H):
                    last = nc.scalar.activation(f.probs[:, b, h, :], f.logits[:, b % 2, h, :], ACT.Exp,
                                                bias=f.neg_max[:, b, 1, h:h + 1], scale=f.q_scale[:, b, h:h + 1],
                                                accum_out=f.sums[:, b, 0, h:h + 1])
                last.then_inc(sem["exp_ready"], 1)

            def oT(i, t, b):
                act.wait_ge(sem["pv_done"], at(i))
                if later(i, t, 2):
                    act.wait_ge(sem["wo_done"], at(i) - 2)
                nc.scalar.copy(f.oT[:, b % 2], mem.bank3[:, :].rearrange("p (c q) -> p c q", c=4)) \
                    .then_inc(sem["oT_ready"], 1)

            def squares(i, t, b):
                act.wait_ge(sem["qk_done"], at(i))
                if later(i, t, 2):
                    act.wait_ge(sem["ss_ready"], at(i) - 2)
                nc.scalar.activation(f.sq[:, b % 2, :], mem.bank12[:, :], ACT.Square) \
                    .then_inc(sem["squares_ready"], 1)

            def qT(i, t, b):
                act.wait_ge(sem["qT_done"], at(i))
                if later(i, t, 2):
                    act.wait_ge(sem["sims_done"], at(i) - 2)
                for e in range(2):
                    rows = slice(e * D, (e + 1) * D)
                    last = nc.scalar.copy(f.qT[rows, b % 2, :, e, :],
                                          mem.bank45[rows, 0:512].rearrange("p (c q) -> p c q", c=4))
                last.then_inc(sem["qT_ready"], 1)

            def values(i, t, b):
                act.wait_ge(sem["v_done"], at(i))
                if later(i, t, B):
                    act.wait_ge(sem["values_kept"], (at(i) - B) - B * run)
                nc.scalar.copy(f.v[:, b, :], mem.bank3[:, :])
                nc.scalar.copy(f.v0[0:W, b, :], mem.bank3[0:W, :]).then_inc(sem["v_ready"], 1)

            copy_tile(0, 0, 0)
            run_steps(act, B, NT, LAG_PV, step_of([
                (LAG_PV, pT), (-1, copy_tile), (0, squares), (LAG_PV, oT), (1, qT), (LAG_SOFTMAX, exps),
                (1, values)]), ahead=1)

        @block.tensor
        def _(pe):
            def transpose_probs(i, t, b):
                pe.wait_ge(sem["probs_ready"], at(i))
                pe.wait_ge(sem["qT_ready"], at(min(i + LAG_PV - 2, NT - 1) if isinstance(i, int) else i + LAG_PV - 2))
                pe.wait_ge(sem["kT_ready"], at(min(i + LAG_PV - 2, NT - 1) if isinstance(i, int) else i + LAG_PV - 2))
                for h in range(H):
                    last = nc.tensor.transpose(mem.bank45[:, h * P:(h + 1) * P], f.probs[:, b, h, :],
                                               mem.ident[:, :])
                last.then_inc(sem["pT_done"], 1)

            def transpose_u(i, t, b):
                pe.wait_ge(sem["tile_copied"], at(i))
                if later(i, t, LAG_PV + 1):
                    pe.wait_ge(sem["u_updated"], at(i) - LAG_PV - 1)
                if later(i, t, 1):
                    pe.wait_ge(sem["hT_ready"], at(i) - 1)
                nc.tensor.transpose(mem.bank0[:, 0:P], f.u_tile[:, b, :], mem.ident[:, :]) \
                    .then_inc(sem["uT_done"], 1)

            def values_by_probs(i, t, b):
                pe.wait_ge(sem["pT_ready"], at(i))
                pe.wait_ge(sem["v_ready"], at(min(i + LAG_PV - 2, NT - 1) if isinstance(i, int) else i + LAG_PV - 2))
                for c in range(4):
                    for e in range(2):
                        cols = slice((2 * c + e) * D, (2 * c + e + 1) * D)
                        for w, v in ((0, f.v0), (1, f.v)):
                            last = nc.tensor.matmul(
                                mem.bank3[e * D:(e + 1) * D, c * P + w * W:c * P + (w + 1) * W],
                                v[:, b, cols], f.pT[:, b % 2, 4 * e + c, w * W:(w + 1) * W],
                                start=True, stop=True)
                last.then_inc(sem["pv_done"], 1)

            def queries_keys(i, t, b):
                pe.wait_ge(sem["hT_ready"], at(i))
                if later(i, t, 1):
                    pe.wait_ge(sem["rotated"], at(i) - 1)
                for a in range(2):
                    last = nc.tensor.matmul(mem.bank12[:, a * 512:(a + 1) * 512], f.hT[:, b, :],
                                            f.wqkv[:, layer, a * 512:(a + 1) * 512], start=True, stop=True)
                last.then_inc(sem["qk_done"], 1)

            def out_proj(i, t, b):
                pe.wait_ge(sem["oT_ready"], at(i))
                pe.wait_ge(sem["hT_ready"], at(min(i + LAG_PV, NT - 1) if isinstance(i, int) else i + LAG_PV))
                if later(i, t, 1):
                    pe.wait_ge(sem["u_updated"], at(i) - 1)
                for c in range(4):
                    last = nc.tensor.matmul(mem.bank0[:, 0:P], f.oT[:, b % 2, c, :], f.wo[:, layer, c, :],
                                            start=(c == 0), stop=(c == 3))
                last.then_inc(sem["wo_done"], 1)

            def transpose_qk(i, t, b):
                pe.wait_ge(sem["qk_normed"], at(i))
                if later(i, t, LAG_PV - 1):
                    pe.wait_ge(sem["pT_ready"], at(i) - (LAG_PV - 1))
                if later(i, t, 1):
                    pe.wait_ge(sem["qT_ready"], at(i) - 1)
                    pe.wait_ge(sem["kT_ready"], at(i) - 1)
                for a, done in ((0, "qT_done"), (1, "kT_done")):
                    for c in range(4):
                        last = nc.tensor.transpose(mem.bank45[:, (4 * a + c) * P:(4 * a + c + 1) * P],
                                                   f.rot_c[:, b % 2, 8 * a + 2 * c:8 * a + 2 * c + 2, :],
                                                   mem.ident[:, :])
                    last.then_inc(sem[done], 1)

            def values(i, t, b):
                if later(i, t, LAG_PV - 1):
                    pe.wait_ge(sem["oT_ready"], at(i) - (LAG_PV - 1))
                if later(i, t, 1):
                    pe.wait_ge(sem["v_ready"], at(i) - 1)
                nc.tensor.matmul(mem.bank3[:, :], f.hT[:, b, :], f.wqkv[:, layer, 1024:1536],
                                 start=True, stop=True).then_inc(sem["v_done"], 1)

            def sims(i, t, b):
                pe.wait_ge(sem["qT_ready"], at(i))
                pe.wait_ge(sem["kT_ready"], at(i))
                if later(i, t, 1):
                    pe.wait_ge(sem["masked"], at(i) - 1)
                for c in range(4):
                    for e in range(2):
                        for w in range(2):
                            keys = f.kT[:, b, c, 0:2, :] if w == 0 else f.kT[:, b, c, 0:3:2, :]
                            last = nc.tensor.matmul(
                                mem.bank67[w * W:(w + 1) * W, e * 512 + c * P:e * 512 + (c + 1) * P],
                                f.qT[:, b % 2, c, e, w * W:(w + 1) * W], keys, start=True, stop=True)
                last.then_inc(sem["sims_done"], 1)

            transpose_u(0, 0, 0)
            run_steps(pe, B, NT, LAG_PV, step_of([
                (LAG_PV, transpose_probs), (0, queries_keys), (LAG_PV, values_by_probs), (1, transpose_qk),
                (1, values), (LAG_PV, out_proj), (1, sims), (-1, transpose_u)]), ahead=1)


def feed_forward(nc, mem, f, sem, src, dst, layer, run):
    n = NT // 2
    base = n * run

    def at(j):
        return base + j + 1

    def later(j, count):
        return not isinstance(j, int) or j >= count

    def step_of(stages):
        def step(k, u, m=None):
            for lag, stage in stages:
                group = tile_of(k, u, m, lag, 2, n)
                if group is not None:
                    stage(*group)
        return step

    LAG = 2

    with nc.Block() as block:

        @block.gpsimd
        def _(pool):
            def low(j, t, r):
                if later(j, 2):
                    pool.wait_ge(sem["f_normed"], at(j) - 2)
                wait_apart(pool, j)
                nc.gpsimd.tensor_copy(f.h[:, r, :, 0:W], src[:, 2 * r:2 * r + 2, t + 1, 0:W]) \
                    .then_inc(sem["f_lo_ready"], 1)

            def rstd(j, t, r):
                pool.wait_ge(sem["f_var_ready"], at(j))
                wait_apart(pool, j)
                nc.gpsimd.tensor_scalar(f.rstd[:, r, :], f.moments[:, r, :, 1], LN_EPS, None,
                                        ALU.add).then_inc(sem["f_eps_added"], 1)
                pool.wait_ge(sem["f_eps_added"], at(j))
                nc.gpsimd.tensor_tensor(f.rstd[:, r, :], f.rstd[:, r, :], f.minus_half[:, 0:2],
                                        ALU.pow).then_inc(sem["f_rstd_ready"], 1)

            def add_bias(j, t, r):
                nc.gpsimd.tensor_tensor(dst[:, 2 * r:2 * r + 2, t + 1, :], src[:, 2 * r:2 * r + 2, t + 1, :],
                                        f.b2[:, layer].unsqueeze(1).to_broadcast([P, 2, P]),
                                        ALU.add).then_inc(sem["f_bias_added"], 1)

            low(0, 0, 0)
            run_steps(pool, 2, n, LAG, step_of([(-1, low), (0, rstd), (1, add_bias)]), ahead=1)

        @block.vector
        def _(dve):
            def stats(j, t, r):
                dve.wait_ge(sem["f_shifted"], at(j))
                if later(j, 2):
                    dve.wait_ge(sem["f_normed"], at(j) - 2)
                nc.vector.tensor_copy(f.h[:, r, :, W:P], mem.bank0[:, 0:P].rearrange("p (a c) -> p a c", a=2)) \
                    .then_inc(sem["f_hi_ready"], 1)
                dve.wait_ge(sem["f_hi_ready"], at(j))
                dve.wait_ge(sem["f_lo_ready"], at(j))
                nc.vector.bn_stats(f.stats[:, r, 0, :], f.h[:, r, 0, :])
                nc.vector.bn_stats(f.stats[:, r, 1, :], f.h[:, r, 1, :]).then_inc(sem["f_stats"], 1)
                dve.wait_ge(sem["f_stats"], at(j))
                wait_apart(dve, j)
                nc.vector.bn_aggr(f.moments[:, r, 0, :], f.stats[:, r, 0, :])
                nc.vector.bn_aggr(f.moments[:, r, 1, :], f.stats[:, r, 1, :]).then_inc(sem["f_var_ready"], 1)

            def normalise(j, t, r):
                dve.wait_ge(sem["f_rstd_ready"], at(j))
                if later(j, 2):
                    dve.wait_ge(sem["f_hnT_done"], at(j) - 2)
                for a in range(2):
                    last = nc.vector.tensor_scalar(f.hn[:, r, a, :], f.h[:, r, a, :], f.moments[:, r, a, 0:1],
                                                   f.rstd[:, r, a:a + 1], ALU.subtract, ALU.mult)
                last.then_inc(sem["f_normed"], 1)

            def gate(j, t, r):
                dve.wait_ge(sem["f_gelu_ready"], at(j))
                dve.wait_ge(sem["f_up_done"], at(j))
                if later(j, 2):
                    dve.wait_ge(sem["f_down_done"], at(j) - 2)
                for c, (_, m) in enumerate(CH):
                    last = nc.vector.scalar_tensor_tensor(
                        out=f.hidden[0:m, r, c, :], in0=mem.bank45[0:m, c * 256:(c + 1) * 256],
                        scalar=f.b1[0:m, layer, 0, c:c + 1], in1=f.gelu[0:m, r, c, :],
                        op0=ALU.add, op1=ALU.mult)
                last.then_inc(sem["f_hidden_ready"], 1)

            def output(j, t, r):
                dve.wait_ge(sem["f_down_done"], at(j))
                dve.wait_ge(sem["f_bias_added"], at(j))
                nc.vector.tensor_tensor(dst[:, 2 * r:2 * r + 2, t + 1, :], dst[:, 2 * r:2 * r + 2, t + 1, :],
                                        mem.bank67[:, 0:256].rearrange("p (a c) -> p a c", a=2),
                                        ALU.add).then_inc(sem["f_out_ready"], 1)

            run_steps(dve, 2, n, LAG, step_of([(LAG, gate), (0, stats), (0, normalise), (LAG, output)]))

        @block.scalar
        def _(act):
            def hnT(j, t, r):
                act.wait_ge(sem["f_hnT_done"], at(j))
                if later(j, 2):
                    act.wait_ge(sem["f_up_done"], at(j) - 2)
                nc.scalar.activation(f.hnT[:, r, :], mem.bank3[:, 0:256], ACT.Identity,
                                     bias=f.lnp[:, layer, 1:2], scale=f.lnp[:, layer, 0:1]) \
                    .then_inc(sem["f_hnT_ready"], 1)

            def gelu(j, t, r):
                act.wait_ge(sem["f_gate_up_done"], at(j))
                if later(j, 2):
                    act.wait_ge(sem["f_hidden_ready"], at(j) - 2)
                for c, (_, m) in enumerate(CH):
                    last = nc.scalar.activation(f.gelu[0:m, r, c, :], mem.bank12[0:m, c * 256:(c + 1) * 256],
                                                ACT.Gelu, bias=f.b1[0:m, layer, 1, c:c + 1])
                last.then_inc(sem["f_gelu_ready"], 1)

            run_steps(act, 2, n, LAG, step_of([(1, gelu), (0, hnT)]))

        @block.tensor
        def _(pe):
            def down(j, t, r):
                pe.wait_ge(sem["f_hidden_ready"], at(j))
                if later(j, 1):
                    pe.wait_ge(sem["f_out_ready"], at(j) - 1)
                for a in range(2):
                    for c, (_, m) in enumerate(CH):
                        last = nc.tensor.matmul(mem.bank67[:, a * P:(a + 1) * P],
                                                f.hidden[0:m, r, c, a * P:(a + 1) * P],
                                                f.w2[0:m, layer, c, :], start=(c == 0), stop=(c == 2))
                last.then_inc(sem["f_down_done"], 1)

            def shift_rows(j, t, r):
                if later(j, 1):
                    pe.wait_ge(sem["f_hi_ready"], at(j) - 1)
                nc.tensor.matmul(mem.bank0[:, 0:P], f.shift[:, 0, :], src[:, 2 * r:2 * r + 2, t + 1, W:P],
                                 start=True, stop=False)
                nc.tensor.matmul(mem.bank0[:, 0:P], f.shift[:, 1, :], src[:, 2 * r:2 * r + 2, t, W:P],
                                 start=False, stop=True).then_inc(sem["f_shifted"], 1)

            def transpose_hn(j, t, r):
                pe.wait_ge(sem["f_normed"], at(j))
                if later(j, 1):
                    pe.wait_ge(sem["f_hnT_ready"], at(j) - 1)
                for a in range(2):
                    last = nc.tensor.transpose(mem.bank3[:, a * P:(a + 1) * P], f.hn[:, r, a, :],
                                               mem.ident[:, :])
                last.then_inc(sem["f_hnT_done"], 1)

            def up(half, bank, rows, done):
                for c, (c0, m) in enumerate(CH):
                    last = nc.tensor.matmul(bank[0:m, c * 256:(c + 1) * 256],
                                            f.w1[:, layer, half * HID + c0:half * HID + c0 + m],
                                            rows, start=True, stop=True)
                last.then_inc(sem[done], 1)

            def up_gate(j, t, r):
                pe.wait_ge(sem["f_hnT_ready"], at(j))
                if later(j, 1):
                    pe.wait_ge(sem["f_gelu_ready"], at(j) - 1)
                up(1, mem.bank12, f.hnT[:, r, :], "f_gate_up_done")

            def up_value(j, t, r):
                if later(j, 1):
                    pe.wait_ge(sem["f_hidden_ready"], at(j) - 1)
                up(0, mem.bank45, f.hnT[:, r, :], "f_up_done")

            run_steps(pe, 2, n, LAG, step_of([
                (0, shift_rows), (1, up_gate), (LAG, down), (1, up_value), (0, transpose_hn)]))



HEADS_A = 16
DA = 8
SCALE_A = DA ** -0.5
GROUP = 4
NG = NT // GROUP
PART = 8


class AttnAMemory:

    def __init__(self, nc, ctx):
        def sb(name, shape):
            return ctx.enter_context(nc.sbuf_tensor(name, shape, F32))

        self.xp = sb("a_x", [P, NT, P])
        self.w = sb("a_weights", [P, 7, P])
        self.bias_ch = sb("a_bias_ch", [P, 3])
        self.bias_row = sb("a_bias_row", [P, 4, P])
        self.blocks = sb("a_blocks", [P, P])
        self.stats = sb("a_stats", [P, NT, 6])
        self.moments = sb("a_moments", [P, NT, 2])
        self.rstd = sb("a_rstd", [P, NT])
        self.xn = sb("a_xn", [P, 2, GROUP, P])
        self.xT = sb("a_xT", [P, 2, GROUP * P])
        self.hq = sb("a_hidden", [P, 2, NG, GROUP * P])
        self.vT = sb("a_vT", [P, NG, GROUP * P])
        self.g_in = sb("a_g_in", [P, 2, GROUP, P])
        self.g = sb("a_g", [P, NG, GROUP, P])
        self.lin = sb("a_lin", [P, NG, 2, GROUP, P])
        self.log = sb("a_log", [P, 4, 2, GROUP, P])
        self.qk = sb("a_qk", [P, 2, 2, GROUP, P])
        self.heads = sb("a_heads", [P, B, P])
        self.z = sb("a_z", [P, B, 3])
        self.mix = sb("a_mix", [P, B, P])
        self.mixT = sb("a_mixT", [P, B, P])
        self.o = self.xp[:, :, :].rearrange("p (a h) (j n) -> p a h j n", a=2, n=DA)
        self.rows = self.lin[:, 0:4].rearrange("p i a n c -> p (i a n c)").rearrange(
            "p (a e h r) -> p a e h r", a=2, e=2, h=HEADS_A)


A_SEMS = ("a_stats_done", "a_var", "a_eps", "a_rstd", "a_normed", "a_xT_done", "a_xT_ready", "a_up_done", "a_hidden_ready",
          "a_g_in_ready", "a_g_ready", "a_lin_done", "a_lin_ready", "a_abs", "a_exp", "a_log_ready", "a_qk_ready",
          "a_heads_done", "a_heads_ready", "a_z_sum", "a_z_den", "a_z_ready", "a_mix_sum", "a_mix_ready", "a_mixT_done",
          "a_mixT_ready", "a_o_done", "a_o_ready", "a_rows_done", "a_rows_ready", "a_y_done", "a_y_added",
          "a_bias_added")


def linear_attention(nc, mem, a, sem):

    def step_of(stages):
        def step(k, u, m=None):
            for lag, stage in stages:
                group = tile_of(k, u, m, lag, 2, NG)
                if group is not None:
                    i, _, r = group
                    stage(i, r)
        return step

    def later(i, count):
        return not isinstance(i, int) or i >= count

    with nc.Block() as block:

        @block.vector
        def _(dve):
            for i in range(NT):
                last = nc.vector.bn_stats(a.stats[:, i, :], a.xp[:, i, :])
            last.then_inc(sem["a_stats_done"], 1)
            dve.wait_ge(sem["a_stats_done"], 1)
            for i in range(NT):
                last = nc.vector.bn_aggr(a.moments[:, i, :], a.stats[:, i, :])
                if i % PART == PART - 1:
                    last.then_inc(sem["a_var"], 1)

            def normalise(i, r):
                dve.wait_ge(sem["a_rstd"], min(i * GROUP // PART, NT // PART - 1) + 1 if isinstance(i, int)
                            else NT // PART)
                if later(i, 2):
                    dve.wait_ge(sem["a_xT_done"], i - 1)
                for n in range(GROUP):
                    tile = GROUP * i + n
                    last = nc.vector.tensor_scalar(a.xn[:, r, n, :], a.xp[:, tile, :], a.moments[:, tile, 0:1],
                                                   a.rstd[:, bass.ds(tile, 1)], ALU.subtract, ALU.mult)
                last.then_inc(sem["a_normed"], 1)

            def xT(i, r):
                dve.wait_ge(sem["a_xT_done"], i + 1)
                if later(i, 2):
                    dve.wait_ge(sem["a_up_done"], i - 1)
                nc.vector.tensor_copy(a.xT[:, r, :], mem.bank0[:, :]).then_inc(sem["a_xT_ready"], 1)

            def g_in(i, r):
                dve.wait_ge(sem["a_up_done"], i + 1)
                if later(i, 2):
                    dve.wait_ge(sem["a_g_ready"], i - 1)
                nc.vector.tensor_tensor(a.g_in[:, r], mem.bank45[:, 0:512].rearrange("p (n c) -> p n c", c=P),
                                        a.bias_row[:, 0].unsqueeze(1).to_broadcast([P, GROUP, P]),
                                        ALU.add).then_inc(sem["a_g_in_ready"], 1)

            normalise(0, 0)
            run_steps(dve, 2, NG, 1, step_of([(0, xT), (-1, normalise), (1, g_in)]), ahead=1)

        @block.gpsimd
        def _(pool):
            for part in range(NT // PART):
                tiles = slice(PART * part, PART * (part + 1))
                pool.wait_ge(sem["a_var"], part + 1)
                nc.gpsimd.tensor_scalar(a.rstd[:, tiles], a.moments[:, tiles, 1], LN_EPS, None,
                                        ALU.add).then_inc(sem["a_eps"], 1)
                pool.wait_ge(sem["a_eps"], part + 1)
                nc.gpsimd.tensor_tensor(a.rstd[:, tiles], a.rstd[:, tiles], mem.minus_half[:, tiles],
                                        ALU.pow).then_inc(sem["a_rstd"], 1)
            nc.gpsimd.tensor_tensor(mem.x[:, :, :, :].rearrange("p b t c -> p (b t) c"),
                                    mem.x[:, :, :, :].rearrange("p b t c -> p (b t) c"),
                                    a.bias_row[:, 3].unsqueeze(1).to_broadcast([P, NT, P]),
                                    ALU.add).then_inc(sem["a_bias_added"], 1)

        @block.scalar
        def _(act):
            def gelus(i, r):
                act.wait_ge(sem["a_up_done"], i + 1)
                nc.scalar.activation(a.hq[:, 0, i, :], mem.bank12[:, 0:512], ACT.Gelu, bias=a.bias_ch[:, 0:1])
                nc.scalar.activation(a.hq[:, 1, i, :], mem.bank12[:, 512:1024], ACT.Gelu, bias=a.bias_ch[:, 1:2])
                nc.scalar.activation(a.vT[:, i, :], mem.bank3[:, :], ACT.Gelu, bias=a.bias_ch[:, 2:3]) \
                    .then_inc(sem["a_hidden_ready"], 1)
                act.wait_ge(sem["a_g_in_ready"], i + 1)
                nc.scalar.activation(a.g[:, i], a.g_in[:, r], ACT.Gelu).then_inc(sem["a_g_ready"], 1)

            run_steps(act, 2, NG, 1, step_of([(1, gelus)]))

        @block.tensor
        def _(pe):
            def transposes(i, r):
                pe.wait_ge(sem["a_normed"], i + 1)
                if later(i, 1):
                    pe.wait_ge(sem["a_xT_ready"], i)
                for n in range(GROUP):
                    last = nc.tensor.transpose(mem.bank0[:, n * P:(n + 1) * P], a.xn[:, r, n, :], mem.ident[:, :])
                last.then_inc(sem["a_xT_done"], 1)

            def products(i, r):
                pe.wait_ge(sem["a_xT_ready"], i + 1)
                if later(i, 1):
                    pe.wait_ge(sem["a_hidden_ready"], i)
                    pe.wait_ge(sem["a_g_in_ready"], i)
                for n, bank in enumerate((mem.bank12[:, 0:512], mem.bank12[:, 512:1024], mem.bank3[:, :])):
                    nc.tensor.matmul(bank, a.w[:, n, :], a.xT[:, r, :], start=True, stop=True)
                for n in range(GROUP):
                    last = nc.tensor.matmul(mem.bank45[:, n * P:(n + 1) * P], a.xT[:, r, n * P:(n + 1) * P],
                                            a.w[:, 3, :], start=True, stop=True)
                last.then_inc(sem["a_up_done"], 1)

            run_steps(pe, 2, NG, 1, step_of([(0, transposes), (1, products)]))

    with nc.Block() as block:

        @block.vector
        def _(dve):
            def linear(i):
                dve.wait_ge(sem["a_lin_done"], i + 1)
                nc.vector.tensor_tensor(a.lin[:, i], (mem.bank12, mem.bank45)[i % 2][:, :].rearrange("p (a n c) -> p a n c", a=2, c=P),
                                        a.bias_row[:, 1:3].unsqueeze(2).to_broadcast([P, 2, GROUP, P]),
                                        ALU.add).then_inc(sem["a_lin_ready"], 1)

            def softplus(i):
                dve.wait_ge(sem["a_log_ready"], i + 1)
                if i >= 2:
                    dve.wait_ge(sem["a_heads_done"], i - 1)
                nc.vector.scalar_tensor_tensor(
                    out=a.qk[:, i % 2].rearrange("p a n c -> p (a n c)"),
                    in0=a.lin[:, i].rearrange("p a n c -> p (a n c)"), scalar=0.0,
                    in1=a.log[:, i % 4].rearrange("p a n c -> p (a n c)"),
                    op0=ALU.max, op1=ALU.add).then_inc(sem["a_qk_ready"], 1)

            def mix(pair):
                dve.wait_ge(sem["a_heads_done"], NG // 2 * (pair + 1))
                for e in range(2):
                    b = 2 * pair + e
                    nc.vector.tensor_tensor(a.heads[:, b, :], mem.bank67[:, e * 512:e * 512 + P], a.blocks[:, :],
                                            ALU.mult).then_inc(sem["a_heads_ready"], 1)
                dve.wait_ge(sem["a_heads_ready"], 2 * (pair + 1))
                bs = slice(2 * pair, 2 * pair + 2)
                nc.vector.tensor_reduce(a.z[:, bs, 0], a.heads[:, bs, :], AX.X, ALU.add).then_inc(sem["a_z_sum"], 1)
                dve.wait_ge(sem["a_z_sum"], pair + 1)
                nc.vector.tensor_scalar(a.z[:, bs, 1], a.z[:, bs, 0], SCALE_A, float(P), ALU.mult,
                                        ALU.add).then_inc(sem["a_z_den"], 1)
                dve.wait_ge(sem["a_z_den"], pair + 1)
                nc.vector.reciprocal(a.z[:, bs, 2], a.z[:, bs, 1]).then_inc(sem["a_z_ready"], 1)
                for b in (2 * pair, 2 * pair + 1):
                    nc.vector.scalar_tensor_tensor(out=a.mix[:, b, :], in0=a.heads[:, b, :], scalar=SCALE_A,
                                                   in1=mem.ident[:, :], op0=ALU.mult,
                                                   op1=ALU.add).then_inc(sem["a_mix_sum"], 1)
                dve.wait_ge(sem["a_z_ready"], pair + 1)
                dve.wait_ge(sem["a_mix_sum"], 2 * (pair + 1))
                for b in (2 * pair, 2 * pair + 1):
                    nc.vector.tensor_scalar(a.mix[:, b, :], a.mix[:, b, :], a.z[:, b, 2:3], None,
                                            ALU.mult).then_inc(sem["a_mix_ready"], 1)
                dve.wait_ge(sem["a_mixT_done"], pair + 1)
                nc.vector.tensor_copy(a.mixT[:, bs, :], mem.bank0[:, 0:256].rearrange("p (b c) -> p b c", b=2)) \
                    .then_inc(sem["a_mixT_ready"], 1)

            def gated(i):
                pair, j = i // 4, GROUP * (i % 4)
                dve.wait_ge(sem["a_o_done"], i + 1)
                nc.vector.tensor_tensor(a.o[:, pair, :, j:j + GROUP, :].rearrange("p h j n -> p j h n"),
                                        mem.bank45[:, i % 2 * 512:(i % 2 + 1) * 512].rearrange("p (j h n) -> p j h n", j=GROUP, n=DA),
                                        a.g[:, i].rearrange("p j (h n) -> p j h n", n=DA),
                                        ALU.mult).then_inc(sem["a_o_ready"], 1)

            def residual(n):
                b, t = n // 2, 4 * (n % 2)
                dve.wait_ge(sem["a_y_done"], n + 1)
                nc.vector.tensor_tensor(mem.x[:, b, t:t + 4, :], mem.x[:, b, t:t + 4, :],
                                        mem.bank67[:, n % 2 * 512:(n % 2 + 1) * 512].rearrange("p (t c) -> p t c", t=4),
                                        ALU.add).then_inc(sem["a_y_added"], 1)

            for i in range(NG + 5):
                if i < NG:
                    linear(i)
                if i >= 5:
                    softplus(i - 5)
                if i - 5 == NG // 2 - 1:
                    mix(0)
            mix(1)
            for i in range(NG):
                gated(i)
            for n in range(NG):
                residual(n)

        @block.scalar
        def _(act):
            for first in (0, 4):
                for i in range(first, first + 4):
                    act.wait_ge(sem["a_lin_ready"], i + 1)
                    if i >= 4:
                        act.wait_ge(sem["a_qk_ready"], i - 3)
                    nc.scalar.activation(a.log[:, i % 4], a.lin[:, i], ACT.Abs).then_inc(sem["a_abs"], 1)
                    act.wait_ge(sem["a_abs"], i + 1)
                    nc.scalar.activation(a.log[:, i % 4], a.log[:, i % 4], ACT.Exp, scale=-1.0) \
                        .then_inc(sem["a_exp"], 1)
                for i in range(first, first + 4):
                    act.wait_ge(sem["a_exp"], i + 1)
                    nc.scalar.activation(a.log[:, i % 4], a.log[:, i % 4], ACT.Ln, bias=1.0) \
                        .then_inc(sem["a_log_ready"], 1)
            for n in range(NG):
                pair, h = n // 4, 4 * (n % 4)
                act.wait_ge(sem["a_rows_done"], n + 1)
                nc.scalar.copy(a.rows[:, pair, :, h:h + 4, :].rearrange("p e h r -> p h e r"),
                               mem.bank12[:, n % 2 * 512:(n % 2 + 1) * 512].rearrange("p (h e r) -> p h e r", h=4, e=2)) \
                    .then_inc(sem["a_rows_ready"], 1)

        @block.tensor
        def _(pe):
            def second(i):
                if i >= 2:
                    pe.wait_ge(sem["a_lin_ready"], i - 1)
                for q in range(2):
                    for n in range(GROUP):
                        last = nc.tensor.matmul((mem.bank12, mem.bank45)[i % 2][:, q * 512 + n * P:q * 512 + (n + 1) * P],
                                                a.hq[:, q, i, n * P:(n + 1) * P], a.w[:, 4 + q, :],
                                                start=True, stop=True)
                last.then_inc(sem["a_lin_done"], 1)

            def heads(i):
                pe.wait_ge(sem["a_qk_ready"], i + 1)
                if i == NG // 2:
                    pe.wait_ge(sem["a_heads_ready"], 2)
                for n in range(GROUP):
                    for e in range(2):
                        rows = slice(e * W, (e + 1) * W)
                        last = nc.tensor.matmul(mem.bank67[:, e * 512:e * 512 + P], a.qk[rows, i % 2, 0, n, :],
                                                a.qk[rows, i % 2, 1, n, :], start=(i % 4 == 0 and n == 0),
                                                stop=(i % 4 == 3 and n == GROUP - 1))
                last.then_inc(sem["a_heads_done"], 1)

            def turn_mix(pair):
                pe.wait_ge(sem["a_mix_ready"], 2 * (pair + 1))
                if pair:
                    pe.wait_ge(sem["a_mixT_ready"], pair)
                for e in range(2):
                    last = nc.tensor.transpose(mem.bank0[:, e * P:(e + 1) * P], a.mix[:, 2 * pair + e, :], mem.ident[:, :])
                last.then_inc(sem["a_mixT_done"], 1)

            def outputs(i):
                pair = i // 4
                pe.wait_ge(sem["a_mixT_ready"], pair + 1)
                if i >= 2:
                    pe.wait_ge(sem["a_o_ready"], i - 1)
                for n in range(GROUP):
                    for e in range(2):
                        last = nc.tensor.matmul(mem.bank45[e * W:(e + 1) * W, i % 2 * 512 + n * P:i % 2 * 512 + (n + 1) * P],
                                                a.vT[:, i, n * P + e * W:n * P + (e + 1) * W], a.mixT[:, 2 * pair + e, :],
                                                start=True, stop=True)
                last.then_inc(sem["a_o_done"], 1)

            def turn_rows(n):
                pair, h = n // 4, 4 * (n % 4)
                pe.wait_ge(sem["a_o_ready"], 4 * (pair + 1))
                if n >= 2:
                    pe.wait_ge(sem["a_rows_ready"], n - 1)
                for q in range(4):
                    last = nc.tensor.transpose(mem.bank12[:, n % 2 * 512 + q * P:n % 2 * 512 + (q + 1) * P],
                                               a.o[:, pair, h + q, :, :], mem.ident[:, :])
                last.then_inc(sem["a_rows_done"], 1)

            def project(n):
                b, t = n // 2, 4 * (n % 2)
                pe.wait_ge(sem["a_rows_ready"], 4 * (b // 2 + 1))
                if n >= 2:
                    pe.wait_ge(sem["a_y_added"], n - 1)
                for q in range(4):
                    last = nc.tensor.matmul(mem.bank67[:, n % 2 * 512 + q * P:n % 2 * 512 + (q + 1) * P],
                                            a.rows[:, b // 2, b % 2, 2 * (t + q):2 * (t + q) + 2, :],
                                            a.w[:, 6, :], start=True, stop=True)
                last.then_inc(sem["a_y_done"], 1)

            for i in range(NG + 5):
                if i < NG:
                    second(i)
                if i >= 5:
                    heads(i - 5)
                if i - 5 == NG // 2 - 1:
                    turn_mix(0)
            turn_mix(1)
            for i in range(NG):
                outputs(i)
            for n in range(NG):
                turn_rows(n)
            for n in range(NG):
                project(n)


def attn_a_inputs(nc, a, arr, loaded):
    loads = [(a.xp[64 * (b % 2):64 * (b % 2) + 64, 16 * (b // 2):16 * (b // 2) + 16, :],
              arr["x"][b].rearrange("(r j) c -> r j c", j=16)) for b in range(B)]
    loads += [(a.w[:, :, :], arr["a_w"]), (a.bias_ch[:, :], arr["a_bias_ch"]),
              (a.bias_row[:, :, :], arr["a_bias_row"]), (a.blocks[:, :], arr["blocks"])]
    for dst, src in loads:
        nc.sync.dma_start(dst, src).then_inc(loaded, 16)
    return len(loads)


def attn_a_layout(v):
    w = np.stack([v[n].T for n in ("q_w1", "k_w1", "v_w", "g_w", "q_w2", "k_w2", "p_w")], 1)
    rows = np.stack([v[n] for n in ("g_b", "q_b2", "k_b2", "p_b")])
    return {"a_w": np.ascontiguousarray(w), "a_bias_ch": np.stack([v[n] for n in ("q_b1", "k_b1", "v_b")], 1),
            "a_bias_row": np.repeat(rows[None], P, 0)}



HB = 2
C = 32
NC = P // C
LEVELS = 5
HALF = 512
GN_EPS = 1e-5 * HB
MIXES = ("r", "w", "k", "v", "a", "g")


class AttnBMemory:

    def __init__(self, nc, ctx):
        def sb(name, shape):
            return ctx.enter_context(nc.sbuf_tensor(name, shape, F32))

        self.sb = sb
        self.ar = sb("b_ar", [P, 2, B, T * P])
        self.kb = sb("b_kb", [P, 2, B, T * P])
        self.xT = sb("b_xT", [P, B, T * P + 1])
        self.cum = self.xT[:, :, 0:T * P]
        self.v_tok = sb("b_v_tok", [P, B, T, P])
        self.g_tok = sb("b_g_tok", [P, B, T, P])
        self.y_tok = self.cum.rearrange("p b (t c) -> p b t c", c=P)
        self.oW = sb("b_oW", [P, P])
        self.bonus_w = sb("b_bonus_w", [P, HB])

    def stage_one(self, nc, ctx):
        def sb(name, shape):
            return ctx.enter_context(nc.sbuf_tensor(name, shape, F32))

        self.w = sb("b_w", [P, B, T * P])
        self.w128 = sb("b_w128", [P, 7, P])
        self.gA = sb("b_gA", [P, P])
        self.vec = sb("b_vec", [P, 10])
        self.ones = sb("b_ones", [P, P])
        self.xA = sb("b_xA", [P, 192])
        self.xB = sb("b_xB", [P, 2, P])
        self.w64 = sb("b_w64", [P, 3, D])
        self.resets = sb("b_resets", [P, HALF])
        self.tiles = sb("b_tiles", [P, 2, 4, P])
        self.dx = sb("b_dx", [P, 2, HALF])
        self.xm = sb("b_xm", [P, HALF])
        self.mix = sb("b_mix", [P, 2, 2, HALF])
        self.xd = sb("b_xd", [P, 6, HALF])
        self.k_ss = sb("b_k_ss", [P, 4])
        self.k_rn = sb("b_k_rn", [P, 4])
        place = self.kb[:, 0].rearrange("p b (n c) -> p (b n) c", c=HALF)
        self.low = place[:, 0:4, :]
        self.k_raw, self.k_sq, self.gate = place[:, 4, :], place[:, 5, :], place[:, 6, :]
        self.k_diag = place[:, 7, :].rearrange("p (t c) -> p t c", c=P)
        self.log = place
        self.half = self.xd[:, 0:2]

    def stage_two(self, nc, ctx, mem):
        def sb(name, shape):
            return ctx.enter_context(nc.sbuf_tensor(name, shape, F32))

        self.masks = sb("b_masks", [P, LEVELS, C // 2])
        self.diag = sb("b_diag", [P, C])
        self.e_in = sb("b_e_in", [P, LEVELS * 3 * D + 2 * P])
        self.e_out = sb("b_e_out", [P, LEVELS * 3 * D + 3 * P])
        self.q_lev = sb("b_q_lev", [P, 2, LEVELS, HB, 2, D])
        self.kb_t = sb("b_kb_t", [P, 2, 2, P])
        self.r_t = sb("b_r_t", [P, 2, HB, P])
        self.acc = sb("b_acc", [P, 2, 8, C])
        self.bd = sb("b_bd", [P, 2, 8, P])
        self.from_start = sb("b_from_start", [P, 4, 2, P])
        self.to_end = sb("b_to_end", [P, 4, 2, P])
        self.decay = sb("b_decay", [P, B, NC])
        self.z = sb("b_z", [P, HB, 2, D])
        self.v_t = sb("b_v_t", [P, P])
        self.hat = sb("b_hat", [P, NC, 2, P])
        place = mem.ua[:, :, :, :].rearrange("p b t c -> p (b t c)")
        n, m = 4 * LEVELS * P, 8 * P
        self.k_lev = place[:, 0:n].rearrange("p (r l x s) -> p r l x s", r=2, l=LEVELS, x=2)
        self.pw = place[:, n:n + m].rearrange("p (r e x s) -> p r e x s", r=2, e=HB, x=2)
        self.m_t = place[:, n + m:n + 2 * m].rearrange("p (b c j) -> p b c j", b=B, c=NC)
        self.g_t = sb("b_g_t", [P, 4, P])
        self.yc = sb("b_yc", [P, 4, P + NC * D])
        self.s = sb("b_s", [P, 2, B, D])
        self.eye = sb("b_eye", [P, D])
        self.decay_diag = sb("b_decay_diag", [P, NC, D])

    def stage_three(self, nc, ctx):
        def sb(name, shape):
            return ctx.enter_context(nc.sbuf_tensor(name, shape, F32))

        self.gn = sb("b_gn", [P, 2, P])
        self.rk = sb("b_rk", [P, 2, 4 * P])
        self.y_stats = sb("b_y_stats", [P, 2, 8, 6])
        self.y_mom = sb("b_y_mom", [P, 2, 8, 2])
        self.y_rstd = sb("b_y_rstd", [P, 2, 8])
        self.coef = sb("b_coef", [P, 2, 8])
        self.y1 = sb("b_y1", [P, 2, 4, P])
        self.bon = sb("b_bon", [P, 2, 4, P])
        self.yT = sb("b_yT", [P, 2, 4, P])


B1_SEMS = ("b_copied", "b_xT_done", "b_xT_ready", "b_dx_ready", "b_xm_ready", "b_mix_done", "b_mix_ready", "b_miu_done",
           "b_xd_part", "b_xd_ready", "b_p_done", "b_p_read", "b_z_done", "b_z_ready", "b_ss_done", "b_ss_ready",
           "b_rn_ready", "b_diag_ready", "b_bc_done", "b_k_ready", "b_gated", "b_consts",
           "b_abs", "b_exp", "b_log", "b_min", "b_w_ready", "b_half", "b_kk_ready", "b_cum_ready")
B2_SEMS = ("c_zeroed", "c_ein", "c_raw", "c_exps", "c_r_raw", "c_levels", "c_levels_done", "c_acc_level", "c_acc", "c_bd", "c_to_end",
           "c_turned", "c_n_turned", "c_z0", "c_hat", "c_diag", "c_eye", "c_n_ready", "c_z_done", "c_sq_done", "c_z_ready", "c_p_ready", "c_m_done", "c_y_done",
           "c_m_ready", "c_yc_ready", "c_s_done", "c_yp_half", "c_yp_done", "c_s_ready", "c_y_ready")
B3_SEMS = ("d_rk", "d_coef_done", "d_coef_ready", "d_stats", "d_mom", "d_eps", "d_rstd", "d_c1", "d_normed", "d_g1", "d_g2",
           "d_bonus", "d_sum", "d_gated", "d_yT_done", "d_yT_ready", "d_o_done", "d_added")


def time_mixing_inputs(nc, mem, a, sem):

    def cols(i):
        b, half = divmod(i, 2)
        return b, half * HALF

    N_ACT = 9

    with nc.Block() as block:

        @block.gpsimd
        def _(pool):
            nc.gpsimd.memset(a.xT[:, :, 0:1], 0.0).then_inc(sem["b_consts"], 1)
            nc.gpsimd.memset(a.ones[:, :], 1.0).then_inc(sem["b_consts"], 1)

            def copy_tiles(i):
                b, c0 = cols(i)
                if i >= 2:
                    pool.wait_ge(sem["b_xT_done"], i - 1)
                nc.gpsimd.tensor_copy(a.tiles[:, i % 2], mem.ua[:, b, c0 // P + 1:c0 // P + 5, :]) \
                    .then_inc(sem["b_copied"], 1)

            def mixed_inputs(i):
                b, c0 = cols(i)
                for g in range(6):
                    pool.wait_ge(sem["b_xd_part"], 6 * i + g + 1)
                    nc.gpsimd.tensor_tensor(a.xd[:, g, :], a.xd[:, g, :], a.xT[:, b, c0 + 1:c0 + 1 + HALF],
                                            ALU.add).then_inc(sem["b_xd_ready"], 1)

            def norms(i):
                pool.wait_ge(sem["b_ss_ready"], i + 1)
                nc.gpsimd.tensor_tensor(a.k_rn[:, :], a.k_ss[:, :], mem.minus_half[:, 0:4],
                                        ALU.pow).then_inc(sem["b_rn_ready"], 1)
                pool.wait_ge(sem["b_rn_ready"], i + 1)
                if i >= 1:
                    pool.wait_ge(sem["b_bc_done"], i)
                nc.gpsimd.tensor_tensor(a.k_diag[:, :, :], mem.ident[:, :].unsqueeze(1).to_broadcast([P, 4, P]),
                                        a.k_rn[:, :].unsqueeze(2).to_broadcast([P, 4, P]),
                                        ALU.mult).then_inc(sem["b_diag_ready"], 1)

            copy_tiles(0)
            for k in range(NG + 1):
                if k + 1 < NG:
                    copy_tiles(k + 1)
                if k >= 1:
                    mixed_inputs(k - 1)
                    norms(k - 1)

        @block.vector
        def _(dve):
            nc.vector.tensor_scalar(a.vec[:, 3:4], a.vec[:, 2:3], -0.5, None, ALU.mult).then_inc(sem["b_consts"], 1)

            def inputs(i):
                for g in range(6):
                    n = 6 * i + g
                    dve.wait_ge(sem["b_miu_done"], n + 1)
                    if i >= 1 and g == 0:
                        dve.wait_ge(sem["b_p_done"], N_ACT * (i - 1) + 6)
                    bank = (mem.bank3[:, :], mem.bank45[:, 0:512])[n % 2]
                    nc.vector.scalar_tensor_tensor(out=a.xd[:, g, :], in0=bank, scalar=a.vec[:, 4 + g:5 + g],
                                                   in1=a.dx[:, i % 2, :], op0=ALU.add,
                                                   op1=ALU.mult).then_inc(sem["b_xd_part"], 1)

            def differences(i):
                b, c0 = cols(i)
                dve.wait_ge(sem["b_xT_ready"], i + 1)
                if i == 0:
                    dve.wait_ge(sem["b_consts"], 3)
                nc.vector.tensor_tensor(a.dx[:, i % 2, :], a.xT[:, b, c0:c0 + HALF], a.xT[:, b, c0 + 1:c0 + 1 + HALF],
                                        ALU.subtract).then_inc(sem["b_dx_ready"], 1)
                dve.wait_ge(sem["b_dx_ready"], i + 1)
                if i >= 1:
                    dve.wait_ge(sem["b_mix_done"], i)
                nc.vector.scalar_tensor_tensor(out=a.xm[:, :], in0=a.dx[:, i % 2, :], scalar=a.vec[:, 0:1],
                                               in1=a.xT[:, b, c0 + 1:c0 + 1 + HALF], op0=ALU.mult,
                                               op1=ALU.add).then_inc(sem["b_xm_ready"], 1)

            def outputs(i):
                b, c0 = cols(i)
                dve.wait_ge(sem["b_z_done"], i + 1)
                nc.vector.tensor_scalar(a.w[:, b, c0:c0 + HALF], mem.bank67[:, 512:1024], a.vec[:, 1:2], None,
                                        ALU.add).then_inc(sem["b_z_ready"], 1)
                dve.wait_ge(sem["b_ss_done"], i + 1)
                nc.vector.tensor_scalar(a.k_ss[:, :], mem.bank67[:, 512:516], 1e-24, None,
                                        ALU.max).then_inc(sem["b_ss_ready"], 1)

            def normalised(i):
                b, c0 = cols(i)
                dve.wait_ge(sem["b_bc_done"], i + 1)
                nc.vector.tensor_tensor(a.ar[:, 0, b, c0:c0 + HALF], a.k_raw[:, :], mem.bank67[:, 512:1024],
                                        ALU.mult).then_inc(sem["b_k_ready"], 1)
                dve.wait_ge(sem["b_k_ready"], i + 1)
                dve.wait_ge(sem["b_p_read"], N_ACT * i + 8)
                nc.vector.scalar_tensor_tensor(out=a.kb[:, 1, b, c0:c0 + HALF], in0=a.gate[:, :], scalar=-1.0,
                                               in1=a.ar[:, 0, b, c0:c0 + HALF], op0=ALU.add,
                                               op1=ALU.mult).then_inc(sem["b_gated"], 1)

            for k in range(NG + 2):
                if k >= 2:
                    normalised(k - 2)
                if 1 <= k <= NG:
                    inputs(k - 1)
                if k < NG:
                    differences(k)
                if 1 <= k <= NG:
                    outputs(k - 1)

        @block.scalar
        def _(act):
            def bank(n):
                return mem.bank67[:, 0:512] if n % 2 else mem.bank45[:, 512:1024]

            def xT(i):
                b, c0 = cols(i)
                act.wait_ge(sem["b_xT_done"], i + 1)
                nc.scalar.copy(a.xT[:, b, c0 + 1:c0 + 1 + HALF], mem.bank0[:, :]).then_inc(sem["b_xT_ready"], 1)

            def mix(i):
                act.wait_ge(sem["b_mix_done"], i + 1)
                if i >= 2:
                    act.wait_ge(sem["b_miu_done"], 6 * (i - 1))
                nc.scalar.activation(a.mix[:, i % 2, 0, :], mem.bank12[:, 0:512], ACT.Tanh)
                nc.scalar.activation(a.mix[0:D, i % 2, 1, :], mem.bank12[0:D, 512:1024], ACT.Tanh) \
                    .then_inc(sem["b_mix_ready"], 1)

            def first(i):
                b, c0 = cols(i)
                n = N_ACT * i
                act.wait_ge(sem["b_p_done"], n + 1)
                nc.scalar.copy(a.ar[:, 1, b, c0:c0 + HALF], bank(n)).then_inc(sem["b_p_read"], 1)
                for q, func in ((0, ACT.Tanh), (1, ACT.Tanh), (2, ACT.Identity)):
                    act.wait_ge(sem["b_p_done"], n + 2 + q)
                    nc.scalar.activation(a.low[0:D, q, :], bank(n + 1 + q)[0:D], func).then_inc(sem["b_p_read"], 1)
                act.wait_ge(sem["b_p_done"], n + 5)
                nc.scalar.activation(a.low[:, 3, :], bank(n + 4), ACT.Tanh).then_inc(sem["b_p_read"], 1)
                act.wait_ge(sem["b_p_done"], n + 6)
                nc.scalar.copy(a.v_tok[:, b, c0 // P:c0 // P + 4, :], bank(n + 5).rearrange("p (t c) -> p t c", c=P)) \
                    .then_inc(sem["b_p_read"], 1)

            def second(i):
                b, c0 = cols(i)
                n = N_ACT * i + 6
                act.wait_ge(sem["b_p_done"], n + 1)
                if i >= 1:
                    act.wait_ge(sem["b_k_ready"], i)
                nc.scalar.copy(a.k_raw[:, :], bank(n))
                nc.scalar.activation(a.k_sq[:, :], bank(n), ACT.Square).then_inc(sem["b_p_read"], 1)
                act.wait_ge(sem["b_p_done"], n + 2)
                if i == 0:
                    act.wait_ge(sem["b_consts"], 3)
                else:
                    act.wait_ge(sem["b_gated"], i)
                nc.scalar.activation(a.gate[:, :], bank(n + 1), ACT.Tanh, bias=a.vec[:, 3:4], scale=-0.5) \
                    .then_inc(sem["b_p_read"], 1)
                act.wait_ge(sem["b_p_done"], n + 3)
                nc.scalar.copy(a.g_tok[:, b, c0 // P:c0 // P + 4, :], bank(n + 2).rearrange("p (t c) -> p t c", c=P)) \
                    .then_inc(sem["b_p_read"], 1)

            for k in range(NG + 1):
                if k < NG:
                    xT(k)
                if k >= 1:
                    first(k - 1)
                    second(k - 1)
                if k < NG:
                    mix(k)

        @block.tensor
        def _(pe):
            def bank(n):
                if n >= 2:
                    pe.wait_ge(sem["b_p_read"], n - 1)
                return mem.bank67[:, 0:512] if n % 2 else mem.bank45[:, 512:1024]

            def turn_x(i):
                pe.wait_ge(sem["b_copied"], i + 1)
                if i >= 1:
                    pe.wait_ge(sem["b_xT_ready"], i)
                for n in range(4):
                    last = nc.tensor.transpose(mem.bank0[:, n * P:(n + 1) * P], a.tiles[:, i % 2, n, :], mem.ident[:, :])
                last.then_inc(sem["b_xT_done"], 1)

            def mix(i):
                pe.wait_ge(sem["b_xm_ready"], i + 1)
                if i >= 1:
                    pe.wait_ge(sem["b_mix_ready"], i)
                nc.tensor.matmul(mem.bank12[:, 0:512], a.xA[:, 0:P], a.xm[:, :], start=True, stop=True)
                nc.tensor.matmul(mem.bank12[0:D, 512:1024], a.xA[:, P:192], a.xm[:, :], start=True, stop=True) \
                    .then_inc(sem["b_mix_done"], 1)

            def miu(i):
                pe.wait_ge(sem["b_mix_ready"], i + 1)
                for g in range(6):
                    n = 6 * i + g
                    rows = slice(32 * (g % 4), 32 * (g % 4) + 32)
                    if n >= 2:
                        pe.wait_ge(sem["b_xd_part"], n - 1)
                    nc.tensor.matmul((mem.bank3[:, :], mem.bank45[:, 0:512])[n % 2], a.xB[rows, g // 4, :],
                                     a.mix[rows, i % 2, g // 4, :], start=True, stop=True) \
                        .then_inc(sem["b_miu_done"], 1)

            def first(i):
                n = N_ACT * i
                R, WI, K, V, A, G = range(6)
                pe.wait_ge(sem["b_xd_ready"], 6 * i + R + 1)
                nc.tensor.matmul(bank(n), a.w128[:, 0, :], a.xd[:, R, :], start=True, stop=True) \
                    .then_inc(sem["b_p_done"], 1)
                for q, g in ((0, K), (1, WI), (2, A)):
                    pe.wait_ge(sem["b_xd_ready"], 6 * i + g + 1)
                    nc.tensor.matmul(bank(n + 1 + q)[0:D], a.w64[:, q, :], a.xd[:, g, :], start=True, stop=True) \
                        .then_inc(sem["b_p_done"], 1)
                pe.wait_ge(sem["b_xd_ready"], 6 * i + G + 1)
                nc.tensor.matmul(bank(n + 4), a.gA[:, :], a.xd[:, G, :], start=True, stop=True) \
                    .then_inc(sem["b_p_done"], 1)
                out = bank(n + 5)
                for t in range(4):
                    last = nc.tensor.matmul(out[:, t * P:(t + 1) * P], a.xd[:, V, t * P:(t + 1) * P], a.w128[:, 2, :],
                                            start=True, stop=True)
                out = bank(n + 6)
                last.then_inc(sem["b_p_done"], 1)
                nc.tensor.matmul(out, a.w128[:, 1, :], a.xd[:, K, :], start=True, stop=False)

            def second(i):
                n = N_ACT * i + 6
                pe.wait_ge(sem["b_p_read"], N_ACT * i + 5)
                nc.tensor.matmul(mem.bank67[:, 0:512] if n % 2 else mem.bank45[:, 512:1024], a.w128[0:D, 3, :],
                                 a.low[0:D, 0, :], start=False, stop=True).then_inc(sem["b_p_done"], 1)
                nc.tensor.matmul(bank(n + 1), a.w128[0:D, 5, :], a.low[0:D, 2, :], start=True, stop=True) \
                    .then_inc(sem["b_p_done"], 1)
                if i >= 1:
                    pe.wait_ge(sem["b_k_ready"], i)
                nc.tensor.matmul(mem.bank67[:, 512:1024], a.w128[0:D, 4, :], a.low[0:D, 1, :], start=True, stop=True) \
                    .then_inc(sem["b_z_done"], 1)
                out = bank(n + 2)
                for t in range(4):
                    last = nc.tensor.matmul(out[:, t * P:(t + 1) * P], a.low[:, 3, t * P:(t + 1) * P], a.w128[:, 6, :],
                                            start=True, stop=True)
                last.then_inc(sem["b_p_done"], 1)
                pe.wait_ge(sem["b_p_read"], n + 1)
                pe.wait_ge(sem["b_z_ready"], i + 1)
                for t in range(4):
                    last = nc.tensor.matmul(mem.bank67[:, 512 + t:513 + t], a.k_sq[:, t * P:(t + 1) * P], a.ones[:, 0:1],
                                            start=True, stop=True)
                last.then_inc(sem["b_ss_done"], 1)

            def norms(i):
                pe.wait_ge(sem["b_diag_ready"], i + 1)
                nc.tensor.matmul(mem.bank67[:, 512:1024], a.ones[:, :], a.k_diag[:, :, :].rearrange("p t c -> p (t c)"),
                                 start=True, stop=True).then_inc(sem["b_bc_done"], 1)

            pe.wait_ge(sem["b_consts"], 3)
            for k in range(NG + 2):
                if k >= 2:
                    norms(k - 2)
                if 1 <= k <= NG:
                    miu(k - 1)
                if k < NG:
                    turn_x(k)
                if 1 <= k <= NG:
                    first(k - 1)
                    second(k - 1)
                if k < NG:
                    mix(k)

    with nc.Block() as block:

        @block.vector
        def _(dve):
            def decay(i):
                b, c0 = cols(i)
                z = a.w[:, b, c0:c0 + HALF]
                dve.wait_ge(sem["b_abs"], i + 1)
                nc.vector.tensor_scalar(z, z, 0.0, -0.5, ALU.min, ALU.add).then_inc(sem["b_min"], 1)
                dve.wait_ge(sem["b_min"], i + 1)
                dve.wait_ge(sem["b_log"], i + 1)
                nc.vector.tensor_tensor(z, z, a.log[:, i], ALU.subtract).then_inc(sem["b_w_ready"], 1)
                dve.wait_ge(sem["b_w_ready"], i + 1)
                nc.vector.tensor_tensor_scan(a.cum[:, b, c0:c0 + HALF], a.resets[:, :], z, 0.0, ALU.mult,
                                             ALU.add).then_inc(sem["b_cum_ready"], 1)

            def kk(i):
                b, c0 = cols(i)
                dve.wait_ge(sem["b_half"], i + 1)
                dve.wait_ge(sem["b_w_ready"], i + 1)
                nc.vector.tensor_tensor(a.kb[:, 0, b, c0:c0 + HALF], a.ar[:, 0, b, c0:c0 + HALF], a.half[:, i % 2],
                                        ALU.mult).then_inc(sem["b_kk_ready"], 1)

            for i in range(NG):
                decay(i)
            for i in range(NG):
                kk(i)

        @block.scalar
        def _(act):
            for i in range(NG):
                b, c0 = cols(i)
                nc.scalar.activation(a.log[:, i], a.w[:, b, c0:c0 + HALF], ACT.Abs).then_inc(sem["b_abs"], 1)
            for i in range(NG):
                act.wait_ge(sem["b_abs"], i + 1)
                nc.scalar.activation(a.log[:, i], a.log[:, i], ACT.Exp, scale=-1.0).then_inc(sem["b_exp"], 1)
            for i in range(NG):
                act.wait_ge(sem["b_exp"], i + 1)
                nc.scalar.activation(a.log[:, i], a.log[:, i], ACT.Ln, bias=1.0).then_inc(sem["b_log"], 1)
            for i in range(NG):
                b, c0 = cols(i)
                act.wait_ge(sem["b_w_ready"], i + 1)
                if i >= 2:
                    act.wait_ge(sem["b_kk_ready"], i - 1)
                nc.scalar.activation(a.half[:, i % 2], a.w[:, b, c0:c0 + HALF], ACT.Exp, scale=0.5) \
                    .then_inc(sem["b_half"], 1)


def recurrence(nc, mem, a, sem):

    def at(i):
        return i + 1

    def later(i, count):
        return not isinstance(i, int) or i >= count

    def step_of(stages):
        def step(k, u, m=None):
            for lag, stage in stages:
                tile = tile_of(k, u, m, lag, B, NT)
                if tile is not None:
                    stage(*tile)
        return step

    EXP, LEV, ACC, DIAG, SOLVE, OUT = 0, 1, 2, 3, 4, 5
    ROUNDS = 5

    def chunk_view(ap, level):
        m = 1 << level
        return ap.rearrange("p (n h m) -> p n h m", h=2, m=m)

    def token_slice(t):
        return bass.ds(t * P, P)

    with nc.Block() as block:

        @block.gpsimd
        def _(pool):
            nc.gpsimd.memset(a.k_lev[:, :, :, :, :], 0.0).then_inc(sem["c_zeroed"], 1)
            nc.gpsimd.memset(a.r_t[:, :, :, :], 0.0).then_inc(sem["c_zeroed"], 1)
            nc.gpsimd.memset(a.acc[:, :, :, :], 0.0).then_inc(sem["c_zeroed"], 1)
            nc.gpsimd.memset(a.bd[:, :, :, :], 0.0).then_inc(sem["c_zeroed"], 1)
            nc.gpsimd.memset(a.q_lev[:, :, :, :, :, :], 0.0).then_inc(sem["c_zeroed"], 1)
            nc.gpsimd.memset(a.s[:, :, :, :], 0.0).then_inc(sem["c_zeroed"], 1)
            nc.gpsimd.memset(a.hat[:, :, :, :], 0.0).then_inc(sem["c_zeroed"], 1)
            nc.gpsimd.memset(a.e_in[:, :], 0.0).then_inc(sem["c_zeroed"], 1)
            pool.wait_ge(sem["c_zeroed"], 8)
            pool.wait_ge(sem["c_eye"], 1)

            def exponents(i, t, b):
                r = b % 2
                cum = a.cum[:, b, token_slice(t)]
                if later(i, 1):
                    pool.wait_ge(sem["c_exps"], at(i) - 1)
                for level in range(LEVELS):
                    m = 1 << level
                    n = D // m
                    left = chunk_view(cum, level)[:, :, 0, :]
                    right = chunk_view(cum, level)[:, :, 1, :]
                    mid = left[:, :, m - 1:m].to_broadcast([P, n, m])
                    out = a.e_in[:, 192 * level:192 * (level + 1)].rearrange("p (q n m) -> p q n m", q=3, m=m)
                    if m > 1:
                        nc.gpsimd.tensor_tensor(out[:, 0, :, 1:m], right[:, :, 0:m - 1],
                                                left[:, :, m - 1:m].to_broadcast([P, n, m - 1]), ALU.subtract)
                    nc.gpsimd.tensor_tensor(out[:, 1], right, mid, ALU.subtract)
                    nc.gpsimd.tensor_tensor(out[:, 2], mid, left, ALU.subtract)
                base = 192 * LEVELS
                chunks = cum.rearrange("p (c s) -> p c s", s=C)
                nc.gpsimd.tensor_tensor(a.e_in[:, base + P:base + 2 * P].rearrange("p (c s) -> p c s", s=C),
                                        chunks[:, :, C - 1:C].to_broadcast([P, NC, C]), chunks, ALU.subtract)
                nc.gpsimd.tensor_copy(a.e_in[:, base:base + P].rearrange("p (c s) -> p c s", s=C)[:, :, 1:C],
                                      chunks[:, :, 0:C - 1]).then_inc(sem["c_ein"], 1)

            def to_end(i, t, b):
                base = 192 * LEVELS
                if later(i, 2):
                    pool.wait_ge(sem["c_levels_done"], at(i) - 2)
                wait_apart(pool, i)
                nc.gpsimd.tensor_copy(a.kb_t[:, b % 2], a.kb[:, :, b, token_slice(t)]).then_inc(sem["c_raw"], 1)
                pool.wait_ge(sem["c_exps"], at(i))
                if later(i, B):
                    pool.wait_ge(sem["c_turned"], at(i) - B)
                    pool.wait_ge(sem["c_diag"], at(i) - B)
                pool.wait_ge(sem["c_raw"], at(i))
                nc.gpsimd.tensor_tensor(a.to_end[:, b], a.kb_t[:, b % 2],
                                        a.e_out[:, base + P:base + 2 * P].unsqueeze(1).to_broadcast([P, 2, P]),
                                        ALU.mult)
                nc.gpsimd.tensor_copy(a.decay[:, b, :], a.e_out[:, base + 2 * P + C - 1:base + 3 * P:C]) \
                    .then_inc(sem["c_to_end"], 1)

            def diagonal(i, t, b):
                pool.wait_ge(sem["c_to_end"], at(i))
                if later(i, 1):
                    pool.wait_ge(sem["c_m_ready"], at(i) - 1)
                nc.gpsimd.tensor_tensor(a.decay_diag[:, :, :], a.eye[:, :].unsqueeze(1).to_broadcast([P, NC, D]),
                                        a.decay[:, b, :].unsqueeze(2).to_broadcast([P, NC, D]),
                                        ALU.mult).then_inc(sem["c_diag"], 1)

            run_steps(pool, B, NT, OUT, step_of([(OUT, diagonal), (EXP, exponents), (LEV, to_end)]))

        @block.scalar
        def _(act):
            def exps(i, t, b):
                base = 192 * LEVELS
                act.wait_ge(sem["c_ein"], at(i))
                if later(i, 1):
                    act.wait_ge(sem["c_levels"], at(i) - 1)
                    act.wait_ge(sem["c_to_end"], at(i) - 1)
                nc.scalar.activation(a.e_out[:, 0:base], a.e_in[:, 0:base], ACT.Exp)
                nc.scalar.activation(a.e_out[:, base:base + 2 * P], a.e_in[:, base:base + 2 * P], ACT.Exp)
                nc.scalar.activation(a.e_out[:, base + 2 * P:base + 3 * P], a.cum[:, b, token_slice(t)],
                                     ACT.Exp).then_inc(sem["c_exps"], 1)
                if later(i, 2):
                    act.wait_ge(sem["c_levels_done"], at(i) - 2)
                elif i == 0:
                    act.wait_ge(sem["c_zeroed"], 8)
                for e in range(HB):
                    rows = slice(e * D, (e + 1) * D)
                    last = nc.scalar.copy(a.r_t[rows, b % 2, e, :], a.ar[rows, 1, b, token_slice(t)])
                last.then_inc(sem["c_r_raw"], 1)

            def block_diagonal(i, t, b):
                act.wait_ge(sem["c_acc"], at(i))
                if later(i, 2):
                    act.wait_ge(sem["c_y_done"], at(i) - 2)
                for c in range(NC):
                    rows = slice(c * C, (c + 1) * C)
                    last = nc.scalar.copy(a.bd[rows, b % 2, :, c * C:(c + 1) * C], a.acc[rows, b % 2])
                last.then_inc(sem["c_bd"], 1)

            def n_turned(i, t, b):
                act.wait_ge(sem["c_n_turned"], at(i))
                if later(i, 1):
                    act.wait_ge(sem["c_z_done"], ROUNDS * i)
                nc.scalar.copy(a.pw[:, 0, :, 0, :], mem.bank45[:, 512:768].rearrange("p (e s) -> p e s", e=2))
                nc.scalar.copy(a.pw[:, 0, :, 1, :], a.bd[:, b % 2, 4:8:2, :]).then_inc(sem["c_n_ready"], 1)

            def turned(i, t, b):
                act.wait_ge(sem["c_turned"], at(i))
                if later(i, 1):
                    act.wait_ge(sem["c_y_done"], at(i) - 1)
                nc.scalar.copy(a.z[:, :, 0, :], mem.bank0[:, 0:P].rearrange("p (e j) -> p e j", e=2))
                nc.scalar.copy(a.z[:, :, 1, :], mem.bank0[:, 3 * P:4 * P].rearrange("p (e j) -> p e j", e=2)) \
                    .then_inc(sem["c_z0"], 1)

            def hats(i, t, b):
                nc.scalar.copy(a.v_t[:, :], a.v_tok[:, b, t, :])
                for c in range(NC):
                    rows = slice(c * C, (c + 1) * C)
                    last = nc.scalar.copy(a.hat[rows, c], mem.bank0[rows, P:3 * P].rearrange("p (x j) -> p x j", x=2))
                last.then_inc(sem["c_hat"], 1)

            def power(n):
                def copy(i, t, b):
                    act.wait_ge(sem["c_sq_done"], (ROUNDS - 1) * i + n + 1)
                    if n:
                        act.wait_ge(sem["c_z_done"], ROUNDS * i + n)
                    nc.scalar.copy(a.pw[:, (n + 1) % 2], mem.bank45[:, 512:1024].rearrange("p (e x s) -> p e x s", e=2, x=2)) \
                        .then_inc(sem["c_p_ready"], 1)
                return copy

            def y_and_own(i, t, b):
                act.wait_ge(sem["c_y_done"], at(i))
                if later(i, B):
                    act.wait_ge(sem["c_y_ready"], t)
                nc.scalar.copy(a.yc[:, b, :], mem.bank67[:, 512:512 + P + NC * D]).then_inc(sem["c_yc_ready"], 1)

            run_steps(act, B, NT, OUT, step_of([
                (SOLVE, n_turned), (SOLVE, turned), (SOLVE, power(0)), (OUT, y_and_own), (SOLVE, power(1)),
                (SOLVE, hats), (SOLVE, power(2)), (DIAG, block_diagonal), (SOLVE, power(3)), (EXP, exps)]))

        @block.vector
        def _(dve):
            dve.wait_ge(sem["c_zeroed"], 8)
            nc.vector.tensor_tensor(a.eye[:, :], mem.ident[:, 0:D], mem.ident[:, D:P], ALU.add) \
                .then_inc(sem["c_eye"], 1)

            def level_inputs(level):
                def inputs(i, t, b):
                    r = b % 2
                    if level == 0:
                        dve.wait_ge(sem["c_exps"], at(i))
                        if later(i, 2):
                            dve.wait_ge(sem["c_levels_done"], at(i) - 2)
                    m = 1 << level
                    e = a.e_out[:, 192 * level:192 * (level + 1)].rearrange("p (q n m) -> p q n m", q=3, m=m)
                    for x in range(2):
                        nc.vector.tensor_tensor(
                            chunk_view(a.k_lev[:, r, level, x, :], level)[:, :, 0, :],
                            chunk_view(a.kb[:, x, b, token_slice(t)], level)[:, :, 0, :], e[:, 2], ALU.mult)
                    for head in range(HB):
                        rows = slice(head * D, (head + 1) * D)
                        for x in range(2):
                            nc.vector.tensor_tensor(
                                a.q_lev[rows, r, level, head, x, :].rearrange("p (n m) -> p n m", m=m),
                                chunk_view(a.ar[rows, x, b, token_slice(t)], level)[:, :, 1, :], e[rows, x], ALU.mult)
                return inputs

            def from_start(i, t, b):
                base = 192 * LEVELS
                if later(i, B):
                    dve.wait_ge(sem["c_m_ready"], at(i) - B)
                nc.vector.tensor_tensor(a.from_start[:, b, 0, :], a.ar[:, 0, b, token_slice(t)],
                                        a.e_out[:, base:base + P], ALU.mult)
                nc.vector.tensor_tensor(a.from_start[:, b, 1, :], a.ar[:, 1, b, token_slice(t)],
                                        a.e_out[:, base + 2 * P:base + 3 * P], ALU.mult).then_inc(sem["c_levels"], 1)

            def accumulate(i, t, b):
                r = b % 2
                dve.wait_ge(sem["c_levels_done"], at(i))
                if later(i, 2):
                    dve.wait_ge(sem["c_bd"], at(i) - 2)
                for level in range(LEVELS):
                    if level:
                        dve.wait_ge(sem["c_acc_level"], LEVELS * i + level)
                    wait_apart(dve, i)
                    m = 1 << level
                    n = C // (2 * m)
                    out = a.acc[:, r].rearrange("p q (n h m) -> p q n h m", h=2, m=m)[:, :, :, 1, :]
                    mask = a.masks[:, level, :].rearrange("p (n m) -> p n m", m=m).unsqueeze(1) \
                        .to_broadcast([P, 8, n, m]).bitcast(mybir.dt.int32)
                    data = mem.bank12[:, P * level:P * (level + 1)].rearrange("p (q n m) -> p q n m", q=8, m=m)
                    nc.vector.copy_predicated(out, mask, data).then_inc(sem["c_acc_level"], 1)
                dve.wait_ge(sem["c_acc_level"], LEVELS * at(i))
                wait_apart(dve, i)
                out = a.acc[:, r, 1:8:2, :]
                last = nc.vector.copy_predicated(
                    out, a.diag[:, :].unsqueeze(1).to_broadcast([P, 4, C]).bitcast(mybir.dt.int32),
                    mem.bank12[:, P * LEVELS:P * (LEVELS + 1)].rearrange("p (q s) -> p q s", q=4))
                last.then_inc(sem["c_acc"], 1)

            def solve(n):
                def add(i, t, b):
                    z = a.z[:, :, :, :].rearrange("p e x j -> p (e x j)")
                    dve.wait_ge(sem["c_z_done"], ROUNDS * i + n + 1)
                    nc.vector.tensor_tensor(z, z, mem.bank67[:, 0:256], ALU.add).then_inc(sem["c_z_ready"], 1)
                return add

            def chunk_parts(i, t, b):
                dve.wait_ge(sem["c_m_done"], at(i))
                dve.wait_ge(sem["c_diag"], at(i))
                if later(i, B):
                    dve.wait_ge(sem["c_y_ready"], t)
                nc.vector.tensor_tensor(a.m_t[:, b], mem.bank67[:, 0:256].rearrange("p (c j) -> p c j", c=NC),
                                        a.decay_diag[:, :, :], ALU.add)
                nc.vector.tensor_tensor(a.g_t[:, b, :], mem.bank67[:, 256:384], a.from_start[:, b, 1, :],
                                        ALU.add).then_inc(sem["c_m_ready"], 1)

            def state(c):
                def add(i, t, b):
                    if b != B - 1:
                        return
                    n = 4 * t + c
                    dve.wait_ge(sem["c_s_done"], n + 1)
                    if c == 0:
                        dve.wait_ge(sem["c_yc_ready"], 4 * t + 4)
                    nc.vector.tensor_tensor(a.s[:, (c + 1) % 2], a.yc[:, :, P + c * D:P + (c + 1) * D],
                                            mem.bank45[:, 0:256].rearrange("p (b j) -> p b j", b=B),
                                            ALU.add).then_inc(sem["c_s_ready"], 1)
                return add

            def outputs(i, t, b):
                if b != B - 1:
                    return
                dve.wait_ge(sem["c_yp_done"], t + 1)
                nc.vector.tensor_tensor(a.y_tok[:, :, t, :], a.yc[:, :, 0:P],
                                        mem.bank3[:, :].rearrange("p (b c) -> p b c", b=B),
                                        ALU.add).then_inc(sem["c_y_ready"], 1)

            order = [(OUT, chunk_parts)]
            for n in range(NC):
                order += [(OUT, state(n)), (SOLVE, solve(n)), (LEV, level_inputs(n))]
            order += [(OUT, outputs), (SOLVE, solve(4)), (LEV, level_inputs(4)), (LEV, from_start), (ACC, accumulate)]
            run_steps(dve, B, NT, OUT, step_of(order))

        @block.tensor
        def _(pe):
            pe.wait_ge(sem["c_zeroed"], 8)

            def chunk_parts(i, t, b):
                r = b % 2
                pe.wait_ge(sem["c_z_ready"], ROUNDS * i + ROUNDS)
                pe.wait_ge(sem["c_hat"], at(i))
                if later(i, 1):
                    pe.wait_ge(sem["c_m_ready"], at(i) - 1)
                    pe.wait_ge(sem["c_yc_ready"], at(i) - 1)
                for e in range(HB):
                    heads = slice(e * D, (e + 1) * D)
                    nc.tensor.matmul(mem.bank67[heads, 0:NC * D], a.z[:, e, 0, :], a.hat[:, :, 1, heads],
                                     start=True, stop=True)
                for e in range(HB):
                    last = nc.tensor.matmul(mem.bank67[e * D:(e + 1) * D, 256:384], a.z[:, e, 0, :],
                                            a.bd[:, r, 4 + 2 * e + 1, :], start=True, stop=True)
                last.then_inc(sem["c_m_done"], 1)
                for e in range(HB):
                    heads = slice(e * D, (e + 1) * D)
                    out = mem.bank67[:, 512 + e * D:512 + (e + 1) * D]
                    nc.tensor.matmul(out, a.bd[:, r, 4 + 2 * e + 1, :], a.z[:, e, 1, :], start=True, stop=False)
                    nc.tensor.matmul(out, a.bd[:, r, 2 * e + 1, :], a.v_t[:, heads], start=False, stop=True)
                for c in range(NC):
                    for e in range(HB):
                        heads = slice(e * D, (e + 1) * D)
                        out = mem.bank67[heads, 512 + P + c * D:512 + P + (c + 1) * D]
                        nc.tensor.matmul(out, a.hat[:, c, 1, heads], a.z[:, e, 1, :], start=True, stop=False)
                        last = nc.tensor.matmul(out, a.hat[:, c, 0, heads], a.v_t[:, heads],
                                                start=False, stop=True)
                last.then_inc(sem["c_y_done"], 1)

            def turn(i, t, b):
                r = b % 2
                pe.wait_ge(sem["c_bd"], at(i))
                if later(i, 1):
                    pe.wait_ge(sem["c_p_ready"], (ROUNDS - 1) * i)
                    pe.wait_ge(sem["c_z0"], at(i) - 1)
                for e in range(HB):
                    last = nc.tensor.transpose(mem.bank45[:, 512 + e * P:512 + (e + 1) * P], a.bd[:, r, 4 + 2 * e, :],
                                               mem.ident[:, :])
                last.then_inc(sem["c_n_turned"], 1)
                pe.wait_ge(sem["c_levels"], at(i))
                pe.wait_ge(sem["c_to_end"], at(i))
                nc.tensor.transpose(mem.bank0[:, 0:P], a.from_start[:, b, 0, :], mem.ident[:, :])
                for x in range(2):
                    nc.tensor.transpose(mem.bank0[:, (1 + x) * P:(2 + x) * P], a.to_end[:, b, x, :], mem.ident[:, :])
                for e in range(HB):
                    last = nc.tensor.matmul(mem.bank0[:, 3 * P + e * D:3 * P + (e + 1) * D], a.bd[:, r, 2 * e, :],
                                            a.v_tok[:, b, t, e * D:(e + 1) * D], start=True, stop=True)
                last.then_inc(sem["c_turned"], 1)

            def square(n, i, t, b):
                if n == 0:
                    pe.wait_ge(sem["c_n_ready"], at(i))
                else:
                    pe.wait_ge(sem["c_p_ready"], (ROUNDS - 1) * i + n)
                for e in range(HB):
                    for x in range(2):
                        last = nc.tensor.matmul(mem.bank45[:, 512 + (2 * e + x) * P:512 + (2 * e + x + 1) * P],
                                                a.pw[:, n % 2, e, 1 - x, :], a.pw[:, n % 2, e, x, :],
                                                start=True, stop=True)
                last.then_inc(sem["c_sq_done"], 1)

            def solve_round(n, i, t, b):
                if n == 0:
                    pe.wait_ge(sem["c_z0"], at(i))
                    if later(i, 1):
                        pe.wait_ge(sem["c_m_ready"], at(i) - 1)
                else:
                    pe.wait_ge(sem["c_z_ready"], ROUNDS * i + n)
                if n == ROUNDS - 1:
                    pe.wait_ge(sem["c_p_ready"], (ROUNDS - 1) * i + n)
                for e in range(HB):
                    last = nc.tensor.matmul(mem.bank67[:, e * P:(e + 1) * P], a.pw[:, n % 2, e, 1, :],
                                            a.z[:, e].rearrange("p x j -> p (x j)"), start=True, stop=True)
                last.then_inc(sem["c_z_done"], 1)

            def level_chunk(c, i, t, b):
                r = b % 2
                if c == 0:
                    pe.wait_ge(sem["c_levels"], at(i))
                    pe.wait_ge(sem["c_raw"], at(i))
                    pe.wait_ge(sem["c_r_raw"], at(i))
                    if later(i, 1):
                        pe.wait_ge(sem["c_acc"], at(i) - 1)
                rows = slice(c * C, (c + 1) * C)
                for level in range(LEVELS):
                    q = a.q_lev[:, r, level, :, :, c * C // 2:(c + 1) * C // 2].rearrange("p e x m -> p (e x) m")
                    for x in range(2):
                        nc.tensor.matmul(mem.bank12[rows, P * level + D * x:P * level + D * (x + 1)],
                                         a.k_lev[:, r, level, x, rows], q, start=True, stop=True)
                for x in range(2):
                    last = nc.tensor.matmul(mem.bank12[rows, P * LEVELS + D * x:P * LEVELS + D * (x + 1)],
                                            a.kb_t[:, r, x, rows], a.r_t[:, r, :, rows], start=True, stop=True)
                if c == NC - 1:
                    last.then_inc(sem["c_levels_done"], 1)

            def state(c, i, t, b):
                if b != B - 1:
                    return
                n = 4 * t + c
                if c == 0:
                    pe.wait_ge(sem["c_m_ready"], 4 * t + 4)
                    if not isinstance(t, int) or t >= 1:
                        pe.wait_ge(sem["c_y_ready"], t)
                if not (isinstance(t, int) and n == 0):
                    pe.wait_ge(sem["c_s_ready"], n)
                wait_apart(pe, i)
                for e in range(HB):
                    heads = slice(e * D, (e + 1) * D)
                    for bb in range(B):
                        last = nc.tensor.matmul(mem.bank45[heads, bb * D:(bb + 1) * D], a.m_t[heads, bb, c, :],
                                                a.s[heads, c % 2, bb, :], start=True, stop=True)
                last.then_inc(sem["c_s_done"], 1)
                state_outputs(c, 0, n)

            def state_outputs(c, e, n):
                if e:
                    pe.wait_ge(sem["c_yp_half"], n + 1)
                    wait_apart(pe, n)
                heads = slice(e * D, (e + 1) * D)
                for bb in range(B):
                    last = nc.tensor.matmul(mem.bank3[c * C:(c + 1) * C, bb * P + e * D:bb * P + (e + 1) * D],
                                            a.g_t[heads, bb, c * C:(c + 1) * C], a.s[heads, c % 2, bb, :],
                                            start=True, stop=True)
                if not e:
                    last.then_inc(sem["c_yp_half"], 1)
                elif c == NC - 1:
                    last.then_inc(sem["c_yp_done"], 1)

            def second_head(c, i, t, b):
                if b == B - 1:
                    state_outputs(c, 1, 4 * t + c)

            def step(k, u, m=None):
                def do(lag, stage, *which):
                    tile = tile_of(k, u, m, lag, B, NT)
                    if tile is not None:
                        stage(*which, *tile)
                do(SOLVE, turn)
                do(OUT, chunk_parts)
                for c in range(NC):
                    do(SOLVE, square, c)
                    do(OUT, state, c)
                    do(SOLVE, solve_round, c)
                    do(ACC, level_chunk, c)
                    do(OUT, second_head, c)
                do(SOLVE, solve_round, ROUNDS - 1)

            run_steps(pe, B, NT, OUT, step)


def time_mixing_outputs(nc, mem, a, sem):

    def cols(i):
        b, half = divmod(i, 2)
        return b, half * HALF

    def heads(ap):
        return ap.rearrange("p t (h j) -> p (t h) j", h=HB)

    def wide(ap):
        return ap.unsqueeze(2).to_broadcast([P, 8, D])

    with nc.Block() as block:

        @block.gpsimd
        def _(pool):
            def products(i):
                b, c0 = cols(i)
                if i >= 2:
                    pool.wait_ge(sem["d_coef_done"], i - 1)
                nc.gpsimd.tensor_tensor(a.rk[:, i % 2, :], a.ar[:, 0, b, c0:c0 + HALF], a.ar[:, 1, b, c0:c0 + HALF],
                                        ALU.mult).then_inc(sem["d_rk"], 1)

            def rstd(i):
                pool.wait_ge(sem["d_mom"], i + 1)
                nc.gpsimd.tensor_scalar(a.y_rstd[:, i % 2, :], a.y_mom[:, i % 2, :, 1], GN_EPS, None,
                                        ALU.add).then_inc(sem["d_eps"], 1)
                pool.wait_ge(sem["d_eps"], i + 1)
                nc.gpsimd.tensor_tensor(a.y_rstd[:, i % 2, :], a.y_rstd[:, i % 2, :], mem.minus_half[:, 0:8],
                                        ALU.pow).then_inc(sem["d_rstd"], 1)

            def bonus(i):
                b, c0 = cols(i)
                t = c0 // P
                pool.wait_ge(sem["d_coef_ready"], i + 1)
                if i >= 2:
                    pool.wait_ge(sem["d_sum"], i - 1)
                nc.gpsimd.tensor_tensor(heads(a.bon[:, i % 2]), heads(a.v_tok[:, b, t:t + 4, :]),
                                        wide(a.coef[:, i % 2, :]), ALU.mult).then_inc(sem["d_bonus"], 1)

            products(0)
            for i in range(NG):
                if i + 1 < NG:
                    products(i + 1)
                rstd(i)
                bonus(i)

        @block.vector
        def _(dve):
            def stats(i):
                b, c0 = cols(i)
                t = c0 // P
                for n in range(8):
                    last = nc.vector.bn_stats(a.y_stats[:, i % 2, n, :],
                                              a.y_tok[:, b, t + n // 2, (n % 2) * D:(n % 2 + 1) * D])
                last.then_inc(sem["d_stats"], 1)
                dve.wait_ge(sem["d_stats"], i + 1)
                for n in range(8):
                    last = nc.vector.bn_aggr(a.y_mom[:, i % 2, n, :], a.y_stats[:, i % 2, n, :])
                last.then_inc(sem["d_mom"], 1)

            def finish(i):
                b, c0 = cols(i)
                t = c0 // P
                y = a.y1[:, i % 2]
                if i >= 2:
                    dve.wait_ge(sem["d_yT_done"], i - 1)
                nc.vector.tensor_tensor(heads(y), heads(a.y_tok[:, b, t:t + 4, :]), wide(a.y_mom[:, i % 2, :, 0]),
                                        ALU.subtract).then_inc(sem["d_c1"], 1)
                dve.wait_ge(sem["d_c1"], i + 1)
                dve.wait_ge(sem["d_rstd"], i + 1)
                nc.vector.tensor_tensor(heads(y), heads(y), wide(a.y_rstd[:, i % 2, :]), ALU.mult) \
                    .then_inc(sem["d_normed"], 1)
                dve.wait_ge(sem["d_normed"], i + 1)
                nc.vector.tensor_tensor(y, y, a.gn[:, 0].unsqueeze(1).to_broadcast([P, 4, P]), ALU.mult) \
                    .then_inc(sem["d_g1"], 1)
                dve.wait_ge(sem["d_g1"], i + 1)
                nc.vector.tensor_tensor(y, y, a.gn[:, 1].unsqueeze(1).to_broadcast([P, 4, P]), ALU.add) \
                    .then_inc(sem["d_g2"], 1)
                dve.wait_ge(sem["d_g2"], i + 1)
                dve.wait_ge(sem["d_bonus"], i + 1)
                nc.vector.tensor_tensor(y, y, a.bon[:, i % 2], ALU.add).then_inc(sem["d_sum"], 1)
                dve.wait_ge(sem["d_sum"], i + 1)
                nc.vector.tensor_tensor(y, y, a.g_tok[:, b, t:t + 4, :], ALU.mult).then_inc(sem["d_gated"], 1)

            def residual(i):
                b, c0 = cols(i)
                t = c0 // P
                dve.wait_ge(sem["d_o_done"], i + 1)
                nc.vector.tensor_tensor(mem.x[:, b, t:t + 4, :], mem.x[:, b, t:t + 4, :],
                                        mem.bank3[:, :].rearrange("p (t c) -> p t c", t=4), ALU.add) \
                    .then_inc(sem["d_added"], 1)

            stats(0)
            for i in range(NG):
                if i + 1 < NG:
                    stats(i + 1)
                finish(i)
                if i >= 1:
                    residual(i - 1)
            residual(NG - 1)

        @block.scalar
        def _(act):
            def coefs(i):
                act.wait_ge(sem["d_coef_done"], i + 1)
                if i >= 2:
                    act.wait_ge(sem["d_bonus"], i - 1)
                nc.scalar.copy(a.coef[:, i % 2, :], mem.bank0[:, 0:8]).then_inc(sem["d_coef_ready"], 1)

            coefs(0)
            for i in range(NG):
                if i + 1 < NG:
                    coefs(i + 1)
                act.wait_ge(sem["d_yT_done"], i + 1)
                if i >= 2:
                    act.wait_ge(sem["d_o_done"], i - 1)
                nc.scalar.copy(a.yT[:, i % 2], mem.bank12[:, 0:512].rearrange("p (t c) -> p t c", t=4)) \
                    .then_inc(sem["d_yT_ready"], 1)

        @block.tensor
        def _(pe):
            def coefs(i):
                pe.wait_ge(sem["d_rk"], i + 1)
                if i >= 1:
                    pe.wait_ge(sem["d_coef_ready"], i)
                for t in range(4):
                    last = nc.tensor.matmul(mem.bank0[:, 2 * t:2 * t + 2], a.rk[:, i % 2, t * P:(t + 1) * P],
                                            a.bonus_w[:, :], start=True, stop=True)
                last.then_inc(sem["d_coef_done"], 1)

            coefs(0)
            for i in range(NG):
                if i + 1 < NG:
                    coefs(i + 1)
                pe.wait_ge(sem["d_gated"], i + 1)
                if i >= 1:
                    pe.wait_ge(sem["d_yT_ready"], i)
                for t in range(4):
                    last = nc.tensor.transpose(mem.bank12[:, t * P:(t + 1) * P], a.y1[:, i % 2, t, :], mem.ident[:, :])
                last.then_inc(sem["d_yT_done"], 1)
                pe.wait_ge(sem["d_yT_ready"], i + 1)
                if i >= 1:
                    pe.wait_ge(sem["d_added"], i)
                for t in range(4):
                    last = nc.tensor.matmul(mem.bank3[:, t * P:(t + 1) * P], a.yT[:, i % 2, t, :], a.oW[:, :],
                                            start=True, stop=True)
                last.then_inc(sem["d_o_done"], 1)


def attn_b_inputs(nc, a, arr, loaded):
    loads = [(a.w128[:, :, :], arr["b_w128"]), (a.oW[:, :], arr["b_oW"]), (a.gA[:, :], arr["b_gA"]), (a.vec[:, :], arr["b_vec"]),
             (a.bonus_w[:, :], arr["b_bonus_w"]), (a.xA[:, :], arr["b_xA"]),
             (a.xB[:, :, :], arr["b_xB"]), (a.w64[:, :, :], arr["b_w64"]), (a.resets[:, :], arr["resets"])]
    for dst, src in loads:
        nc.sync.dma_start(dst, src).then_inc(loaded, 16)
    return len(loads)


def attn_b_layout(v):
    w128 = np.zeros((P, 7, P), np.float32)
    for n, name in enumerate(("rW", "kW", "vW")):
        w128[:, n] = v[name].T
    for n, name in enumerate(("k_B", "w_B", "a_B", "g_B")):
        w128[:v[name].shape[0], 3 + n] = v[name]
    vec = np.zeros((P, 10), np.float32)
    vec[:, 0], vec[:, 1], vec[:, 2] = v["x_miu"].ravel(), v["w_miu"].ravel(), v["a_time"].ravel()
    vec[:, 4:10] = v["lambdas"].reshape(6, P).T
    bonus = np.zeros((P, HB), np.float32)
    xb = np.zeros((P, 2, P), np.float32)
    for h in range(HB):
        bonus[h * D:(h + 1) * D, h] = v["x_time"][h]
    for g in range(6):
        xb[32 * (g % 4):32 * (g % 4) + 32, g // 4] = v["x_B"][g]
    return {"b_w128": w128, "b_oW": np.ascontiguousarray(v["oW"].T), "b_gA": v["g_A"], "b_vec": vec, "b_bonus_w": bonus, "b_xA": v["x_A"], "b_xB": xb,
            "b_w64": np.ascontiguousarray(np.stack([v["k_A"], v["w_A"], v["a_A"]], 1)),
            "b_gn": np.repeat(np.stack([v["gn_gamma"], v["gn_beta"]])[None], P, 0)}


def attn_b_constants():
    s, t = np.arange(P)[:, None] % C, np.arange(C)[None, :]
    masks = np.zeros((P, LEVELS, C // 2), np.float32)
    for level in range(LEVELS):
        m = 1 << level
        right = t[:, (t[0] // m) % 2 == 1]
        masks[:, level] = (s // (2 * m) == right // (2 * m)) & ((s // m) % 2 == 0)
    resets = np.ones((P, HALF), np.float32)
    resets[:, ::C] = 0.0
    return {"b_masks": masks, "b_diag": (s == t).astype(np.float32), "resets": resets}


LN_SEMS = ("l_summed", "l_stats", "l_var", "l_eps", "l_rstd", "l_ready")


def layernorm(nc, mem, sem, run, addend, loads=None, memsets=()):

    def at(b):
        return B * run + b + 1

    with nc.Block() as block:

        @block.vector
        def _(dve):
            def stats(b):
                if addend is not None:
                    nc.vector.tensor_tensor(mem.x[:, b], mem.x[:, b], addend[:, b, 1:T + 1, :],
                                            ALU.add).then_inc(sem["l_summed"], 1)
                    dve.wait_ge(sem["l_summed"], b + 1)
                for i in range(T * b, T * (b + 1)):
                    last = nc.vector.bn_stats(mem.stats[:, i, :], mem.x[:, b, i % T, :])
                last.then_inc(sem["l_stats"], 1)
                dve.wait_ge(sem["l_stats"], at(b))
                for i in range(T * b, T * (b + 1)):
                    last = nc.vector.bn_aggr(mem.moments[:, i, :], mem.stats[:, i, :])
                last.then_inc(sem["l_var"], 1)

            def normalise(b):
                dve.wait_ge(sem["l_rstd"], at(b))
                for i in range(T * b, T * (b + 1)):
                    last = nc.vector.tensor_scalar(mem.ua[:, b, i % T + 1, :], mem.x[:, b, i % T, :],
                                                   mem.moments[:, i, 0:1], mem.rstd[:, i:i + 1],
                                                   ALU.subtract, ALU.mult)
                last.then_inc(sem["l_ready"], 1)

            for b in range(B + 1):
                if b < B:
                    stats(b)
                if b:
                    normalise(b - 1)
            dve.wait_ge(sem["l_ready"], at(B - 1))

        @block.gpsimd
        def _(pool):
            for ap, value in memsets:
                nc.gpsimd.memset(ap, value)
            for b in range(B):
                tiles = slice(T * b, T * (b + 1))
                pool.wait_ge(sem["l_var"], at(b))
                nc.gpsimd.tensor_scalar(mem.rstd[:, tiles], mem.moments[:, tiles, 1], LN_EPS, None,
                                        ALU.add).then_inc(sem["l_eps"], 1)
                pool.wait_ge(sem["l_eps"], at(b))
                nc.gpsimd.tensor_tensor(mem.rstd[:, tiles], mem.rstd[:, tiles], mem.minus_half[:, tiles],
                                        ALU.pow).then_inc(sem["l_rstd"], 1)

        if loads is not None:
            @block.sync
            def _(sync):
                sync.wait_ge(mem.loaded, 16 * loads())


def ffn_inputs(nc, mem, f, a, loaded):
    loads = [
        (f.wqkv[:, :, :], a["wqkv"].rearrange("l c n -> c l n")),
        (f.wo[:, :, :, :], a["wo"].rearrange("l (k p) n -> p (l k) n", p=P)),
        (f.w1[:, :, :], a["w1"].rearrange("l c n -> c l n")),
        (f.w2[:, :, :, :], a["w2"]),
        (f.b1[:, :, :, :], a["b1"]),
        (f.b2[:, :, :], a["b2"]),
        (f.lnp[:, :, :], a["lnp"]),
        (f.rope_raw[:, :, :, :], a["rope"]),
        (f.qk_scales[:, :, :, :], a["qk_scales"]),
        (f.mask[:, :, :], a["mask"]),
        (f.shift[:, :, :], a["shift"]),
    ]
    for dst, src in loads:
        nc.sync.dma_start(dst, src).then_inc(loaded, 16)
    return len(loads)


def shape_constants():
    k = np.arange(P)
    shift = np.zeros((P, 2, P), np.float32)
    shift[k[:-1], 0, k[1:]] = 1.0
    shift[P - 1, 1, 0] = 1.0
    tok = np.arange(P)[:, None]
    keys = np.empty((P, P), np.int64)
    keys[:W] = np.concatenate([np.arange(W), np.arange(-W, 0)])
    keys[W:] = np.arange(P)
    seen = (tok >= keys) & (tok <= keys + W)
    mask = np.zeros((P, T, P), np.float32)
    mask[~np.repeat(seen[:, None, :], T, 1)] = MASKED
    mask[:, 0][keys < 0] = MASKED
    half = np.arange(0, D, 2, dtype=np.float32)
    inv_freq = (np.float32(1.0) / np.float32(10000.0) ** (half / np.float32(D))).astype(np.float32)
    pos = np.arange(T * P, dtype=np.float32)
    freqs = (pos[:, None] * inv_freq[None, :]).astype(np.float32)
    base = ((half + np.float32(0.4 * D)) / np.float32(1.4 * D)).astype(np.float32)
    power = ((pos - T * P // 2) / np.float32(W // 2)).astype(np.float32)
    scale = base[None, :].astype(np.float64) ** power[:, None].astype(np.float64)
    cos, sin = np.cos(freqs.astype(np.float64)), np.sin(freqs.astype(np.float64))
    cos, sin, scale = (np.concatenate([v, v], 1) for v in (cos, sin, scale))
    sin[:, :D // 2] *= -1.0
    rope = np.stack([cos * scale, cos / scale, sin * scale, sin / scale], 1).astype(np.float32)
    rope = np.ascontiguousarray(rope.reshape(T, P, 4, D).transpose(1, 0, 2, 3))
    head = np.arange(P) // DA
    return {"blocks": (head[:, None] == head[None, :]).astype(np.float32),
            "ident": np.eye(P, dtype=np.float32), "shift": shift, "mask": mask, "rope": rope}


def ffn_layout(v):
    b1 = np.zeros((P, DEPTH, 2, 3), np.float32)
    for half in range(2):
        for c, (c0, m) in enumerate(CH):
            b1[:m, :, half, c] = v["b1"][:, half * HID + c0:half * HID + c0 + m].T
    w2 = np.zeros((P, DEPTH, 3, P), np.float32)
    for c, (c0, m) in enumerate(CH):
        w2[:m, :, c] = v["w2"][:, c0:c0 + m].transpose(1, 0, 2)
    qs, ks = v["q_scale"], v["k_scale"]
    swap = np.r_[D // 2:D, 0:D // 2]
    rows = np.stack([qs, ks, qs[:, swap], ks[:, swap]], 1)
    return {"wqkv": v["wqkv"], "wo": v["wo"], "w1": v["w1"], "w2": w2, "b1": b1,
            "b2": np.repeat(v["b2"][None], P, 0),
            "lnp": np.ascontiguousarray(np.stack([v["ln_g"], v["ln_b"]], 2).transpose(1, 0, 2)),
            "qk_scales": np.repeat(rows[None], P, 0)}


@contextmanager
def semaphores(nc, names):
    sem = {name: nc.alloc_semaphore(name) for name in names}
    yield sem
    nc.clear_and_free_semaphores(list(sem.values()))
    nc.all_engine_barrier()


def load_block(nc, loads, loaded, before, memsets=()):
    count = {}
    with nc.Block() as block:

        @block.sync
        def _(sync):
            count["all"] = before + loads()
            sync.wait_ge(loaded, 16 * count["all"])

        if memsets:
            @block.gpsimd
            def _(pool):
                for ap, value in memsets:
                    nc.gpsimd.memset(ap, value)
    return count["all"]


def hybrid_block(nc, arr, out):
    with ExitStack() as ctx:
        mem = Memory(nc, ctx)
        loaded = mem.loaded
        stored = ctx.enter_context(nc.semaphore("stored"))
        lasting = {name: ctx.enter_context(nc.semaphore(name)) for name in LN_SEMS + ATT_SEMS + FF_SEMS}

        def load(pairs):
            for dst, src in pairs:
                nc.sync.dma_start(dst, src).then_inc(loaded, 16)
            return len(pairs)

        with ExitStack() as phase:
            a = AttnAMemory(nc, phase)
            n = load_block(nc, lambda: attn_a_inputs(nc, a, arr, loaded) + load(
                [(mem.x[:, b], arr["x"][b].rearrange("(t p) c -> p t c", p=P)) for b in range(B)]
                + [(mem.ident[:, :], arr["ident"])]), loaded, 0,
                [(mem.minus_half[:, :], -0.5), (mem.ua[:, :, 0, :], 0.0)])
            with semaphores(nc, A_SEMS) as sem:
                linear_attention(nc, mem, a, sem)

        def transformer(n, times):
            with ExitStack() as phase:
                f = FfnMemory(nc, phase, mem, times)
                count = []

                def loads():
                    count.append(n + ffn_inputs(nc, mem, f, arr, loaded))
                    return count[0]

                layernorm(nc, mem, lasting, 2 * times, None, loads,
                          [(f.ub[:, :, 0, :], 0.0), (mem.ua[:, :, 0, :], 0.0)])
                for layer in range(DEPTH):
                    src, dst = (f.ub, mem.ua) if layer % 2 else (mem.ua, f.ub)
                    run = DEPTH * times + layer
                    attention(nc, mem, f, lasting, src, layer, run)
                    feed_forward(nc, mem, f, lasting, src, dst, layer, run)
            return count[0]

        n = transformer(n, 0)

        with ExitStack() as phase:
            a = AttnBMemory(nc, phase)
            with ExitStack() as stage, semaphores(nc, B1_SEMS) as sem:
                a.stage_one(nc, stage)
                count = []

                def loads():
                    count.append(n + attn_b_inputs(nc, a, arr, loaded))
                    return count[0]

                layernorm(nc, mem, lasting, 1, mem.ua, loads)
                n = count[0]
                time_mixing_inputs(nc, mem, a, sem)
            with ExitStack() as stage, semaphores(nc, B2_SEMS) as sem:
                a.stage_two(nc, stage, mem)
                n = load_block(nc, lambda: load([(a.masks[:, :, :], arr["b_masks"]), (a.diag[:, :], arr["b_diag"])]),
                               loaded, n)
                recurrence(nc, mem, a, sem)
            with ExitStack() as stage, semaphores(nc, B3_SEMS) as sem:
                a.stage_three(nc, stage)
                n = load_block(nc, lambda: load([(a.gn[:, :, :], arr["b_gn"])]), loaded, n)
                time_mixing_outputs(nc, mem, a, sem)

        transformer(n, 1)

        with nc.Block() as block:

            @block.vector
            def _(dve):
                for b in range(B):
                    nc.vector.tensor_tensor(mem.x[:, b], mem.x[:, b], mem.ua[:, b, 1:T + 1, :],
                                            ALU.add).then_inc(lasting["l_summed"], 1)

            @block.sync
            def _(sync):
                for b in range(B):
                    sync.wait_ge(lasting["l_summed"], B + b + 1)
                    nc.sync.dma_start(out[b].rearrange("(t p) c -> p t c", p=P), mem.x[:, b]).then_inc(stored, 16)
                sync.wait_ge(stored, 16 * B)


def kernel(**inputs):
    import concourse.bacc as bacc
    from concourse.bass_utils import run_bass_kernel_spmd

    def part(prefix):
        return {name[len(prefix):]: np.asarray(v) for name, v in inputs.items() if name.startswith(prefix)}

    a, b, f = part("L0_attn_a_"), part("L0_attn_b_"), part("L0_ffn_")
    arrays = {"x": a["x"], **shape_constants(), **attn_b_constants(), **attn_a_layout(a), **attn_b_layout(b),
              **ffn_layout(f)}
    arrays = {name: np.ascontiguousarray(v) for name, v in arrays.items()}
    nc = bacc.Bacc("TRN2", target_bir_lowering=False, num_devices=1)
    arr = {name: nc.dram_tensor(f"in_{name}_dram", v.shape, F32, kind="ExternalInput").ap()
           for name, v in arrays.items()}
    out = nc.dram_tensor("out_0_dram", (B, T * P, P), F32, kind="ExternalOutput").ap()
    hybrid_block(nc, arr, out)
    run = run_bass_kernel_spmd(nc, [{f"in_{name}_dram": v for name, v in arrays.items()}], core_ids=[0])
    return run.results[0]["out_0_dram"]
```
